# Optimizing a Trainium2 kernel written in Bass

```python
import numpy as np
import jax
import jax.numpy as jnp

def _softmax(x, axis=-1):
    return jax.nn.softmax(x, axis=axis)

def _gelu(x):
    return jax.nn.gelu(x, approximate=True)

def _silu(x):
    return jax.nn.silu(x)

def _sigmoid(x):
    return jax.nn.sigmoid(x)

def _layernorm(x, axis=-1, eps=1e-05):
    m = jnp.mean(x, axis=axis, keepdims=True)
    v = jnp.var(x, axis=axis, keepdims=True)
    return (x - m) / jnp.sqrt(v + eps)

def _scatter_add(tgt, idx, src, axis=0):
    return tgt.at[idx].add(src)

def _segment_sum(src, seg, n):
    return jax.ops.segment_sum(src, seg, n)
kernel_name = 'mk_adj_ffn_d2_adj_r2_5e0f9f'

def setup_inputs(seed: int=0):
    np.random.seed(seed)
    _w = jnp.asarray

    def _rec_inputs():
        import jax
        import jax.numpy as jnp
        _gk = jax.random.key(seed)
        x = -0.0002928 + 1 * jax.random.normal(jax.random.fold_in(_gk, 1), (16, 512, 128), jnp.float32)
        _a = jax.random.bernoulli(jax.random.fold_in(_gk, 2), 0.0078125, (512, 512))
        _a = jnp.logical_or(_a, jnp.eye(512, dtype=bool))
        _af = _a.astype(jnp.float32)
        adj = _af
        return (x, adj)
    x, adj = _rec_inputs()

    def _L0_gnn_setup():
        import jax, jax.numpy as jnp
        import numpy as np
        ALPHA = 0.2
        key = jax.random.key(seed)
        k1, k2, k3, k4 = jax.random.split(key, 4)
        B, N, Fin, Fout = (8, 1024, 128, 128)
        h = jax.random.normal(k1, (B, N, Fin), dtype=jnp.float32)
        adj = jax.random.randint(k2, (N, N), 0, 2).astype(jnp.float32)
        adj = jnp.maximum(adj, jnp.eye(N, dtype=jnp.float32))

        def xavier(k, shape, gain=1.414):
            fan_in, fan_out = (shape[0], shape[1])
            a = gain * np.sqrt(6.0 / (fan_in + fan_out))
            return jax.random.uniform(k, shape, dtype=jnp.float32, minval=-a, maxval=a)
        W = xavier(k3, (Fin, Fout))
        a = xavier(k4, (2 * Fout, 1))
        return {'h': h, 'adj_matrix': adj, 'W': W, 'a': a}
    _L0_gnn_all = _L0_gnn_setup()
    _L0_gnn_in = {k: v for k, v in _L0_gnn_all.items() if k in ('W', 'a')}
    del _L0_gnn_all

    def _L0_ffn_setup():
        import jax, jax.numpy as jnp
        import numpy as np
        D_MODEL = 128
        D_STATE = 64
        D_CONV = 4
        EXPAND = 2
        HEADDIM = 64
        D_INNER = EXPAND * D_MODEL
        NHEADS = D_INNER // HEADDIM
        CONV_DIM = D_INNER + 2 * D_STATE
        D_IN_PROJ = 2 * D_INNER + 2 * D_STATE + NHEADS
        CHUNK = 128
        EPS = 1e-05

        def segsum(a):
            T = a.shape[-1]
            cs = jnp.cumsum(a, axis=-1)
            ss = cs[..., :, None] - cs[..., None, :]
            mask = jnp.tril(jnp.ones((T, T), dtype=bool))
            return jnp.where(mask, ss, -jnp.inf)

        def mamba2_block(x, W_in, conv_w, conv_b, dt_bias, A_log, D, norm_w, W_out, W_lin, b_lin):
            Bsz, L, _ = x.shape
            zxbcdt = x @ W_in
            z, xBC, dt = jnp.split(zxbcdt, [D_INNER, D_INNER + CONV_DIM], axis=-1)
            xp = jnp.pad(xBC, ((0, 0), (D_CONV - 1, 0), (0, 0)))
            conv = conv_b + sum((xp[:, k:k + L, :] * conv_w[:, k] for k in range(D_CONV)))
            xBC = jax.nn.silu(conv)
            xh, Bmat, Cmat = jnp.split(xBC, [D_INNER, D_INNER + D_STATE], axis=-1)
            dt = jax.nn.softplus(dt + dt_bias)
            A = -jnp.exp(A_log)
            nc = L // CHUNK
            xh = xh.reshape(Bsz, nc, CHUNK, NHEADS, HEADDIM)
            Bc = Bmat.reshape(Bsz, nc, CHUNK, D_STATE)
            Cc = Cmat.reshape(Bsz, nc, CHUNK, D_STATE)
            dtc = dt.reshape(Bsz, nc, CHUNK, NHEADS)
            dA = jnp.einsum('bclh,h->bhcl', dtc, A)
            A_cum = jnp.cumsum(dA, axis=-1)
            Lmat = jnp.exp(segsum(dA))
            xdt = xh * dtc[..., None]
            Y_diag = jnp.einsum('bcln,bcsn,bhcls,bcshp->bclhp', Cc, Bc, Lmat, xdt)
            decay_states = jnp.exp(A_cum[..., -1:] - A_cum)
            states = jnp.einsum('bcln,bhcl,bclhp->bchpn', Bc, decay_states, xdt)
            chunk_decay = jnp.exp(A_cum[..., -1])

            def step(h, inp):
                s, d = inp
                return (h * d[..., None, None] + s, h)
            _, prevs = jax.lax.scan(step, jnp.zeros_like(states[:, 0]), (jnp.moveaxis(states, 1, 0), jnp.moveaxis(chunk_decay, 2, 0)))
            prevs = jnp.moveaxis(prevs, 0, 1)
            Y_off = jnp.einsum('bcln,bchpn,bhcl->bclhp', Cc, prevs, jnp.exp(A_cum))
            Y = (Y_diag + Y_off + xh * D[:, None]).reshape(Bsz, L, D_INNER)
            Y = Y * jax.nn.silu(z)
            Y = Y * jax.lax.rsqrt(jnp.mean(Y * Y, axis=-1, keepdims=True) + EPS) * norm_w
            out = Y @ W_out
            return out @ W_lin + b_lin
        key = jax.random.key(seed)
        ks = jax.random.split(key, 12)
        B, L = (8, 2048)

        def gauss(k, shape, scale):
            return jax.random.normal(k, shape, dtype=jnp.float32) * scale
        return {'x': gauss(ks[0], (B, L, D_MODEL), 1.0), 'W_in': gauss(ks[1], (D_MODEL, D_IN_PROJ), D_MODEL ** (-0.5)), 'conv_w': gauss(ks[2], (CONV_DIM, D_CONV), 0.3), 'conv_b': gauss(ks[3], (CONV_DIM,), 0.1), 'dt_bias': jax.random.uniform(ks[4], (NHEADS,), minval=-4.0, maxval=-1.0), 'A_log': jnp.log(jax.random.uniform(ks[5], (NHEADS,), minval=1.0, maxval=16.0)), 'D': jnp.ones((NHEADS,), jnp.float32), 'norm_w': jnp.ones((D_INNER,), jnp.float32), 'W_out': gauss(ks[6], (D_INNER, D_MODEL), D_INNER ** (-0.5)), 'W_lin': gauss(ks[7], (D_MODEL, D_MODEL), D_MODEL ** (-0.5)), 'b_lin': jnp.zeros((D_MODEL,), jnp.float32)}
    _L0_ffn_all = _L0_ffn_setup()
    _L0_ffn_in = {k: v for k, v in _L0_ffn_all.items() if k in ('W_in', 'conv_w', 'conv_b', 'dt_bias', 'A_log', 'D', 'norm_w', 'W_out', 'W_lin', 'b_lin')}
    del _L0_ffn_all

    def _L1_gnn_setup():
        import jax, jax.numpy as jnp
        import numpy as np
        N_STEPS = 8
        SPATIAL_SCALE = 1.0
        key = jax.random.key(seed)
        ks = jax.random.split(key, 6)
        B, N, D = (32, 512, 128)
        x = jax.random.normal(ks[0], (B, N, D), dtype=jnp.float32)
        adj_mx = jax.random.uniform(ks[1], (N, N), dtype=jnp.float32) / N
        alpha_train = jnp.ones((N,), dtype=jnp.float32)
        w = jnp.eye(D, dtype=jnp.float32) + 0.01 * jax.random.normal(ks[2], (D, D), dtype=jnp.float32)
        d = jax.random.uniform(ks[3], (D,), dtype=jnp.float32)
        fc_in_w = jax.random.normal(ks[4], (D, D), dtype=jnp.float32) * (1.0 / np.sqrt(D))
        fc_in_b = jnp.zeros((D,), dtype=jnp.float32)
        return {'x': x, 'adj_mx': adj_mx, 'alpha_train': alpha_train, 'w': w, 'd': d, 'fc_in_w': fc_in_w, 'fc_in_b': fc_in_b, 'vt': 0}
    _L1_gnn_all = _L1_gnn_setup()
    _L1_gnn_in = {k: v for k, v in _L1_gnn_all.items() if k in ('alpha_train', 'w', 'd', 'fc_in_w', 'fc_in_b')}
    del _L1_gnn_all

    def _L1_ffn_setup():
        import jax, jax.numpy as jnp
        import numpy as np
        BN_EPS = 0.001

        def _bn(h, g, b, m, v):
            return g * (h - m) * jax.lax.rsqrt(v + BN_EPS) + b
        key = jax.random.key(seed)
        ks = jax.random.split(key, 8)
        B, F, Df = (128, 64, 128)
        E, H, D = (8, 128, 128)
        s1 = 1.0 / np.sqrt(Df)
        s2 = 1.0 / np.sqrt(H)
        return {'x': jax.random.normal(ks[0], (B, F, Df), jnp.float32), 'Wr': jax.random.normal(ks[1], (Df, E), jnp.float32) * s1, 'br': jnp.zeros((E,), jnp.float32), 'W1': jax.random.normal(ks[2], (E, Df, H), jnp.float32) * s1, 'b1': jnp.zeros((E, H), jnp.float32), 'g1': jnp.ones((E, H), jnp.float32), 'be1': jnp.zeros((E, H), jnp.float32), 'm1': jnp.zeros((E, H), jnp.float32), 'v1': jnp.ones((E, H), jnp.float32), 'W2': jax.random.normal(ks[3], (E, H, H), jnp.float32) * s2, 'b2': jnp.zeros((E, H), jnp.float32), 'g2': jnp.ones((E, H), jnp.float32), 'be2': jnp.zeros((E, H), jnp.float32), 'm2': jnp.zeros((E, H), jnp.float32), 'v2': jnp.ones((E, H), jnp.float32), 'Wo': jax.random.normal(ks[4], (E, H, D), jnp.float32) * s2, 'bo': jnp.zeros((E, D), jnp.float32)}
    _L1_ffn_all = _L1_ffn_setup()
    _L1_ffn_in = {k: v for k, v in _L1_ffn_all.items() if k in ('Wr', 'br', 'W1', 'b1', 'g1', 'be1', 'm1', 'v1', 'W2', 'b2', 'g2', 'be2', 'm2', 'v2', 'Wo', 'bo')}
    del _L1_ffn_all
    return {'x': x, 'adj': adj, 'L0_gnn_W': _L0_gnn_in['W'], 'L0_gnn_a': _L0_gnn_in['a'], 'L0_ffn_W_in': _L0_ffn_in['W_in'], 'L0_ffn_conv_w': _L0_ffn_in['conv_w'], 'L0_ffn_conv_b': _L0_ffn_in['conv_b'], 'L0_ffn_dt_bias': _L0_ffn_in['dt_bias'], 'L0_ffn_A_log': _L0_ffn_in['A_log'], 'L0_ffn_D': _L0_ffn_in['D'], 'L0_ffn_norm_w': _L0_ffn_in['norm_w'], 'L0_ffn_W_out': _L0_ffn_in['W_out'], 'L0_ffn_W_lin': _L0_ffn_in['W_lin'], 'L0_ffn_b_lin': _L0_ffn_in['b_lin'], 'L1_gnn_alpha_train': _L1_gnn_in['alpha_train'], 'L1_gnn_w': _L1_gnn_in['w'], 'L1_gnn_d': _L1_gnn_in['d'], 'L1_gnn_fc_in_w': _L1_gnn_in['fc_in_w'], 'L1_gnn_fc_in_b': _L1_gnn_in['fc_in_b'], 'L1_ffn_Wr': _L1_ffn_in['Wr'], 'L1_ffn_br': _L1_ffn_in['br'], 'L1_ffn_W1': _L1_ffn_in['W1'], 'L1_ffn_b1': _L1_ffn_in['b1'], 'L1_ffn_g1': _L1_ffn_in['g1'], 'L1_ffn_be1': _L1_ffn_in['be1'], 'L1_ffn_m1': _L1_ffn_in['m1'], 'L1_ffn_v1': _L1_ffn_in['v1'], 'L1_ffn_W2': _L1_ffn_in['W2'], 'L1_ffn_b2': _L1_ffn_in['b2'], 'L1_ffn_g2': _L1_ffn_in['g2'], 'L1_ffn_be2': _L1_ffn_in['be2'], 'L1_ffn_m2': _L1_ffn_in['m2'], 'L1_ffn_v2': _L1_ffn_in['v2'], 'L1_ffn_Wo': _L1_ffn_in['Wo'], 'L1_ffn_bo': _L1_ffn_in['bo']}

def reference(x, adj, L0_gnn_W, L0_gnn_a, L0_ffn_W_in, L0_ffn_conv_w, L0_ffn_conv_b, L0_ffn_dt_bias, L0_ffn_A_log, L0_ffn_D, L0_ffn_norm_w, L0_ffn_W_out, L0_ffn_W_lin, L0_ffn_b_lin, L1_gnn_alpha_train, L1_gnn_w, L1_gnn_d, L1_gnn_fc_in_w, L1_gnn_fc_in_b, L1_ffn_Wr, L1_ffn_br, L1_ffn_W1, L1_ffn_b1, L1_ffn_g1, L1_ffn_be1, L1_ffn_m1, L1_ffn_v1, L1_ffn_W2, L1_ffn_b2, L1_ffn_g2, L1_ffn_be2, L1_ffn_m2, L1_ffn_v2, L1_ffn_Wo, L1_ffn_bo):
    import jax
    import jax.numpy as jnp

    def _L0_gnn_ref(h, adj_matrix, W, a):
        import jax, jax.numpy as jnp
        import numpy as np
        ALPHA = 0.2
        Fout = W.shape[1]
        Wh = jnp.einsum('bnf,fo->bno', h, W)
        a1, a2 = (a[:Fout, 0], a[Fout:, 0])
        s1 = Wh @ a1
        s2 = Wh @ a2
        e = s1[:, :, None] + s2[:, None, :]
        e = jnp.where(e >= 0, e, ALPHA * e)
        e = jnp.where(adj_matrix[None] == 0, -jnp.inf, e)
        attention = jax.nn.softmax(e, axis=-1)
        h_prime = jnp.einsum('bij,bjo->bio', attention, Wh)
        return h_prime

    def _L0_ffn_ref(x, W_in, conv_w, conv_b, dt_bias, A_log, D, norm_w, W_out, W_lin, b_lin):
        import jax, jax.numpy as jnp
        import numpy as np
        D_MODEL = 128
        D_STATE = 64
        D_CONV = 4
        EXPAND = 2
        HEADDIM = 64
        D_INNER = EXPAND * D_MODEL
        NHEADS = D_INNER // HEADDIM
        CONV_DIM = D_INNER + 2 * D_STATE
        D_IN_PROJ = 2 * D_INNER + 2 * D_STATE + NHEADS
        CHUNK = 128
        EPS = 1e-05

        def segsum(a):
            T = a.shape[-1]
            cs = jnp.cumsum(a, axis=-1)
            ss = cs[..., :, None] - cs[..., None, :]
            mask = jnp.tril(jnp.ones((T, T), dtype=bool))
            return jnp.where(mask, ss, -jnp.inf)

        def mamba2_block(x, W_in, conv_w, conv_b, dt_bias, A_log, D, norm_w, W_out, W_lin, b_lin):
            Bsz, L, _ = x.shape
            zxbcdt = x @ W_in
            z, xBC, dt = jnp.split(zxbcdt, [D_INNER, D_INNER + CONV_DIM], axis=-1)
            xp = jnp.pad(xBC, ((0, 0), (D_CONV - 1, 0), (0, 0)))
            conv = conv_b + sum((xp[:, k:k + L, :] * conv_w[:, k] for k in range(D_CONV)))
            xBC = jax.nn.silu(conv)
            xh, Bmat, Cmat = jnp.split(xBC, [D_INNER, D_INNER + D_STATE], axis=-1)
            dt = jax.nn.softplus(dt + dt_bias)
            A = -jnp.exp(A_log)
            nc = L // CHUNK
            xh = xh.reshape(Bsz, nc, CHUNK, NHEADS, HEADDIM)
            Bc = Bmat.reshape(Bsz, nc, CHUNK, D_STATE)
            Cc = Cmat.reshape(Bsz, nc, CHUNK, D_STATE)
            dtc = dt.reshape(Bsz, nc, CHUNK, NHEADS)
            dA = jnp.einsum('bclh,h->bhcl', dtc, A)
            A_cum = jnp.cumsum(dA, axis=-1)
            Lmat = jnp.exp(segsum(dA))
            xdt = xh * dtc[..., None]
            Y_diag = jnp.einsum('bcln,bcsn,bhcls,bcshp->bclhp', Cc, Bc, Lmat, xdt)
            decay_states = jnp.exp(A_cum[..., -1:] - A_cum)
            states = jnp.einsum('bcln,bhcl,bclhp->bchpn', Bc, decay_states, xdt)
            chunk_decay = jnp.exp(A_cum[..., -1])

            def step(h, inp):
                s, d = inp
                return (h * d[..., None, None] + s, h)
            _, prevs = jax.lax.scan(step, jnp.zeros_like(states[:, 0]), (jnp.moveaxis(states, 1, 0), jnp.moveaxis(chunk_decay, 2, 0)))
            prevs = jnp.moveaxis(prevs, 0, 1)
            Y_off = jnp.einsum('bcln,bchpn,bhcl->bclhp', Cc, prevs, jnp.exp(A_cum))
            Y = (Y_diag + Y_off + xh * D[:, None]).reshape(Bsz, L, D_INNER)
            Y = Y * jax.nn.silu(z)
            Y = Y * jax.lax.rsqrt(jnp.mean(Y * Y, axis=-1, keepdims=True) + EPS) * norm_w
            out = Y @ W_out
            return out @ W_lin + b_lin
        return mamba2_block(x, W_in, conv_w, conv_b, dt_bias, A_log, D, norm_w, W_out, W_lin, b_lin)

    def _L1_gnn_ref(x, adj_mx, alpha_train, w, d, fc_in_w, fc_in_b, vt):
        import jax, jax.numpy as jnp
        import numpy as np
        N_STEPS = 8
        SPATIAL_SCALE = 1.0
        x0 = jax.lax.stop_gradient(x)
        h = jnp.einsum('bnd,ed->bne', x, fc_in_w) + fc_in_b
        alph = jax.nn.sigmoid(alpha_train)[:, None]
        d_clamped = jnp.clip(d, 0.0, 1.0)
        w_eff = w * d_clamped @ w.T
        dt = jnp.float32(SPATIAL_SCALE / N_STEPS)

        def euler_step(h, _):
            ax = jnp.einsum('nm,bmd->bnd', adj_mx, h)
            f = alph * 0.5 * (ax - h) + h @ w_eff - h + x0
            return (h + dt * f, None)
        h, _ = jax.lax.scan(euler_step, h, None, length=N_STEPS)
        return h

    def _L1_ffn_ref(x, Wr, br, W1, b1, g1, be1, m1, v1, W2, b2, g2, be2, m2, v2, Wo, bo):
        import jax, jax.numpy as jnp
        import numpy as np
        BN_EPS = 0.001

        def _bn(h, g, b, m, v):
            return g * (h - m) * jax.lax.rsqrt(v + BN_EPS) + b
        feat = jnp.mean(x, axis=0)
        w = jax.nn.softmax(feat @ Wr + br, axis=-1)
        h = jnp.einsum('bfd,edh->bfeh', x, W1) + b1
        h = jax.nn.relu(_bn(h, g1, be1, m1, v1))
        h = jnp.einsum('bfeh,ehk->bfek', h, W2) + b2
        h = jax.nn.relu(_bn(h, g2, be2, m2, v2))
        y = jnp.einsum('bfeh,ehd->bfed', h, Wo) + bo
        return jnp.einsum('bfed,fe->bfd', y, w)
    x = x + _L0_gnn_ref(_layernorm(x, axis=-1), adj, L0_gnn_W, L0_gnn_a)
    x = x + _L0_ffn_ref(_layernorm(x, axis=-1), L0_ffn_W_in, L0_ffn_conv_w, L0_ffn_conv_b, L0_ffn_dt_bias, L0_ffn_A_log, L0_ffn_D, L0_ffn_norm_w, L0_ffn_W_out, L0_ffn_W_lin, L0_ffn_b_lin)
    x = x + _L1_gnn_ref(_layernorm(x, axis=-1), adj, L1_gnn_alpha_train, L1_gnn_w, L1_gnn_d, L1_gnn_fc_in_w, L1_gnn_fc_in_b, 0)
    x = x + _L1_ffn_ref(_layernorm(x, axis=-1), L1_ffn_Wr, L1_ffn_br, L1_ffn_W1, L1_ffn_b1, L1_ffn_g1, L1_ffn_be1, L1_ffn_m1, L1_ffn_v1, L1_ffn_W2, L1_ffn_b2, L1_ffn_g2, L1_ffn_be2, L1_ffn_m2, L1_ffn_v2, L1_ffn_Wo, L1_ffn_bo)
    return x

_drawn_inputs = setup_inputs


def setup_inputs(seed=0):
    import zlib

    import numpy as np

    out = dict(_drawn_inputs(seed))
    spreads = {'L0_ffn_D': (1.0, 0.2),
     'L0_ffn_norm_w': (1.0, 0.2),
     'L0_ffn_b_lin': (0.0, 0.1),
     'L1_gnn_alpha_train': (1.0, 0.6),
     'L1_gnn_fc_in_b': (0.0, 0.1),
     'L1_ffn_br': (0.0, 0.8),
     'L1_ffn_b1': (0.0, 0.8),
     'L1_ffn_g1': (1.0, 0.6),
     'L1_ffn_be1': (0.0, 0.8),
     'L1_ffn_m1': (0.0, 0.8),
     'L1_ffn_v1': (1.0, 0.6),
     'L1_ffn_b2': (0.0, 0.8),
     'L1_ffn_g2': (1.0, 0.6),
     'L1_ffn_be2': (0.0, 0.8),
     'L1_ffn_m2': (0.0, 0.8),
     'L1_ffn_v2': (1.0, 0.6),
     'L1_ffn_bo': (0.0, 0.584)}
    factors = {'L0_ffn_A_log': 7.686}
    for name, (base, spread) in spreads.items():
        noise = np.random.default_rng([zlib.crc32(name.encode()), seed]).standard_normal(out[name].shape)
        drawn = base * np.exp(spread * noise) if base else spread * noise
        out[name] = jnp.asarray(drawn.astype(out[name].dtype))
    for name, factor in factors.items():
        out[name] = (out[name] * factor).astype(out[name].dtype)
    return out
```

```python
from contextlib import ExitStack
from math import comb

import concourse.bass as bass
from concourse import mybir

F32 = mybir.dt.float32
ALU = mybir.AluOpType
ACT = mybir.ActivationFunctionType

P = 128
B, N, D = 16, 512, 128
T = N // P
Q = B * T
LN_EPS = 1e-5
NEG = -1e30
LEAK = 0.2
HEADS, HD, STATE, INNER, TAPS = 4, 64, 64, 256, 4
STEPS = 8
DT = 1.0 / STEPS
EXPERTS = 8
BN_EPS = 1e-3


def wait(eng, sem, value):
    if isinstance(value, int) and value <= 0:
        return
    eng.wait_ge(sem, value)


def wait_apart(eng, sem, value, seen):
    wait(eng, sem, value)
    eng.sem_inc(seen, 1)


def over_batches(eng, body):
    body(0, 0, True, False)
    with eng.Fori(0, B // 2 - 1) as i:
        body(2 * i + 1, 1, False, False)
        body(2 * i + 2, 0, False, False)
    body(B - 1, 1, False, True)


def nothing(*unused):
    pass


class Shared:
    pass


class Extra:

    def __init__(self, pe_end, act_end, dve_end, pool, wait_h_free=nothing, wait_ht_free=nothing,
                 pe=nothing, dve=nothing, dve_start=nothing):
        self.pe, self.dve, self.pool = pe, dve, pool
        self.pe_end, self.act_end, self.dve_end, self.dve_start = pe_end, act_end, dve_end, dve_start
        self.wait_h_free, self.wait_ht_free = wait_h_free, wait_ht_free


class Memory:

    def __init__(self, nc, stack):
        self.nc, self.stack = nc, stack
        self.known = {}

    def sb(self, name, *shape, dt=F32):
        return self.stack.enter_context(self.nc.sbuf_tensor(name, list(shape), dt))

    def banks(self, name, count):
        return [self.stack.enter_context(self.nc.psum_tensor(f"{name}{k}", [P, 512], F32)) for k in range(count)]

    def sem(self, name):
        if name not in self.known:
            self.known[name] = self.stack.enter_context(self.nc.semaphore(name))
        return self.known[name]


def retire(nc, mem):
    numbers = sorted(s.num for s in mem.known.values())
    with nc.Block() as block:

        @block.sync
        def _(sp):
            first = prev = numbers[0]
            for n in numbers[1:] + [None]:
                if n is not None and n == prev + 1:
                    prev = n
                    continue
                sp.sem_clear(range(first, prev + 1))
                first = prev = n


def tiles(ap, t=T):
    return ap.rearrange("p (t d) -> p t d", t=t)




def setup(nc, m, IN):
    with ExitStack() as stack:
        mem = Memory(nc, stack)
        S = mem.sem
        W0 = mem.sb("gat_w", P, 128)
        A12 = mem.sb("gat_a", P, 2)
        GW = mem.sb("ode_w", P, 128)
        FW = mem.sb("fc_w", P, 128)
        FB = mem.sb("fc_b", P, 1)
        DC = mem.sb("ode_d", P, 1)
        WO = mem.sb("mamba_out_w", P, 2, 128)
        WL = mem.sb("mamba_lin_w", P, 128)
        NW = mem.sb("mamba_norm_w", P, 2)
        AL = mem.sb("alpha", P, T)
        SG = mem.sb("alpha_scaled", P, 3, T)
        BNR = mem.sb("bn_rows", 80, 128)
        BNT = mem.sb("bn_tmp", P, 2, 16)
        WT = mem.sb("turned_weights", P, 336)
        WOT = mem.sb("mamba_out_w_turned", P, 256)
        WTD = mem.sb("ode_wt_scaled", P, 128)
        RI = mem.sb("ode_decay_ident", P, 128)
        ADJ = mem.sb("adj", P, T, N)
        L = mem.sb("L", P, T, N)
        L3 = mem.sb("L3", P, T, N)
        RP = mem.sb("R_powers", P, 9, 128)
        FRP = mem.sb("F_R_powers", P, 9, 128)
        BK = mem.sb("fc_b_columns", P, 9, 9)
        V = mem.sb("L_powers_on_ones", P, T, 9)
        VT = mem.sb("L_powers_rows", 9, N)
        RB = mem.sb("fc_b_R_powers", 9, 128)
        ST = mem.sb("stats", P, Q, 6)
        bank = mem.banks("setup_bank", 8)

        def col(ap):
            return ap.rearrange("(p o) -> p o", o=1)

        def wide(ap, n):
            return ap.rearrange("(o n) -> o n", o=1).broadcast_to([P, n])

        with nc.Block() as block:

            @block.sync
            def _(sp):
                sp.dma_start(ADJ[:, :, :], IN["adj"].rearrange("(t p) m -> p t m", p=P)).then_inc(S("adj_loaded"), 16)
                for g in range(4):
                    for b in range(4 * g, 4 * g + 4):
                        sp.dma_start(tiles(m.X[:, b * 512:(b + 1) * 512]),
                                     IN["x"][b].rearrange("(t p) d -> p t d", p=P)).then_inc(S(f"x_loaded{g}"), 16)
                for dst, name, form in ((m.W1, "L1_ffn_W1", "e d h -> d e h"), (m.W2, "L1_ffn_W2", "e d h -> d e h"),
                                        (m.W3, "L1_ffn_Wo", "e d h -> d e h")):
                    sp.dma_start(dst[:, :, :], IN[name].rearrange(form)).then_inc(S("experts_loaded"), 16)
                sp.wait_ge(S("experts_loaded"), 48)

            @block.gpsimd
            def _(pool):
                pool.memset(m.IDENT[:, :], 0.0).then_inc(S("pool_zero"), 1)
                pool.memset(m.LE[:, :], 1.0).then_inc(S("pool_zero"), 1)
                pool.memset(m.GT[:, :], 1.0).then_inc(S("pool_zero"), 1)
                pool.memset(m.ONES[:, :], 1.0).then_inc(S("pool_zero"), 1)
                pool.memset(m.MHALF[:, :], -0.5).then_inc(S("pool_zero"), 1)
                pool.memset(BK[:, :, :], 0.0).then_inc(S("columns_zero"), 1)
                pool.memset(V[:, :, :], 1.0).then_inc(S("columns_zero"), 1)
                pool.wait_ge(S("pool_zero"), 5)
                pool.affine_select(out=m.IDENT[:, :], in_=m.IDENT[:, :], compare_op=ALU.not_equal, fill=1.0,
                                   base=0, pattern=[[-1, P]], channel_multiplier=1).then_inc(S("masks"), 1)
                pool.affine_select(out=m.LE[:, :], in_=m.LE[:, :], compare_op=ALU.is_ge, fill=0.0,
                                   base=0, pattern=[[1, P]], channel_multiplier=-1).then_inc(S("masks"), 1)
                pool.affine_select(out=m.GT[:, :], in_=m.GT[:, :], compare_op=ALU.is_gt, fill=0.0,
                                   base=0, pattern=[[-1, P]], channel_multiplier=1).then_inc(S("masks"), 1)
                pool.wait_ge(S("turned_copied"), 1)
                for k, at in enumerate((256 + 32, 256 + 72)):
                    pool.tensor_scalar(BNT[:, 0, 8 * k:8 * k + 8], WT[:, at:at + 8], BN_EPS, None,
                                       ALU.add).then_inc(S("bn_var"), 1)
                pool.wait_ge(S("bn_var"), 2)
                pool.tensor_tensor(BNT[:, 1, :], BNT[:, 0, :], m.MHALF[:, 0:16], ALU.pow).then_inc(S("bn_rstd"), 1)
                pool.wait_ge(S("stats_known"), Q)
                pool.tensor_scalar(m.RSTD[:, :], m.MV[:, :, 1], LN_EPS, None, ALU.add).then_inc(S("ln_var"), 1)
                pool.wait_ge(S("ln_var"), 1)
                pool.tensor_tensor(m.RSTD[:, :], m.RSTD[:, :], m.MHALF[:, :], ALU.pow)

            @block.scalar
            def _(act):
                n = 0
                for dst, src in ((W0[:, :], IN["L0_gnn_W"]), (A12[:, :], IN["L0_gnn_a"].rearrange("(k p) o -> p (k o)", k=2)),
                                 (GW[:, :], IN["L1_gnn_w"]), (FW[:, :], IN["L1_gnn_fc_in_w"]),
                                 (FB[:, :], col(IN["L1_gnn_fc_in_b"])), (DC[:, :], col(IN["L1_gnn_d"])),
                                 (WO[:, :, :], IN["L0_ffn_W_out"].rearrange("(g p) n -> p g n", p=P)),
                                 (WL[:, :], IN["L0_ffn_W_lin"]),
                                 (NW[:, :], IN["L0_ffn_norm_w"].rearrange("(g p) -> p g", p=P)),
                                 (AL[:, :], IN["L1_gnn_alpha_train"].rearrange("(t p) -> p t", p=P))):
                    act.dma_start(dst, src).then_inc(S("weights_loaded"), 16)
                for k, name in enumerate(("b1", "g1", "be1", "m1", "v1", "b2", "g2", "be2", "m2", "v2")):
                    act.dma_start(BNR[8 * k:8 * k + 8, :], IN["L1_ffn_" + name]).then_inc(S("weights_loaded"), 16)
                for dst, src in ((m.WIN[:, :], IN["L0_ffn_W_in"]),
                                 (m.CW[:, :, :], IN["L0_ffn_conv_w"].rearrange("(g p) k -> p g k", p=P)),
                                 (m.CB[:, :], IN["L0_ffn_conv_b"].rearrange("(g p) -> p g", p=P)),
                                 (m.DTB[:, :], wide(IN["L0_ffn_dt_bias"], 4)), (m.AH[:, :], wide(IN["L0_ffn_A_log"], 4)),
                                 (m.DH[:, :], wide(IN["L0_ffn_D"], 4)), (m.BLIN[:, :], wide(IN["L0_ffn_b_lin"], 128)),
                                 (m.WR[:, :], IN["L1_ffn_Wr"]), (m.BR[:, :], wide(IN["L1_ffn_br"], 8)),
                                 (m.BO[:, :], IN["L1_ffn_bo"])):
                    act.dma_start(dst, src).then_inc(S("later_loaded"), 16)
                act.wait_ge(S("weights_loaded"), 16 * 20)
                act.activation(SG[:, 0, :], AL[:, :], ACT.Exp, scale=-1.0).then_inc(S("alpha_exp"), 1)
                act.wait_ge(S("turned"), 1)
                act.activation(WT[:, :], bank[0][:, 0:336], ACT.Copy).then_inc(S("turned_copied"), 1)
                act.wait_ge(S("turned"), 2)
                act.activation(WOT[:, :], bank[1][:, 0:256], ACT.Copy).then_inc(S("turned_copied"), 1)
                for k, dst in enumerate((m.LT, m.L2T, m.L3T, L3, m.L6T)):
                    for t in range(T):
                        act.wait_ge(S("L_product"), T * k + t + 1)
                        act.activation(dst[:, t, :], bank[4 + t][:, :], ACT.Copy).then_inc(S("L_copied"), 1)
                act.wait_ge(S("later_loaded"), 16 * 10)
                act.activation(m.AH[:, :], m.AH[:, :], ACT.Exp)

            @block.tensor
            def _(pe):
                pe.wait_ge(S("masks"), 3)
                pe.wait_ge(S("weights_loaded"), 16 * 20)
                pe.transpose(bank[0][:, 0:128], W0[:, :], m.IDENT[:, :])
                pe.transpose(bank[0][:, 128:256], GW[:, :], m.IDENT[:, :])
                pe.transpose(bank[0][:, 256:336], BNR[:, :], m.IDENT[0:80, 0:80]).then_inc(S("turned"), 1)
                pe.transpose(bank[1][:, 0:128], WO[:, 0, :], m.IDENT[:, :])
                pe.transpose(bank[1][:, 128:256], WO[:, 1, :], m.IDENT[:, :]).then_inc(S("turned"), 1)
                pe.wait_ge(S("turned_copied"), 2)
                pe.wait_ge(S("ode_wt_scaled"), 1)
                pe.matmul(bank[2][:, 0:2], WT[:, 0:128], A12[:, :], start=True, stop=True)
                pe.matmul(bank[2][:, 128:256], WT[:, 128:256], WTD[:, :], start=True, stop=True)
                for g in range(2):
                    mm = pe.matmul(bank[2][:, 256 + 128 * g:384 + 128 * g], WOT[:, 128 * g:128 * g + 128], WL[:, :],
                                   start=True, stop=True)
                mm.then_inc(S("small_products"), 1)
                pe.wait_ge(S("R_known"), 1)
                pe.matmul(bank[3][:, 0:128], RP[:, 1, :], RP[:, 1, :], start=True, stop=True).then_inc(S("R_product"), 1)
                pe.wait_ge(S("R_known"), 2)
                pe.matmul(bank[3][:, 0:256], RP[:, 2, :], RP[:, 1:3, :], start=True, stop=True).then_inc(S("R_product"), 1)
                pe.wait_ge(S("R_known"), 3)
                pe.matmul(bank[3][:, :], RP[:, 4, :], RP[:, 1:5, :], start=True, stop=True).then_inc(S("R_product"), 1)
                pe.wait_ge(S("R_known"), 4)
                for k, n in ((0, 4), (4, 4), (8, 1)):
                    if k:
                        pe.wait_ge(S("FR_copied"), k // 4)
                    pe.matmul(bank[3][:, 0:128 * n], FW[:, :], RP[:, k:k + n, :], start=True, stop=True)\
                      .then_inc(S("FR_product"), 1)
                pe.wait_ge(S("L_known"), T)
                for t in range(T):
                    for s in range(T):
                        mm = pe.transpose(bank[4 + t][:, s * P:(s + 1) * P], L[:, s, t * P:(t + 1) * P], m.IDENT[:, :])
                    mm.then_inc(S("L_product"), 1)

                def power(k, left, right):
                    pe.wait_ge(S("L_copied"), T * k)
                    for t in range(T):
                        for s in range(T):
                            mm = pe.matmul(bank[4 + t][:, :], left[:, s, t * P:(t + 1) * P], right[:, s, :],
                                           start=(s == 0), stop=(s == T - 1))
                        mm.then_inc(S("L_product"), 1)

                power(1, L, m.LT)
                power(2, L, m.L2T)
                pe.wait_ge(S("L_copied"), 3 * T)
                for t in range(T):
                    for s in range(T):
                        mm = pe.transpose(bank[4 + t][:, s * P:(s + 1) * P], m.L3T[:, s, t * P:(t + 1) * P], m.IDENT[:, :])
                    mm.then_inc(S("L_product"), 1)
                power(4, L3, m.L3T)
                pe.wait_ge(S("L_copied"), 5 * T)
                pe.wait_ge(S("columns_zero"), 2)
                pe.wait_ge(S("FR_copied"), 3)
                for t in range(T):
                    for k, mat in ((1, m.LT), (2, m.L2T), (3, m.L3T), (6, m.L6T)):
                        for s in range(T):
                            mm = pe.matmul(bank[3][:, 16 * t + k:16 * t + k + 1], mat[:, s, t * P:(t + 1) * P], V[:, s, 0:1],
                                           start=(s == 0), stop=(s == T - 1))
                mm.then_inc(S("V_product"), 1)
                pe.wait_ge(S("V_known"), 4)
                for t in range(T):
                    for k, mat in ((4, m.L3T), (7, m.L6T)):
                        for s in range(T):
                            mm = pe.matmul(bank[3][:, 16 * t + k:16 * t + k + 2], mat[:, s, t * P:(t + 1) * P], V[:, s, 1:3],
                                           start=(s == 0), stop=(s == T - 1))
                mm.then_inc(S("V_product"), 1)
                pe.wait_ge(S("V_known"), 6)
                for t in range(T):
                    mm = pe.transpose(bank[0][0:9, t * P:(t + 1) * P], V[:, t, :], m.IDENT[:, :])
                mm.then_inc(S("V_turned"), 1)
                pe.wait_ge(S("fc_b_columns"), 9)
                for k in range(9):
                    mm = pe.matmul(bank[1][0:9, 0:128], BK[:, k, :], RP[:, 8 - k, :], start=(k == 0), stop=(k == 8))
                mm.then_inc(S("fc_b_products"), 1)
                pe.wait_ge(S("const_parts"), 2)
                for t in range(T):
                    mm = pe.matmul(bank[2][:, t * P:(t + 1) * P], VT[:, t * P:(t + 1) * P], RB[:, :], start=True, stop=True)
                mm.then_inc(S("const_known"), 1)

            @block.vector
            def _(dve):
                dve.wait_ge(S("weights_loaded"), 16 * 20)
                dve.wait_ge(S("alpha_exp"), 1)
                dve.tensor_scalar(SG[:, 0, :], SG[:, 0, :], 1.0, None, ALU.add).then_inc(S("alpha"), 1)
                dve.wait_ge(S("alpha"), 1)
                dve.reciprocal(SG[:, 2, :], SG[:, 0, :]).then_inc(S("alpha"), 1)
                dve.wait_ge(S("alpha"), 2)
                dve.tensor_scalar(SG[:, 1, :], SG[:, 2, :], 0.5 * DT, None, ALU.mult).then_inc(S("alpha"), 1)
                dve.wait_ge(S("alpha"), 3)
                dve.tensor_scalar(SG[:, 2, :], SG[:, 1, :], -1.0, None, ALU.mult).then_inc(S("alpha"), 1)
                dve.wait_ge(S("alpha"), 4)
                dve.wait_ge(S("adj_loaded"), 16)
                dve.wait_ge(S("masks"), 3)
                for t in range(T):
                    dve.tensor_scalar(L[:, t, :], ADJ[:, t, :], SG[:, 1, t:t + 1], None, ALU.mult).then_inc(S("L_adj"), 1)
                for t in range(T):
                    dve.wait_ge(S("L_adj"), t + 1)
                    diag = L[:, t, t * P:(t + 1) * P]
                    dve.scalar_tensor_tensor(out=diag, in0=m.IDENT[:, :], scalar=SG[:, 2, t:t + 1], in1=diag,
                                             op0=ALU.mult, op1=ALU.add).then_inc(S("L_known"), 1)
                dve.tensor_scalar(m.NEGM[:, :, :], ADJ[:, :, :], 0.0, NEG, ALU.is_equal, ALU.mult)
                dve.tensor_scalar(DC[:, :], DC[:, :], 0.0, 1.0, ALU.max, ALU.min).then_inc(S("clipped"), 1)
                dve.wait_ge(S("clipped"), 1)
                dve.wait_ge(S("turned_copied"), 1)
                dve.tensor_scalar(WTD[:, :], WT[:, 128:256], DC[:, 0:1], None, ALU.mult).then_inc(S("ode_wt_scaled"), 1)
                dve.tensor_scalar(RI[:, :], m.IDENT[:, :], 1.0 - DT, None, ALU.mult).then_inc(S("decay_ident"), 1)
                dve.tensor_copy(RP[:, 0, :], m.IDENT[:, :])
                dve.tensor_copy(m.WEXT[:, 0:128], W0[:, :])
                dve.wait_ge(S("decay_ident"), 1)
                dve.wait_ge(S("small_products"), 1)
                dve.scalar_tensor_tensor(out=RP[:, 1, :], in0=bank[2][:, 128:256], scalar=DT, in1=RI[:, :],
                                         op0=ALU.mult, op1=ALU.add).then_inc(S("R_known"), 1)
                dve.tensor_copy(m.WEXT[:, 128:130], bank[2][:, 0:2]).then_inc(S("wa_known"), 1)
                for g in range(2):
                    dve.tensor_scalar(m.WF[:, g, :], bank[2][:, 256 + 128 * g:384 + 128 * g], NW[:, g:g + 1], None, ALU.mult)
                dve.wait_ge(S("wa_known"), 1)
                dve.tensor_copy(m.WA2B[:, :], m.WEXT[:, 129:130].broadcast_to([P, P]))
                for k, (at, n) in enumerate(((2, 1), (3, 2), (5, 4))):
                    dve.wait_ge(S("R_product"), k + 1)
                    dve.tensor_copy(RP[:, at:at + n, :], bank[3][:, 0:128 * n].rearrange("p (k n) -> p k n", k=n))\
                       .then_inc(S("R_known"), 1)
                for k, n in ((0, 4), (4, 4), (8, 1)):
                    dve.wait_ge(S("FR_product"), k // 4 + 1)
                    dve.tensor_copy(FRP[:, k:k + n, :], bank[3][:, 0:128 * n].rearrange("p (k n) -> p k n", k=n))\
                       .then_inc(S("FR_copied"), 1)
                dve.wait_ge(S("R_known"), 4)
                dve.wait_ge(S("FR_copied"), 3)
                done = 0
                last = [0] * 9
                for k in range(9):
                    done += 1
                    last[k] = done
                    dve.tensor_scalar(m.E[:, k, :], FRP[:, STEPS - k, :], float(comb(STEPS, k)), None,
                                      ALU.mult).then_inc(S("E_terms"), 1)
                for r in range(STEPS):
                    for k in range(STEPS - r):
                        dve.wait_ge(S("E_terms"), last[k])
                        done += 1
                        last[k] = done
                        dve.scalar_tensor_tensor(out=m.E[:, k, :], in0=RP[:, r, :], scalar=DT * comb(r + k, k),
                                                 in1=m.E[:, k, :], op0=ALU.mult, op1=ALU.add).then_inc(S("E_terms"), 1)
                dve.wait_ge(S("bn_rstd"), 1)
                for k in range(2):
                    bb, g, be, mm_ = (WT[:, 256 + 40 * k + 8 * j:264 + 40 * k + 8 * j] for j in range(4))
                    a, c = m.BNA[:, 8 * k:8 * k + 8], m.BNC[:, 8 * k:8 * k + 8]
                    dve.tensor_tensor(a, g, BNT[:, 1, 8 * k:8 * k + 8], ALU.mult).then_inc(S("bn"), 1)
                    dve.tensor_tensor(c, bb, mm_, ALU.subtract).then_inc(S("bn"), 1)
                    dve.wait_ge(S("bn"), 4 * k + 2)
                    dve.tensor_tensor(c, c, a, ALU.mult).then_inc(S("bn"), 1)
                    dve.wait_ge(S("bn"), 4 * k + 3)
                    dve.tensor_tensor(c, c, be, ALU.add).then_inc(S("bn"), 1)
                for q in range(Q):
                    if q % 16 == 0:
                        dve.wait_ge(S(f"x_loaded{q // 16}"), 64)
                    dve.bn_stats(ST[:, q, :], m.X[:, q * P:(q + 1) * P]).then_inc(S("stats"), 1)
                for q in range(Q):
                    dve.wait_ge(S("stats"), q + 1)
                    dve.bn_aggr(m.MV[:, q, :], ST[:, q, :]).then_inc(S("stats_known"), 1)
                dve.wait_ge(S("columns_zero"), 2)
                for k in range(9):
                    dve.tensor_scalar(BK[:, k, k:k + 1], FB[:, :], float(comb(STEPS, k)), None,
                                      ALU.mult).then_inc(S("fc_b_columns"), 1)
                dve.wait_ge(S("V_product"), 1)
                pv = bank[3][:, 0:16 * T].rearrange("p (t k) -> p t k", t=T)
                dve.tensor_copy(V[:, :, 1:4], pv[:, :, 1:4]).then_inc(S("V_known"), 2)
                dve.tensor_copy(V[:, :, 6:7], pv[:, :, 6:7]).then_inc(S("V_known"), 2)
                dve.wait_ge(S("V_product"), 2)
                dve.tensor_copy(V[:, :, 4:6], pv[:, :, 4:6]).then_inc(S("V_known"), 1)
                dve.tensor_copy(V[:, :, 7:9], pv[:, :, 7:9]).then_inc(S("V_known"), 1)
                dve.wait_ge(S("V_turned"), 1)
                dve.tensor_copy(VT[:, :], bank[0][0:9, :]).then_inc(S("const_parts"), 1)
                dve.wait_ge(S("fc_b_products"), 1)
                dve.tensor_copy(RB[:, :], bank[1][0:9, 0:128]).then_inc(S("const_parts"), 1)
                dve.wait_ge(S("const_known"), 1)
                dve.tensor_copy(m.GB[:, :], bank[2][:, :])
        retire(nc, mem)




def attention(nc, m):
    with ExitStack() as stack:
        mem = Memory(nc, stack)
        S = mem.sem
        H = [mem.sb(f"gat_h{u}", P, T, P) for u in range(2)]
        HTS = [mem.sb(f"gat_ht{u}", P, N) for u in range(2)]
        WH = [mem.sb(f"gat_wh{u}", P, T, 130) for u in range(2)]
        ZM = [mem.sb(f"gat_masked{u}", P, T, N) for u in range(2)]
        V2 = mem.sb("gat_leaky", P, T, N)
        PS = mem.sb("gat_probs", P, T, N)
        PT = [mem.sb(f"gat_probs_t{k}", P, T, P) for k in range(2)]
        C = [mem.sb(f"gat_cols{u}", P, 6, T) for u in range(2)]
        RC = mem.sb("gat_recip", P, T)
        ST = mem.sb("gat_stats", P, T, 6)
        MVS = mem.sb("gat_mean_var", P, T, 2)
        b_ht, = mem.banks("gat_b_ht", 1)
        b_wh = mem.banks("gat_b_wh", 2)
        b_s2 = mem.banks("gat_b_s2", 2)
        b_pt = mem.banks("gat_b_pt", 2)
        b_o, = mem.banks("gat_b_o", 1)

        def turns(eng, body):
            body(0, 0, True, True, True)
            with eng.Fori(0, B // 2 - 2) as i:
                body(2 * i + 1, 1, False, True, True)
                body(2 * i + 2, 0, False, True, True)
            body(B - 3, 1, False, True, True)
            body(B - 2, 0, False, True, False)
            body(B - 1, 1, False, False, False)

        with nc.Block() as block:

            @block.vector
            def _(dve):
                def norm(b, u):
                    wait(dve, S("h_turned"), b - 1)
                    for t in range(T):
                        q = b * T + t
                        dve.tensor_scalar(H[u][:, t, :], m.X[:, bass.ds(q * P, P)], m.MV[:, bass.ds(q, 1), 0],
                                          m.RSTD[:, bass.ds(q, 1)], ALU.subtract, ALU.mult).then_inc(S("h_ready"), 1)

                def mask(b, u, ts):
                    if 0 in ts:
                        wait_apart(dve, S("s2_ready"), b + 1, m.waited)
                        wait_apart(dve, S("exped"), (b - 1) * T, m.waited)
                    for t in ts:
                        dve.tensor_tensor_reduce(ZM[u][:, t, :], b_s2[u][:, :], m.NEGM[:, t, :], 1.0, 3 * NEG, ALU.add,
                                                 ALU.max, C[u][:, 0, t:t + 1]).then_inc(S("masked"), 1)

                def columns(b, u):
                    s1 = WH[u][:, :, 128]
                    dve.wait_ge(S("masked"), b * T + T)
                    dve.wait_ge(S("wh_ready"), b + 1)
                    dve.tensor_tensor(C[u][:, 1, :], s1, C[u][:, 0, :], ALU.add).then_inc(S("cols"), 1)
                    dve.wait_ge(S("cols"), b * 4 + 1)
                    dve.scalar_tensor_tensor(out=C[u][:, 2, :], in0=C[u][:, 1, :], scalar=LEAK, in1=C[u][:, 1, :],
                                             op0=ALU.mult, op1=ALU.max).then_inc(S("cols"), 1)
                    dve.wait_ge(S("cols"), b * 4 + 2)
                    dve.tensor_tensor(C[u][:, 3, :], s1, C[u][:, 2, :], ALU.subtract).then_inc(S("cols"), 1)
                    dve.scalar_tensor_tensor(out=C[u][:, 4, :], in0=s1, scalar=LEAK, in1=C[u][:, 2, :],
                                             op0=ALU.mult, op1=ALU.subtract).then_inc(S("cols"), 1)

                def score(b, u, t):
                    if t == 0:
                        dve.wait_ge(S("cols"), b * 4 + 4)
                    dve.wait_ge(S("leaky_made"), b * T + t + 1)
                    dve.scalar_tensor_tensor(out=ZM[u][:, t, :], in0=ZM[u][:, t, :], scalar=C[u][:, 3, t:t + 1],
                                             in1=V2[:, t, :], op0=ALU.add, op1=ALU.max).then_inc(S("scored"), 1)

                def update(b, u):
                    dve.wait_ge(S("exped"), b * T + T)
                    dve.reciprocal(RC[:, :], C[u][:, 5, :]).then_inc(S("recip"), 1)
                    dve.wait_ge(S("recip"), b + 1)
                    for t in range(T):
                        dve.wait_ge(S("mixed"), b * T + T)
                        xt = m.X[:, bass.ds((b * T + t) * P, P)]
                        dve.scalar_tensor_tensor(out=xt, in0=b_o[:, t * P:(t + 1) * P], scalar=RC[:, t:t + 1], in1=xt,
                                                 op0=ALU.mult, op1=ALU.add).then_inc(S("x1"), 1)

                def stats(b):
                    wait_apart(dve, S("x1"), b * T + T, m.waited)
                    wait_apart(dve, S("stats1_known"), b * T, m.waited)
                    for t in range(T):
                        dve.bn_stats(ST[:, t, :], m.X[:, bass.ds((b * T + t) * P, P)]).then_inc(S("stats1"), 1)

                def means(b):
                    wait_apart(dve, S("stats1"), b * T + T, m.waited)
                    wait_apart(dve, S("stats1_kept"), b, m.waited)
                    for t in range(T):
                        dve.bn_aggr(MVS[:, t, :], ST[:, t, :]).then_inc(S("stats1_known"), 1)

                def keep(b):
                    dve.wait_ge(S("stats1_known"), b * T + T)
                    dve.tensor_scalar(m.MV[:, bass.ds(b * T, T), :], MVS[:, :, :], 1.0, None, ALU.mult)\
                       .then_inc(S("stats1_kept"), 1)

                norm(0, 0)
                norm(1, 1)
                mask(0, 0, range(T))
                columns(0, 0)

                def body(b, u, first, one_ahead, two_ahead):
                    for t in range(T):
                        score(b, u, t)
                    if not first:
                        update(b - 1, 1 - u)
                    if one_ahead:
                        mask(b + 1, 1 - u, (0, 1))
                    if not first:
                        stats(b - 1)
                    if one_ahead:
                        mask(b + 1, 1 - u, (2, 3))
                    if not first:
                        means(b - 1)
                    if one_ahead:
                        columns(b + 1, 1 - u)
                    if not first:
                        keep(b - 1)
                    if two_ahead:
                        norm(b + 2, u)

                turns(dve, body)
                update(B - 1, 1)
                stats(B - 1)
                means(B - 1)
                keep(B - 1)

            @block.tensor
            def _(pe):
                def transposes(b, u):
                    wait(pe, S("ht_ready"), b)
                    for t in range(T):
                        pe.wait_ge(S("h_ready"), b * T + t + 1)
                        mm = pe.transpose(b_ht[:, t * P:(t + 1) * P], H[u][:, t, :], m.IDENT[:, :])
                    mm.then_inc(S("h_turned"), 1)

                def project(b, u):
                    pe.wait_ge(S("ht_ready"), b + 1)
                    wait(pe, S("masked"), (b - 1) * T)
                    pe.matmul(b_s2[u][:, :], m.WA2B[:, :], HTS[u][:, :], start=True, stop=True).then_inc(S("s2_ready"), 1)
                    wait(pe, S("wh_ready"), b)
                    for t in range(T):
                        at = 130 * (t % 2)
                        mm = pe.matmul(b_wh[t // 2][:, at:at + 130], HTS[u][:, t * P:(t + 1) * P], m.WEXT[:, :],
                                       start=True, stop=True)
                    mm.then_inc(S("wh_product"), 1)

                def turn(b, u, t):
                    pe.wait_ge(S("exped"), b * T + t + 1)
                    wait(pe, S("probs_t"), b * T + t - 1)
                    for s in range(T):
                        mm = pe.transpose(b_pt[t % 2][:, s * P:(s + 1) * P], PS[:, t, s * P:(s + 1) * P], m.IDENT[:, :])
                    mm.then_inc(S("probs_turned"), 1)

                def mix(b, u, t):
                    pe.wait_ge(S("probs_t"), b * T + t + 1)
                    if t == 0:
                        wait(pe, S("x1"), b * T)
                    for s in range(T):
                        mm = pe.matmul(b_o[:, t * P:(t + 1) * P], PT[t % 2][:, s, :], WH[u][:, s, 0:128],
                                       start=(s == 0), stop=(s == T - 1))
                    mm.then_inc(S("mixed"), 1)

                for u in range(2):
                    transposes(u, u)
                    project(u, u)

                def body(b, u, first, one_ahead, two_ahead):
                    turn(b, u, 0)
                    turn(b, u, 1)
                    mix(b, u, 0)
                    turn(b, u, 2)
                    mix(b, u, 1)
                    turn(b, u, 3)
                    mix(b, u, 2)
                    if two_ahead:
                        transposes(b + 2, u)
                    mix(b, u, 3)
                    if two_ahead:
                        project(b + 2, u)

                turns(pe, body)

            @block.scalar
            def _(act):
                def keep_ht(b, u):
                    act.wait_ge(S("h_turned"), b + 1)
                    wait(act, S("wh_product"), b - 1)
                    act.activation(HTS[u][:, :], b_ht[:, :], ACT.Copy).then_inc(S("ht_ready"), 1)

                def keep_wh(b, u):
                    act.wait_ge(S("wh_product"), b + 1)
                    wait(act, S("mixed"), (b - 1) * T)
                    wait(act, S("cols"), (b - 1) * 4)
                    act.activation(WH[u][:, 0:2, :], b_wh[0][:, 0:260].rearrange("p (t n) -> p t n", t=2), ACT.Copy)
                    act.activation(WH[u][:, 2:4, :], b_wh[1][:, 0:260].rearrange("p (t n) -> p t n", t=2), ACT.Copy)\
                       .then_inc(S("wh_ready"), 1)

                def leaky(b, u):
                    act.wait_ge(S("cols"), b * 4 + 4)
                    wait(act, S("scored"), b * T)
                    for t in range(T):
                        act.activation(V2[:, t, :], ZM[u][:, t, :], ACT.Identity, bias=C[u][:, 4, t:t + 1], scale=LEAK)\
                           .then_inc(S("leaky_made"), 1)

                def exp(b, u, t):
                    act.wait_ge(S("scored"), b * T + t + 1)
                    if t == 0:
                        wait(act, S("recip"), b - 1)
                        wait(act, S("probs_turned"), b * T)
                    act.activation(PS[:, t, :], ZM[u][:, t, :], ACT.Exp, accum_out=C[u][:, 5, t:t + 1])\
                       .then_inc(S("exped"), 1)

                def evacuate(b, t):
                    act.wait_ge(S("probs_turned"), b * T + t + 1)
                    wait(act, S("mixed"), b * T + t - 1)
                    act.activation(PT[t % 2][:, :, :], tiles(b_pt[t % 2][:, :]), ACT.Copy).then_inc(S("probs_t"), 1)

                for u in range(2):
                    keep_ht(u, u)
                    keep_wh(u, u)
                leaky(0, 0)

                def body(b, u, first, one_ahead, two_ahead):
                    exp(b, u, 0)
                    exp(b, u, 1)
                    evacuate(b, 0)
                    exp(b, u, 2)
                    evacuate(b, 1)
                    exp(b, u, 3)
                    evacuate(b, 2)
                    evacuate(b, 3)
                    if two_ahead:
                        keep_ht(b + 2, u)
                    if one_ahead:
                        leaky(b + 1, 1 - u)
                    if two_ahead:
                        keep_wh(b + 2, u)

                turns(act, body)

        retire(nc, mem)




def normalise(nc, m, name, extra):
    with ExitStack() as stack:
        mem = Memory(nc, stack)
        S = mem.sem
        H = [mem.sb(f"{name}_h{u}", P, T, P) for u in range(2)]
        HTS = [mem.sb(f"{name}_ht{u}", P, N) for u in range(2)]
        b_ht = mem.banks(f"{name}_b_ht", 2)
        x = extra(nc, m, mem, H, HTS)

        with nc.Block() as block:

            @block.gpsimd
            def _(pool):
                pool.tensor_scalar(m.RSTD[:, :], m.MV[:, :, 1], LN_EPS, None, ALU.add).then_inc(S("ln_var"), 1)
                pool.wait_ge(S("ln_var"), 1)
                pool.tensor_tensor(m.RSTD[:, :], m.RSTD[:, :], m.MHALF[:, :], ALU.pow).then_inc(S("rstd_ready"), 1)
                over_batches(pool, lambda *a: x.pool(pool, *a))

            @block.vector
            def _(dve):
                x.dve_start(dve)
                dve.wait_ge(S("rstd_ready"), 1)

                def body(b, u, first, last):
                    wait(dve, S("h_turned"), b - 1)
                    x.wait_h_free(dve, b)
                    for t in range(T):
                        q = b * T + t
                        dve.tensor_scalar(H[u][:, t, :], m.X[:, bass.ds(q * P, P)], m.MV[:, bass.ds(q, 1), 0],
                                          m.RSTD[:, bass.ds(q, 1)], ALU.subtract, ALU.mult).then_inc(S("h_ready"), 1)
                    x.dve(dve, b, u, first, last)

                over_batches(dve, body)
                x.dve_end(dve)

            @block.tensor
            def _(pe):
                def body(b, u, first, last):
                    wait(pe, S("ht_ready"), b - 1)
                    for t in range(T):
                        pe.wait_ge(S("h_ready"), b * T + t + 1)
                        mm = pe.transpose(b_ht[u][:, t * P:(t + 1) * P], H[u][:, t, :], m.IDENT[:, :])
                    mm.then_inc(S("h_turned"), 1)
                    x.pe(pe, b, u, first, last)

                over_batches(pe, body)
                x.pe_end(pe)

            @block.scalar
            def _(act):
                def body(b, u, first, last):
                    act.wait_ge(S("h_turned"), b + 1)
                    wait(act, S(f"ht_kept{u}"), (b - u) * 8)
                    x.wait_ht_free(act, b)
                    act.activation(HTS[u][:, :], b_ht[u][:, :], ACT.Copy).then_inc(S("ht_ready"), 1)

                over_batches(act, body)
                x.act_end(act)

            @block.sync
            def _(sp):
                def body(b, u, first, last):
                    wait_apart(sp, S("ht_ready"), b + 1, m.waited)
                    sp.dma_start(m.HT[:, bass.ds(b * N, N)], HTS[u][:, :]).then_inc(S(f"ht_kept{u}"), 16)

                over_batches(sp, body)
                for u in range(2):
                    sp.wait_ge(S(f"ht_kept{u}"), 16 * B // 2)
        retire(nc, mem)


def mamba_steps(nc, m, mem, H, HTS):
    S = mem.sem
    RAW = mem.sb("dt_raw", P, Q, HEADS)
    EX = mem.sb("dt_exp", P, Q, HEADS)
    U = mem.sb("dt_one_plus", P, Q, HEADS)
    R = mem.sb("dt_recip", P, Q, HEADS)
    LN = mem.sb("dt_ln", P, Q, HEADS)
    b_dt = mem.banks("dt_b", 2)
    b_sum = mem.banks("dt_b_sum", 3)
    wide = [P, Q, HEADS]

    def flat(ap):
        return ap.rearrange("p q h -> p (q h)")

    def pe(e, b, u, first, last):
        e.wait_ge(S("ht_ready"), b + 1)
        wait(e, S("dt_raw"), b - 1)
        for t in range(T):
            mm = e.matmul(b_dt[u][:, HEADS * t:HEADS * t + HEADS], HTS[u][:, t * P:(t + 1) * P], m.WIN[:, 640:644],
                          start=True, stop=True)
        mm.then_inc(S("dt_product"), 1)

    def dve(e, b, u, first, last):
        e.wait_ge(S("dt_product"), b + 1)
        e.scalar_tensor_tensor(out=RAW[:, bass.ds(b * T, T), :].rearrange("p q h -> p (q h)"),
                               in0=b_dt[u][:, 0:T * HEADS], scalar=1.0, in1=DTB16[:, :],
                               op0=ALU.mult, op1=ALU.add).then_inc(S("dt_raw"), 1)

    DTB16 = mem.sb("dt_bias_wide", P, T * HEADS)
    AR = mem.sb("dt_abs", P, Q, HEADS)

    def dve_start(e):
        e.tensor_copy(DTB16[:, :].rearrange("p (t h) -> p t h", t=T), m.DTB[:, :].unsqueeze(1).broadcast_to([P, T, HEADS]))\
         .then_inc(S("dt_bias_wide"), 1)
        e.wait_ge(S("dt_bias_wide"), 1)

    def dve_end(e):
        e.wait_ge(S("dt_exp"), 1)
        e.tensor_scalar(U[:, :, :], EX[:, :, :], 1.0, None, ALU.add).then_inc(S("dt_one_plus"), 1)
        e.wait_ge(S("dt_one_plus"), 1)
        e.reciprocal(R[:, :, :], U[:, :, :]).then_inc(S("dt_rest"), 1)
        e.scalar_tensor_tensor(out=flat(EX[:, :, :]), in0=flat(U[:, :, :]), scalar=1.0, in1=flat(EX[:, :, :]),
                               op0=ALU.subtract, op1=ALU.subtract).then_inc(S("dt_rest"), 1)
        e.wait_ge(S("dt_rest"), 2)
        e.tensor_tensor(EX[:, :, :], EX[:, :, :], R[:, :, :], ALU.mult).then_inc(S("dt_rest"), 1)
        e.wait_ge(S("dt_rest"), 3)
        e.wait_ge(S("dt_ln"), 1)
        e.tensor_tensor(LN[:, :, :], LN[:, :, :], EX[:, :, :], ALU.subtract).then_inc(S("dt_rest"), 1)
        e.wait_ge(S("dt_rest"), 4)
        e.scalar_tensor_tensor(out=flat(m.DTS[:, :, :]), in0=flat(RAW[:, :, :]), scalar=0.0, in1=flat(LN[:, :, :]),
                               op0=ALU.max, op1=ALU.add).then_inc(S("dt_rest"), 1)
        e.wait_ge(S("dt_rest"), 5)
        e.tensor_tensor(m.DA[:, :, :], m.DTS[:, :, :], m.AH[:, :].unsqueeze(1).broadcast_to(wide), ALU.mult)\
         .then_inc(S("dA_positive"), 1)
        e.wait_ge(S("dA_positive"), 1)
        e.tensor_scalar(m.DA[:, :, :], m.DA[:, :, :], -1.0, None, ALU.mult).then_inc(S("dA_ready"), 1)
        e.wait_ge(S("decays"), 3)
        e.tensor_tensor(m.DD[:, :, :], m.DD[:, :, :], m.DTS[:, :, :], ALU.mult)

    def pe_end(e):
        e.wait_ge(S("dA_ready"), 1)
        for k, mask in enumerate((m.LE, m.GT, m.ONES)):
            e.matmul(b_sum[k][:, 0:Q * HEADS], mask[:, :], flat(m.DA[:, :, :]), start=True, stop=True)\
             .then_inc(S("dA_sums"), 1)

    def act_end(act):
        act.wait_ge(S("dt_raw"), B)
        act.activation(AR[:, :, :], RAW[:, :, :], ACT.Abs).then_inc(S("dt_abs"), 1)
        act.wait_ge(S("dt_abs"), 1)
        act.activation(EX[:, :, :], AR[:, :, :], ACT.Exp, scale=-1.0).then_inc(S("dt_exp"), 1)
        act.wait_ge(S("dt_one_plus"), 1)
        act.activation(LN[:, :, :], U[:, :, :], ACT.Ln).then_inc(S("dt_ln"), 1)
        for k, dst in enumerate((m.EA, m.DD, m.CD)):
            act.wait_ge(S("dA_sums"), k + 1)
            act.activation(dst[:, :, :], b_sum[k][:, 0:Q * HEADS].rearrange("p (q h) -> p q h", h=HEADS), ACT.Exp)\
               .then_inc(S("decays"), 1)

    def pool(e, b, u, first, last):
        xb = tiles(m.X[:, bass.ds(b * N, N)])
        wait_apart(e, S("h_ready"), b * T + T, m.waited)
        e.tensor_tensor(xb, xb, m.BLIN[:, :].unsqueeze(1).broadcast_to([P, T, P]), ALU.add)

    return Extra(pe_end, act_end, dve_end, pool, pe=pe, dve=dve, dve_start=dve_start,
                 wait_ht_free=lambda act, b: wait(act, S("dt_product"), b - 1))


def mamba_norm(nc, m):
    normalise(nc, m, "mamba", mamba_steps)




def mamba(nc, m):
    with ExitStack() as stack:
        mem = Memory(nc, stack)
        S = mem.sem
        HB = [mem.sb(f"mb_ht{u}", P, N) for u in range(2)]
        CV = [mem.sb(f"mb_conv{u}", P, 3, N) for u in range(2)]
        XC = [mem.sb(f"mb_xbc{u}", P, 3, N) for u in range(2)]
        CT = [mem.sb(f"mb_ct{u}", STATE, N) for u in range(2)]
        ZS = [mem.sb(f"mb_z{u}", P, T, INNER) for u in range(2)]
        XH = [mem.sb(f"mb_xh{k}", P, 320) for k in range(2)]
        SR = [mem.sb(f"mb_seg_rhs{k}", P, HEADS, P) for k in range(2)]
        ES = [mem.sb(f"mb_seg_exp{k}", P, HEADS, P) for k in range(2)]
        CM = [mem.sb(f"mb_cb{k}", P, P) for k in range(2)]
        XDT = [mem.sb(f"mb_xdt{k}", P, INNER) for k in range(2)]
        XW = [mem.sb(f"mb_xw{k}", P, INNER) for k in range(2)]
        XD = [mem.sb(f"mb_xd{k}", P, INNER) for k in range(2)]
        SS = [mem.sb(f"mb_state{c}", STATE, INNER) for c in range(1, T)]
        Y = [mem.sb(f"mb_y{k}", P, INNER) for k in range(2)]
        YT = [mem.sb(f"mb_yt{k}", P, 2, P) for k in range(2)]
        SQ = mem.sb("mb_square", P, INNER)
        RS = [mem.sb(f"mb_rms{k}", P, 2) for k in range(2)]
        ST = mem.sb("mb_stats", P, T, 6)
        MVS = mem.sb("mb_mean_var", P, T, 2)
        b_pj = mem.banks("mb_b_proj", 2)
        b_x, = mem.banks("mb_b_x", 1)
        b_seg, = mem.banks("mb_b_seg", 1)
        b_cs, = mem.banks("mb_b_cs", 1)
        b_y, = mem.banks("mb_b_y", 1)
        b_yt, = mem.banks("mb_b_yt", 1)
        b_o, = mem.banks("mb_b_o", 1)

        def heads(ap, n=HEADS):
            return ap.rearrange("p (h d) -> p h d", h=n)

        def over_heads(ap, b, c, width=HD, parts=P):
            return ap[0:parts, bass.ds(b * T + c, 1), :].rearrange("p q h -> p (q h)").unsqueeze(2)\
                .broadcast_to([parts, HEADS, width])

        def slot(u, k):
            return (5 * u + k) % 2

        with nc.Block() as block:

            @block.sync
            def _(sp):
                def load(b, u):
                    wait_apart(sp, S("z_product"), 2 * (b - 1), m.waited)
                    sp.dma_start(HB[u][:, :], m.HT[:, bass.ds(b * N, N)]).then_inc(S(f"ht_loaded{u}"), 16)

                def body(b, u, first, last):
                    if not last:
                        load(b + 1, 1 - u)
                    wait_apart(sp, S("xbc_ready"), 3 * b + 3, m.waited)
                    wait_apart(sp, S("outputs"), T * (b - 1), m.waited)
                    sp.dma_start(CT[u][:, :], XC[u][STATE:2 * STATE, 2, :]).then_inc(S(f"c_moved{u}"), 16)

                load(0, 0)
                over_batches(sp, body)
                for u in range(2):
                    sp.wait_ge(S(f"c_moved{u}"), 16 * B // 2)
                    sp.wait_ge(S(f"ht_loaded{u}"), 16 * B // 2)

            @block.tensor
            def _(pe):
                def project(b, u, k):
                    if k == 0:
                        pe.wait_ge(S(f"ht_loaded{u}"), (b - u) * 8 + 16)
                    if k == 0:
                        wait(pe, S("z_ready"), 2 * b - 1)
                    elif k == 1:
                        wait(pe, S("z_ready"), 2 * b)
                    else:
                        pe.wait_ge(S("conv_ready"), 3 * b + k - 1)
                    bank = b_pj[slot(u, k)]
                    if k < 3:
                        pe.matmul(bank[:, :], m.WIN[:, 256 + 128 * k:384 + 128 * k], HB[u][:, :],
                                  start=True, stop=True).then_inc(S("xbc_product"), 1)
                    else:
                        for t in range(2):
                            c = 2 * (k - 3) + t
                            mm = pe.matmul(bank[:, INNER * t:INNER * t + INNER], HB[u][:, c * P:(c + 1) * P],
                                           m.WIN[:, 0:INNER], start=True, stop=True)
                        mm.then_inc(S("z_product"), 1)

                def scores(b, u, c):
                    k = c % 2
                    at = slice(c * P, (c + 1) * P)
                    if c == 0:
                        pe.wait_ge(S("xbc_ready"), 3 * b + 3)
                    wait(pe, S("xh_ready"), T * b + c)
                    for g in range(2):
                        pe.transpose(b_x[:, g * P:(g + 1) * P], XC[u][:, g, at], m.IDENT[:, :])
                    pe.transpose(b_x[:, 256:320], XC[u][0:STATE, 2, at], m.IDENT[0:STATE, 0:STATE])\
                      .then_inc(S("x_turned"), 1)
                    pe.wait_ge(S("seg_rhs"), T * b + c + 1)
                    wait(pe, S("seg_exp"), T * b + c)
                    pe.matmul(b_seg[:, :], m.GT[:, :], SR[k][:, :, :].rearrange("p h l -> p (h l)"),
                              start=True, stop=True).then_inc(S("seg_sums"), 1)
                    if c == 0:
                        pe.wait_ge(S(f"c_moved{u}"), (b - u) * 8 + 16)
                    wait(pe, S("x2"), T * b + c - 2)
                    wait(pe, S("cb_masked"), T * b + c)
                    pe.matmul(b_o[:, 256:384], XC[u][0:STATE, 2, at], CT[u][:, at], start=True, stop=True)\
                      .then_inc(S("cb_product"), 1)

                def outputs(b, u, c):
                    k = c % 2
                    q = T * b + c
                    pe.wait_ge(S("m_ready"), q + 1)
                    pe.wait_ge(S("x_scaled"), 3 * q + 2)
                    wait(pe, S("y_summed"), q)
                    for h in range(HEADS):
                        mm = pe.matmul(b_y[:, HD * h:HD * h + HD], ES[k][:, h, :], XDT[k][:, HD * h:HD * h + HD],
                                       start=True, stop=True)
                    if c:
                        pe.wait_ge(S("states_done"), q)
                        mm = pe.matmul(b_y[:, INNER:2 * INNER], CT[u][:, c * P:(c + 1) * P], SS[c - 1][:, :],
                                       start=True, stop=True)
                    mm.then_inc(S("outputs"), 1)
                    if c < T - 1:
                        wait(pe, S("states_done"), q)
                        pe.matmul(b_cs[0:STATE, 256:512], XH[k][:, 256:320], XW[k][:, :], start=True, stop=True)\
                          .then_inc(S("state_products"), 1)

                def finish(b, u, c):
                    k = c % 2
                    q = T * b + c
                    pe.wait_ge(S("y_ready"), q + 1)
                    wait(pe, S("yt_ready"), q)
                    for g in range(2):
                        mm = pe.transpose(b_yt[:, g * P:(g + 1) * P], Y[k][:, g * P:(g + 1) * P], m.IDENT[:, :])
                    mm.then_inc(S("y_turned"), 1)
                    pe.wait_ge(S("yt_ready"), q + 1)
                    wait(pe, S("x2"), q)
                    pe.wait_ge(S("cb_masked"), min(q + 3, Q) if isinstance(q, int) else q + 3)
                    for g in range(2):
                        mm = pe.matmul(b_o[:, 0:P], YT[k][:, g, :], m.WF[:, g, :], start=(g == 0), stop=(g == 1))
                    mm.then_inc(S("out_product"), 1)

                for k in range(5):
                    project(0, 0, k)
                scores(0, 0, 0)

                def body(b, u, first, last):
                    for c in range(T):
                        if c < T - 1:
                            if not last:
                                project(b + 1, 1 - u, c)
                            scores(b, u, c + 1)
                        elif not last:
                            project(b + 1, 1 - u, 3)
                            project(b + 1, 1 - u, 4)
                            scores(b + 1, 1 - u, 0)
                        outputs(b, u, c)
                        if c:
                            finish(b, u, c - 1)
                        elif not first:
                            finish(b - 1, 1 - u, T - 1)

                over_batches(pe, body)
                finish(B - 1, 1, T - 1)

            @block.scalar
            def _(act):
                def tap(b, u, g):
                    act.wait_ge(S("xbc_product"), 3 * b + g + 1)
                    wait(act, S("xbc_ready"), 3 * (b - 1))
                    act.activation(CV[u][:, g, :], b_pj[slot(u, g)][:, :], ACT.Identity, bias=m.CB[:, g:g + 1],
                                   scale=m.CW[:, g, 3:4]).then_inc(S("tap_ready"), 1)

                def gate(b, u, k):
                    act.wait_ge(S("z_product"), 2 * b + k + 1)
                    wait(act, S("y_ready"), T * (b - 1))
                    act.activation(ZS[u][:, 2 * k:2 * k + 2, :], b_pj[slot(u, 3 + k)][:, :].rearrange("p (t n) -> p t n", t=2),
                                   ACT.Silu).then_inc(S("z_ready"), 1)

                def silu(b, u, g):
                    act.wait_ge(S("conv_ready"), 3 * b + g + 1)
                    wait(act, S("outputs"), T * (b - 1))
                    act.activation(XC[u][:, g, :], CV[u][:, g, :], ACT.Silu).then_inc(S("xbc_ready"), 1)

                def scores(b, u, c):
                    k = c % 2
                    q = T * b + c
                    act.wait_ge(S("x_turned"), q + 1)
                    wait(act, S("x_scaled"), 3 * (q - 1))
                    wait(act, S("outputs"), q - 1)
                    wait(act, S("state_products"), 3 * b + (c - 1 if c else 0))
                    act.activation(XH[k][:, :], b_x[:, 0:320], ACT.Copy).then_inc(S("xh_ready"), 1)
                    act.wait_ge(S("seg_sums"), q + 1)
                    act.activation(ES[k][:, :, :], b_seg[:, :].rearrange("p (h l) -> p h l", h=HEADS), ACT.Exp)\
                       .then_inc(S("seg_exp"), 1)

                def finish(b, u, c):
                    k = c % 2
                    q = T * b + c
                    act.wait_ge(S("y_ready"), q + 1)
                    wait(act, S("rms_ready"), q - 1)
                    wait(act, S("squared"), q)
                    act.activation(SQ[:, :], Y[k][:, :], ACT.Square, accum_out=RS[k][:, 0:1]).then_inc(S("squared"), 1)
                    act.wait_ge(S("y_turned"), q + 1)
                    wait(act, S("out_product"), q - 1)
                    act.activation(YT[k][:, :, :], b_yt[:, 0:256].rearrange("p (g l) -> p g l", g=2), ACT.Copy)\
                       .then_inc(S("yt_ready"), 1)

                for g in range(3):
                    tap(0, 0, g)
                for k in range(2):
                    gate(0, 0, k)
                for g in range(3):
                    silu(0, 0, g)
                scores(0, 0, 0)

                def body(b, u, first, last):
                    for c in range(T):
                        if c < T - 1:
                            if not last:
                                tap(b + 1, 1 - u, c)
                            scores(b, u, c + 1)
                        elif not last:
                            for g in range(3):
                                silu(b + 1, 1 - u, g)
                            for k in range(2):
                                gate(b + 1, 1 - u, k)
                            scores(b + 1, 1 - u, 0)
                        if c:
                            finish(b, u, c - 1)
                        elif not first:
                            finish(b - 1, 1 - u, T - 1)

                over_batches(act, body)
                finish(B - 1, 1, T - 1)

            @block.gpsimd
            def _(pool):
                def rhs(b, u, c):
                    k = c % 2
                    wait_apart(pool, S("seg_sums"), T * b + c - 1, m.waited)
                    pool.tensor_tensor(SR[k][:, :, :], m.LE[:, :].unsqueeze(1).broadcast_to([P, HEADS, P]),
                                       over_heads(m.DA, b, c, P), ALU.mult).then_inc(S("seg_rhs"), 1)

                def scale(b, u, c):
                    k = c % 2
                    q = T * b + c
                    wait(pool, S("outputs"), q - 1)
                    wait(pool, S("state_products"), 3 * b + (c - 1 if c else 0))
                    wait(pool, S("y_ready"), q - 1)
                    wait_apart(pool, S("xh_ready"), q + 1, m.waited)
                    xh = heads(XH[k][:, 0:INNER])
                    pool.tensor_tensor(heads(XDT[k][:, :]), xh, over_heads(m.DTS, b, c), ALU.mult).then_inc(S("x_scaled"), 1)
                    pool.tensor_tensor(heads(XW[k][:, :]), xh, over_heads(m.DD, b, c), ALU.mult).then_inc(S("x_scaled"), 1)
                    pool.tensor_tensor(heads(XD[k][:, :]), xh, m.DH[:, :].unsqueeze(2).broadcast_to([P, HEADS, HD]),
                                       ALU.mult).then_inc(S("x_scaled"), 1)

                def rms(b, u, c):
                    k = c % 2
                    q = T * b + c
                    pool.wait_ge(S("squared"), q + 1)
                    wait_apart(pool, S("x2"), q - 1, m.waited)
                    pool.tensor_scalar(RS[k][:, 1:2], RS[k][:, 0:1], 1.0 / INNER, LN_EPS, ALU.mult, ALU.add)\
                        .then_inc(S("mean_square"), 1)
                    pool.wait_ge(S("mean_square"), q + 1)
                    pool.tensor_tensor(RS[k][:, 1:2], RS[k][:, 1:2], m.MHALF[:, 0:1], ALU.pow).then_inc(S("rms_ready"), 1)

                rhs(0, 0, 0)

                def body(b, u, first, last):
                    for c in range(T):
                        if c < T - 1:
                            rhs(b, u, c + 1)
                        elif not last:
                            rhs(b + 1, 1 - u, 0)
                        scale(b, u, c)
                        if c:
                            rms(b, u, c - 1)
                        elif not first:
                            rms(b - 1, 1 - u, T - 1)

                over_batches(pool, body)
                rms(B - 1, 1, T - 1)

            @block.vector
            def _(dve):
                def conv(b, u, g):
                    for back in range(1, TAPS):
                        if back == 1:
                            dve.wait_ge(S("tap_ready"), 3 * b + g + 1)
                        else:
                            dve.wait_ge(S("taps"), (3 * b + g) * 2 + back - 1)
                        dst = CV[u][:, g, back:N]
                        op = dve.scalar_tensor_tensor(out=dst, in0=b_pj[slot(u, g)][:, 0:N - back],
                                                      scalar=m.CW[:, g, 3 - back:4 - back], in1=dst,
                                                      op0=ALU.mult, op1=ALU.add)
                        op.then_inc(S("taps") if back < TAPS - 1 else S("conv_ready"), 1)

                def scores(b, u, c):
                    k = c % 2
                    q = T * b + c
                    dve.wait_ge(S("cb_product"), q + 1)
                    dve.tensor_tensor(CM[k][:, :], b_o[:, 256:384], m.LE[:, :], ALU.mult).then_inc(S("cb_masked"), 1)
                    dve.wait_ge(S("cb_masked"), q + 1)
                    dve.wait_ge(S("seg_exp"), q + 1)
                    dve.tensor_tensor(ES[k][:, :, :], ES[k][:, :, :], CM[k][:, :].unsqueeze(1).broadcast_to([P, HEADS, P]),
                                      ALU.mult).then_inc(S("m_ready"), 1)

                def states(b, u, c):
                    q = T * b + c
                    if c == T - 1:
                        dve.sem_inc(S("states_done"), 1)
                        return
                    dve.wait_ge(S("state_products"), 3 * b + c + 1)
                    new = SS[c][:, :]
                    if c == 0:
                        wait(dve, S("y_summed"), q - 2)
                        dve.tensor_copy(new, b_cs[0:STATE, 256:512]).then_inc(S("states_done"), 1)
                        return
                    dve.wait_ge(S("states_done"), q)
                    wait_apart(dve, S("states_done"), q, m.waited)
                    dve.tensor_tensor(heads(new), heads(SS[c - 1][:, :]), over_heads(m.CD, b, c, parts=STATE), ALU.mult)\
                       .then_inc(S("decayed"), 1)
                    dve.wait_ge(S("decayed"), 2 * b + c)
                    dve.tensor_tensor(new, new, b_cs[0:STATE, 256:512], ALU.add).then_inc(S("states_done"), 1)

                def combine(b, u, c):
                    k = c % 2
                    q = T * b + c
                    y = Y[k][:, :]
                    dve.wait_ge(S("outputs"), q + 1)
                    dve.wait_ge(S("x_scaled"), 3 * q + 3)
                    wait(dve, S("squared"), q - 1)
                    wait(dve, S("y_turned"), q - 1)
                    if c:
                        wait_apart(dve, S("x_scaled"), 3 * q + 3, m.waited)
                        dve.tensor_tensor(heads(y), heads(b_y[:, INNER:2 * INNER]), over_heads(m.EA, b, c), ALU.mult)\
                           .then_inc(S("y_off"), 1)
                        dve.wait_ge(S("y_off"), 3 * b + c)
                        dve.tensor_tensor(XD[k][:, :], y, XD[k][:, :], ALU.add).then_inc(S("y_off_d"), 1)
                        dve.wait_ge(S("y_off_d"), 3 * b + c)
                    dve.tensor_tensor(y, b_y[:, 0:INNER], XD[k][:, :], ALU.add).then_inc(S("y_summed"), 1)
                    dve.wait_ge(S("y_summed"), q + 1)
                    if c % 2 == 0:
                        dve.wait_ge(S("z_ready"), 2 * b + c // 2 + 1)
                    dve.tensor_tensor(y, y, ZS[u][:, c, :], ALU.mult).then_inc(S("y_ready"), 1)

                def finish(b, u, c):
                    k = c % 2
                    q = T * b + c
                    dve.wait_ge(S("out_product"), q + 1)
                    dve.wait_ge(S("rms_ready"), q + 1)
                    xq = m.X[:, bass.ds(q * P, P)]
                    dve.scalar_tensor_tensor(out=xq, in0=b_o[:, 0:P], scalar=RS[k][:, 1:2], in1=xq, op0=ALU.mult,
                                             op1=ALU.add).then_inc(S("x2"), 1)
                    wait_apart(dve, S("x2"), q + 1, m.waited)
                    wait_apart(dve, S("stats_kept"), b, m.waited) if c == 0 else None
                    dve.bn_stats(ST[:, c, :], xq).then_inc(S("stats2"), 1)
                    wait_apart(dve, S("stats2"), q + 1, m.waited)
                    dve.bn_aggr(MVS[:, c, :], ST[:, c, :]).then_inc(S("stats2_known"), 1)
                    if c == T - 1:
                        dve.wait_ge(S("stats2_known"), q + 1)
                        dve.tensor_scalar(m.MV[:, bass.ds(b * T, T), :], MVS[:, :, :], 1.0, None, ALU.mult)\
                           .then_inc(S("stats_kept"), 1)

                for g in range(3):
                    conv(0, 0, g)
                scores(0, 0, 0)

                def body(b, u, first, last):
                    for c in range(T):
                        if c < T - 1:
                            if not last:
                                conv(b + 1, 1 - u, c)
                            scores(b, u, c + 1)
                        elif not last:
                            scores(b + 1, 1 - u, 0)
                        states(b, u, c)
                        combine(b, u, c)
                        if c:
                            finish(b, u, c - 1)
                        elif not first:
                            finish(b - 1, 1 - u, T - 1)

                over_batches(dve, body)
                finish(B - 1, 1, T - 1)
        retire(nc, mem)




def ode(nc, m):
    with ExitStack() as stack:
        mem = Memory(nc, stack)
        S = mem.sem
        H = [mem.sb(f"ode_h{u}", P, T, P) for u in range(2)]
        ZK = [mem.sb(f"ode_z{u}", P, 3, N) for u in range(2)]
        G = [mem.sb(f"ode_g{u}", P, T, 2 * P) for u in range(2)]
        ST = mem.sb("ode_stats", P, T, 6)
        MVS = mem.sb("ode_mean_var", P, T, 2)
        b_x, = mem.banks("ode_b_x", 1)
        b_z = mem.banks("ode_b_z", 2)
        b_g = mem.banks("ode_b_g", 2)
        b_h = mem.banks("ode_b_h", 2)
        E4 = m.E[:, :, :].rearrange("p (q k) e -> p q k e", k=3)

        with nc.Block() as block:

            @block.gpsimd
            def _(pool):
                pool.tensor_scalar(m.RSTD[:, :], m.MV[:, :, 1], LN_EPS, None, ALU.add).then_inc(S("ln_var"), 1)
                pool.wait_ge(S("ln_var"), 1)
                pool.tensor_tensor(m.RSTD[:, :], m.RSTD[:, :], m.MHALF[:, :], ALU.pow).then_inc(S("rstd_ready"), 1)

                def body(b, u, first, last):
                    wait_apart(pool, S("h_ready"), b * T + T, m.waited)
                    xb = m.X[:, bass.ds(b * N, N)]
                    pool.tensor_tensor(xb, xb, m.GB[:, :], ALU.add).then_inc(S("const_added"), 1)

                over_batches(pool, body)

            @block.vector
            def _(dve):
                def norm(b, u):
                    wait(dve, S("z_product"), 2 * (b - 1))
                    for t in range(T):
                        q = b * T + t
                        dve.tensor_scalar(H[u][:, t, :], m.X[:, bass.ds(q * P, P)], m.MV[:, bass.ds(q, 1), 0],
                                          m.RSTD[:, bass.ds(q, 1)], ALU.subtract, ALU.mult).then_inc(S("h_ready"), 1)

                def z2(b, u):
                    dve.wait_ge(S("z_product"), 2 * b + 2)
                    wait(dve, S("h8"), b - 1)
                    dve.tensor_copy(ZK[u][:, 2, :], b_z[1][:, :]).then_inc(S("z2_ready"), 1)

                def g(b, u):
                    dve.wait_ge(S("g_product"), 2 * b + 2)
                    wait(dve, S("h8"), b - 1)
                    dve.tensor_copy(G[u][:, 2:4, :], b_g[1][:, :].rearrange("p (t n) -> p t n", t=2)).then_inc(S("g_high"), 1)

                def update(b, u):
                    xb = m.X[:, bass.ds(b * N, N)]
                    dve.wait_ge(S("h8"), b + 1)
                    dve.wait_ge(S("const_added"), b + 1)
                    dve.tensor_tensor(xb, b_h[u][:, :], xb, ALU.add).then_inc(S("x3"), 1)
                    wait_apart(dve, S("x3"), b + 1, m.waited)
                    wait_apart(dve, S("stats_kept"), b, m.waited)
                    for t in range(T):
                        dve.bn_stats(ST[:, t, :], m.X[:, bass.ds((b * T + t) * P, P)]).then_inc(S("stats3"), 1)
                    wait_apart(dve, S("stats3"), b * T + T, m.waited)
                    for t in range(T):
                        dve.bn_aggr(MVS[:, t, :], ST[:, t, :]).then_inc(S("stats3_known"), 1)
                    dve.wait_ge(S("stats3_known"), b * T + T)
                    dve.tensor_scalar(m.MV[:, bass.ds(b * T, T), :], MVS[:, :, :], 1.0, None, ALU.mult)\
                       .then_inc(S("stats_kept"), 1)

                dve.wait_ge(S("rstd_ready"), 1)
                norm(0, 0)
                z2(0, 0)
                g(0, 0)

                def body(b, u, first, last):
                    if not last:
                        norm(b + 1, 1 - u)
                        z2(b + 1, 1 - u)
                        update(b, u)
                        g(b + 1, 1 - u)
                    else:
                        update(b, u)

                over_batches(dve, body)

            @block.scalar
            def _(act):
                def z(b, u):
                    wait(act, S("h8"), b - 1)
                    act.wait_ge(S("h_turned"), b + 1)
                    act.activation(ZK[u][:, 0, :], b_x[:, :], ACT.Copy).then_inc(S("z01_ready"), 1)
                    act.wait_ge(S("z_product"), 2 * b + 1)
                    act.activation(ZK[u][:, 1, :], b_z[0][:, :], ACT.Copy).then_inc(S("z01_ready"), 1)

                def g(b, u):
                    act.wait_ge(S("g_product"), 2 * b + 1)
                    act.activation(G[u][:, 0:2, :], b_g[0][:, :].rearrange("p (t n) -> p t n", t=2), ACT.Copy)\
                       .then_inc(S("g_low"), 1)

                z(0, 0)
                g(0, 0)

                def body(b, u, first, last):
                    if not last:
                        z(b + 1, 1 - u)
                        g(b + 1, 1 - u)

                over_batches(act, body)

            @block.tensor
            def _(pe):
                def z(b, u):
                    pe.wait_ge(S("h_ready"), b * T + T)
                    wait(pe, S("z01_ready"), 2 * b)
                    for t in range(T):
                        mm = pe.transpose(b_x[:, t * P:(t + 1) * P], H[u][:, t, :], m.IDENT[:, :])
                    mm.then_inc(S("h_turned"), 1)
                    for k, mat in enumerate((m.LT, m.L2T)):
                        if k:
                            wait(pe, S("z2_ready"), b)
                        for s in range(T):
                            mm = pe.matmul(b_z[k][:, :], H[u][:, s, :], mat[:, s, :], start=(s == 0), stop=(s == T - 1))
                        mm.then_inc(S("z_product"), 1)

                def g(b, u):
                    pe.wait_ge(S("z01_ready"), 2 * b + 2)
                    pe.wait_ge(S("z2_ready"), b + 1)
                    for t in range(T):
                        if t % 2 == 0:
                            wait(pe, S("g_high") if t else S("g_low"), b)
                        for k in range(3):
                            mm = pe.matmul(b_g[t // 2][:, 256 * (t % 2):256 * (t % 2) + 256], ZK[u][:, k, t * P:(t + 1) * P],
                                           E4[:, 1:3, k, :], start=(k == 0), stop=(k == 2))
                        if t % 2:
                            mm.then_inc(S("g_product"), 1)

                def h(b, u, ts):
                    if 0 in ts:
                        pe.wait_ge(S("g_low"), b + 1)
                        pe.wait_ge(S("g_high"), b + 1)
                        wait(pe, S("x3"), b - 1)
                    for t in ts:
                        at = slice(t * P, (t + 1) * P)
                        for k in range(3):
                            pe.matmul(b_h[u][:, at], ZK[u][:, k, at], m.E[:, k, :], start=(k == 0), stop=False)
                        for k, mat in enumerate((m.L3T, m.L6T)):
                            for s in range(T):
                                mm = pe.matmul(b_h[u][:, at], mat[:, s, at], G[u][:, s, k * P:(k + 1) * P],
                                               start=False, stop=(k == 1 and s == T - 1))
                    if T - 1 in ts:
                        mm.then_inc(S("h8"), 1)

                z(0, 0)
                g(0, 0)

                def body(b, u, first, last):
                    h(b, u, (0, 1))
                    if not last:
                        z(b + 1, 1 - u)
                    h(b, u, (2, 3))
                    if not last:
                        g(b + 1, 1 - u)

                over_batches(pe, body)
        retire(nc, mem)




def router(nc, m, mem, H, HTS):
    S = mem.sem
    FE = mem.sb("feat_sum", P, T, P)
    FT = mem.sb("feat_t", P, N)
    LG = mem.sb("logits", P, T, EXPERTS)
    CO = mem.sb("router_cols", P, 2, T)
    W8 = mem.sb("router_rows", EXPERTS, N)
    b_f = mem.banks("rt_b", 6)
    per_expert = [P, T, EXPERTS]

    def pool(e, b, u, first, last):
        e.wait_ge(S("h_ready"), b * T + T)
        if first:
            e.tensor_copy(FE[:, :, :], H[u][:, :, :]).then_inc(S("feat_added"), 1)
        else:
            e.wait_ge(S("feat_added"), b)
            e.tensor_tensor(FE[:, :, :], FE[:, :, :], H[u][:, :, :], ALU.add).then_inc(S("feat_added"), 1)

    def pe_end(pe):
        pe.wait_ge(S("feat_added"), B)
        for t in range(T):
            mm = pe.transpose(b_f[0][:, t * P:(t + 1) * P], FE[:, t, :], m.IDENT[:, :])
        mm.then_inc(S("feat_turned"), 1)
        pe.wait_ge(S("feat_ready"), 1)
        for t in range(T):
            mm = pe.matmul(b_f[1][:, EXPERTS * t:EXPERTS * (t + 1)], FT[:, t * P:(t + 1) * P], m.WR[:, :],
                           start=True, stop=True)
        mm.then_inc(S("logits"), 1)
        pe.wait_ge(S("router_ready"), 1)
        for t in range(T):
            mm = pe.transpose(b_f[0][0:EXPERTS, t * P:(t + 1) * P], LG[:, t, :], m.IDENT[:, :])
        mm.then_inc(S("router_turned"), 1)
        for e in range(EXPERTS):
            k = e % 4
            wait(pe, S("wide_copied"), e - 3)
            for t in range(T):
                mm = pe.matmul(b_f[2 + k][:, t * P:(t + 1) * P], LG[:, t, e:e + 1].broadcast_to([P, P]), m.IDENT[:, :],
                               start=True, stop=True)
            mm.then_inc(S("wide"), 1)
        pe.wait_ge(S("router_rows"), 1)
        for t in range(T):
            mm = pe.matmul(b_f[1][:, t * P:(t + 1) * P], W8[:, t * P:(t + 1) * P], m.BO[:, :], start=True, stop=True)
        mm.then_inc(S("out_bias"), 1)

    def act_end(act):
        act.wait_ge(S("feat_turned"), 1)
        act.activation(FT[:, :], b_f[0][:, :], ACT.Copy, scale=1.0 / B).then_inc(S("feat_ready"), 1)
        act.wait_ge(S("logits_shifted"), 1)
        act.activation(LG[:, :, :], LG[:, :, :], ACT.Exp).then_inc(S("router_exp"), 1)
        for e in range(EXPERTS):
            act.wait_ge(S("wide"), e + 1)
            act.activation(m.RW[:, e, :], b_f[2 + e % 4][:, :], ACT.Copy).then_inc(S("wide_copied"), 1)

    def dve_end(e):
        e.wait_ge(S("logits"), 1)
        e.tensor_tensor(LG[:, :, :], b_f[1][:, 0:T * EXPERTS].rearrange("p (t e) -> p t e", t=T),
                        m.BR[:, :].unsqueeze(1).broadcast_to(per_expert), ALU.add).then_inc(S("softmax"), 1)
        e.wait_ge(S("softmax"), 1)
        e.tensor_reduce(CO[:, 0, :], LG[:, :, :], mybir.AxisListType.X, ALU.max).then_inc(S("softmax"), 1)
        e.wait_ge(S("softmax"), 2)
        e.tensor_tensor(LG[:, :, :], LG[:, :, :], CO[:, 0, :].unsqueeze(2).broadcast_to(per_expert), ALU.subtract)\
         .then_inc(S("logits_shifted"), 1)
        e.wait_ge(S("router_exp"), 1)
        e.tensor_reduce(CO[:, 0, :], LG[:, :, :], mybir.AxisListType.X, ALU.add).then_inc(S("softmax"), 1)
        e.wait_ge(S("softmax"), 3)
        e.reciprocal(CO[:, 1, :], CO[:, 0, :]).then_inc(S("softmax"), 1)
        e.wait_ge(S("softmax"), 4)
        e.tensor_tensor(LG[:, :, :], LG[:, :, :], CO[:, 1, :].unsqueeze(2).broadcast_to(per_expert), ALU.mult)\
         .then_inc(S("router_ready"), 1)
        e.wait_ge(S("router_turned"), 1)
        e.tensor_copy(W8[:, :], b_f[0][0:EXPERTS, :]).then_inc(S("router_rows"), 1)
        e.wait_ge(S("out_bias"), 1)
        e.tensor_copy(m.YB[:, :], b_f[1][:, :])

    return Extra(pe_end, act_end, dve_end, pool, wait_h_free=lambda dve, b: wait(dve, S("feat_added"), b - 1))


def experts(nc, m, out):
    with ExitStack() as stack:
        mem = Memory(nc, stack)
        m.RW = mem.sb("router_wide", P, EXPERTS, N)
        m.YB = mem.sb("expert_bias", P, N)
        normalise(nc, m, "moe", router)
        S = mem.sem
        HB = [mem.sb(f"ex_ht{u}", P, N) for u in range(2)]
        H1 = [mem.sb(f"ex_h1_{k}", P, N) for k in range(4)]
        R2 = [mem.sb(f"ex_r2_{k}", P, N) for k in range(2)]
        HW = [mem.sb(f"ex_hw_{k}", P, N) for k in range(4)]
        O = [mem.sb(f"ex_out{u}", P, N) for u in range(2)]
        b_1 = mem.banks("ex_b_1", 2)
        b_2 = mem.banks("ex_b_2", 2)
        b_y = mem.banks("ex_b_y", 2)
        E = EXPERTS

        def ahead(b, u, e):
            return (b, u, e + 2) if e < E - 2 else (b + 1, 1 - u, e + 2 - E)

        def behind(b, u, e):
            return (b, u, e - 2) if e >= 2 else (b - 1, 1 - u, e - 2 + E)

        with nc.Block() as block:

            @block.sync
            def _(sp):
                def load(b, u):
                    wait_apart(sp, S("product1"), E * (b - 1), m.waited)
                    sp.dma_start(HB[u][:, :], m.HT[:, bass.ds(b * N, N)]).then_inc(S(f"ht_loaded{u}"), 16)

                def body(b, u, first, last):
                    if not last:
                        load(b + 1, 1 - u)
                    wait_apart(sp, S("x4"), b + 1, m.waited)
                    sp.dma_start(out[bass.ds(b, 1)].rearrange("o (t p) d -> p (o t) d", p=P), tiles(O[u][:, :]))\
                      .then_inc(S(f"stored{u}"), 16)

                load(0, 0)
                over_batches(sp, body)
                for u in range(2):
                    sp.wait_ge(S(f"stored{u}"), 16 * B // 2)
                    sp.wait_ge(S(f"ht_loaded{u}"), 16 * B // 2)

            @block.gpsimd
            def _(pool):
                def body(b, u, first, last):
                    xb = m.X[:, bass.ds(b * N, N)]
                    pool.tensor_tensor(xb, xb, m.YB[:, :], ALU.add).then_inc(S("bias_added"), 1)

                over_batches(pool, body)

            @block.tensor
            def _(pe):
                def layer1(b, u, e):
                    if e == 0:
                        pe.wait_ge(S(f"ht_loaded{u}"), (b - u) * 8 + 16)
                    wait(pe, S("relu1"), E * b + e - 1)
                    pe.matmul(b_1[e % 2][:, :], m.W1[:, e, :], HB[u][:, :], start=True, stop=True).then_inc(S("product1"), 1)

                def layer2(b, u, e):
                    pe.wait_ge(S("relu1"), E * b + e + 1)
                    wait(pe, S("relu2"), E * b + e - 1)
                    pe.matmul(b_2[e % 2][:, :], m.W2[:, e, :], H1[e % 4][:, :], start=True, stop=True)\
                      .then_inc(S("product2"), 1)

                def layer3(b, u, e):
                    pe.wait_ge(S("weighted"), E * b + e + 1)
                    if e == 0:
                        wait(pe, S("x4"), b - 1)
                    for t in range(T):
                        at = slice(t * P, (t + 1) * P)
                        mm = pe.matmul(b_y[u][:, at], HW[e % 4][:, at], m.W3[:, e, :], start=(e == 0 and t == 0),
                                       stop=(e == E - 1 and t == T - 1), skip_group_check=True)
                    mm.then_inc(S("product3"), 1)

                layer1(0, 0, 0)
                layer1(0, 0, 1)

                def body(b, u, first, last):
                    for e in range(E):
                        if not (last and e >= E - 2):
                            layer1(*ahead(b, u, e))
                        layer2(b, u, e)
                        if not (first and e < 2):
                            layer3(*behind(b, u, e))

                over_batches(pe, body)
                layer3(B - 1, 1, E - 2)
                layer3(B - 1, 1, E - 1)

            @block.scalar
            def _(act):
                def relu1(b, u, e):
                    act.wait_ge(S("product1"), E * b + e + 1)
                    wait(act, S("product2"), E * b + e - 3)
                    act.activation(H1[e % 4][:, :], b_1[e % 2][:, :], ACT.Relu, bias=m.BNC[:, e:e + 1],
                                   scale=m.BNA[:, e:e + 1]).then_inc(S("relu1"), 1)

                def relu2(b, u, e):
                    act.wait_ge(S("product2"), E * b + e + 1)
                    wait(act, S("weighted"), E * b + e - 1)
                    act.activation(R2[e % 2][:, :], b_2[e % 2][:, :], ACT.Relu, bias=m.BNC[:, E + e:E + e + 1],
                                   scale=m.BNA[:, E + e:E + e + 1]).then_inc(S("relu2"), 1)

                relu1(0, 0, 0)
                relu1(0, 0, 1)

                def body(b, u, first, last):
                    for e in range(E):
                        if not (last and e >= E - 2):
                            relu1(*ahead(b, u, e))
                        relu2(b, u, e)

                over_batches(act, body)

            @block.vector
            def _(dve):
                def weigh(b, u, e):
                    dve.wait_ge(S("relu2"), E * b + e + 1)
                    wait(dve, S("product3"), E * b + e - 3)
                    dve.tensor_tensor(HW[e % 4][:, :], R2[e % 2][:, :], m.RW[:, e, :], ALU.mult).then_inc(S("weighted"), 1)

                def update(b, u):
                    dve.wait_ge(S("product3"), E * b + E)
                    dve.wait_ge(S("bias_added"), b + 1)
                    wait(dve, S(f"stored{u}"), (b - u) * 8)
                    dve.tensor_tensor(O[u][:, :], b_y[u][:, :], m.X[:, bass.ds(b * N, N)], ALU.add).then_inc(S("x4"), 1)

                def body(b, u, first, last):
                    for e in range(E):
                        weigh(b, u, e)
                        if e == 2 and not first:
                            update(b - 1, 1 - u)

                over_batches(dve, body)
                update(B - 1, 1)
        retire(nc, mem)



def build(nc, IN, out):
    with ExitStack() as stack:
        mem = Memory(nc, stack)
        sb = mem.sb
        m = Shared()
        m.waited = mem.sem("waited")
        m.X = sb("X", P, Q * P)
        m.HT = sb("HT", P, Q * P)
        m.MV = sb("mean_var", P, Q, 2)
        m.RSTD = sb("rstd", P, Q)
        m.IDENT = sb("ident", P, P)
        m.LE = sb("mask_le", P, P)
        m.GT = sb("mask_gt", P, P)
        m.ONES = sb("ones", P, P)
        m.MHALF = sb("minus_half", P, Q)
        m.NEGM = sb("neg_mask", P, T, N)
        m.WEXT = sb("gat_w_ext", P, 130)
        m.WA2B = sb("gat_wa2_wide", P, P)
        m.LT = sb("LT", P, T, N)
        m.L2T = sb("L2T", P, T, N)
        m.L3T = sb("L3T", P, T, N)
        m.L6T = sb("L6T", P, T, N)
        m.E = sb("E", P, 9, 128)
        m.GB = sb("ode_const", P, N)
        m.WIN = sb("mamba_in_w", P, 644)
        m.CW = sb("conv_w", P, 3, 4)
        m.CB = sb("conv_b", P, 3)
        m.DTB = sb("dt_bias", P, 4)
        m.AH = sb("exp_a_log", P, 4)
        m.DH = sb("d_wide", P, 4)
        m.BLIN = sb("b_lin_wide", P, 128)
        m.WF = sb("mamba_w_out_lin", P, 2, 128)
        m.DTS = sb("dt", P, Q, HEADS)
        m.DA = sb("dA", P, Q, HEADS)
        m.EA = sb("decay_in", P, Q, HEADS)
        m.DD = sb("dt_decay_out", P, Q, HEADS)
        m.CD = sb("chunk_decay", P, Q, HEADS)
        m.W1 = sb("w1", P, 8, 128)
        m.W2 = sb("w2", P, 8, 128)
        m.W3 = sb("w3", P, 8, 128)
        m.WR = sb("w_router", P, 8)
        m.BR = sb("b_router", P, 8)
        m.BO = sb("b_out", 8, 128)
        m.BNA = sb("bn_a", P, 16)
        m.BNC = sb("bn_c", P, 16)
        with nc.allow_non_contiguous_dma(reason="a few columns of weights"):
            setup(nc, m, IN)
        attention(nc, m)
        mamba_norm(nc, m)
        mamba(nc, m)
        ode(nc, m)
        experts(nc, m, out)


_INS = ['x', 'adj', 'L0_gnn_W', 'L0_gnn_a', 'L0_ffn_W_in', 'L0_ffn_conv_w', 'L0_ffn_conv_b', 'L0_ffn_dt_bias',
        'L0_ffn_A_log', 'L0_ffn_D', 'L0_ffn_norm_w', 'L0_ffn_W_out', 'L0_ffn_W_lin', 'L0_ffn_b_lin',
        'L1_gnn_alpha_train', 'L1_gnn_w', 'L1_gnn_d', 'L1_gnn_fc_in_w', 'L1_gnn_fc_in_b', 'L1_ffn_Wr', 'L1_ffn_br',
        'L1_ffn_W1', 'L1_ffn_b1', 'L1_ffn_g1', 'L1_ffn_be1', 'L1_ffn_m1', 'L1_ffn_v1', 'L1_ffn_W2', 'L1_ffn_b2',
        'L1_ffn_g2', 'L1_ffn_be2', 'L1_ffn_m2', 'L1_ffn_v2', 'L1_ffn_Wo', 'L1_ffn_bo']


def kernel(**inputs):
    import numpy as np
    import concourse.bacc as bacc
    from concourse.bass_utils import run_bass_kernel_spmd

    nc = bacc.Bacc("TRN2", target_bir_lowering=False, num_devices=1)
    arrays, IN = {}, {}
    for name in _INS:
        a = np.ascontiguousarray(inputs[name])
        arrays[f"in_{name}"] = a
        IN[name] = nc.dram_tensor(f"in_{name}", a.shape, mybir.dt.from_np(a.dtype), kind="ExternalInput").ap()
    out = nc.dram_tensor("out", (B, N, D), F32, kind="ExternalOutput").ap()
    build(nc, IN, out)
    r = run_bass_kernel_spmd(nc, [arrays], core_ids=[0])
    return r.results[0]["out"]
```

```python
from contextlib import ExitStack
from math import comb

import concourse.bass as bass
from concourse import mybir

F32 = mybir.dt.float32
F32R = mybir.dt.float32r
ALU = mybir.AluOpType
ACT = mybir.ActivationFunctionType

P = 128
B, N, D = 16, 512, 128
T = N // P
Q = B * T
LN_EPS = 1e-5
NEG = -1e30
LEAK = 0.2
HEADS, HD, STATE, INNER, TAPS = 4, 64, 64, 256, 4
STEPS = 8
DT = 1.0 / STEPS
EXPERTS = 8
BN_EPS = 1e-3


def wait(eng, sem, value):
    if isinstance(value, int) and value <= 0:
        return
    eng.wait_ge(sem, value)


def wait_apart(eng, sem, value, seen):
    wait(eng, sem, value)
    eng.sem_inc(seen, 1)


def over_batches(eng, body):
    body(0, 0, True, False)
    body(1, 1, False, False)
    body(2, 0, False, False)
    with eng.Fori(0, B // 2 - 2) as i:
        body(2 * i + 3, 1, False, False)
        body(2 * i + 4, 0, False, False)
    body(B - 1, 1, False, True)


def turns(eng, body):
    body(0, 0, True, True, True)
    body(1, 1, False, True, True)
    body(2, 0, False, True, True)
    with eng.Fori(0, B // 2 - 3) as i:
        body(2 * i + 3, 1, False, True, True)
        body(2 * i + 4, 0, False, True, True)
    body(B - 3, 1, False, True, True)
    body(B - 2, 0, False, True, False)
    body(B - 1, 1, False, False, False)


def nothing(*unused):
    pass


class Shared:
    pass


class Extra:

    def __init__(self, pe_end, act_end, dve_end, pool, wait_h_free=nothing, wait_ht_free=nothing,
                 pe=nothing, dve=nothing, dve_start=nothing, pe_start=nothing):
        self.pe, self.dve, self.pool = pe, dve, pool
        self.pe_end, self.act_end, self.dve_end = pe_end, act_end, dve_end
        self.pe_start, self.dve_start = pe_start, dve_start
        self.wait_h_free, self.wait_ht_free = wait_h_free, wait_ht_free


class Memory:

    def __init__(self, nc, stack):
        self.nc, self.stack = nc, stack
        self.known = {}

    def sb(self, name, *shape, dt=F32):
        return self.stack.enter_context(self.nc.sbuf_tensor(name, list(shape), dt))

    def banks(self, name, count):
        return [self.stack.enter_context(self.nc.psum_tensor(f"{name}{k}", [P, 512], F32)) for k in range(count)]

    def sem(self, name):
        if name not in self.known:
            self.known[name] = self.stack.enter_context(self.nc.semaphore(name))
        return self.known[name]


class Halves:

    def __init__(self, mem, name, *shape):
        self.high = mem.sb(name + "_high", *shape, dt=F32R)
        self.low = mem.sb(name + "_low", *shape, dt=F32R)
        self.seen = self.high[tuple(slice(None) for _ in shape)].bitcast(F32)

    def at(self, *index):
        return self.high[(slice(None), *index)], self.low[(slice(None), *index)]


def in_halves(pe, out, left, right, start, stop):
    pe.matmul(out, left[0], right[0], start=start, stop=False, skip_group_check=True)
    pe.matmul(out, left[0], right[1], start=False, stop=False, skip_group_check=True)
    return pe.matmul(out, left[1], right[0], start=False, stop=stop, skip_group_check=True)


def retire(nc, mem):
    numbers = sorted(s.num for s in mem.known.values())
    with nc.Block() as block:

        @block.sync
        def _(sp):
            first = prev = numbers[0]
            for n in numbers[1:] + [None]:
                if n is not None and n == prev + 1:
                    prev = n
                    continue
                sp.sem_clear(range(first, prev + 1))
                first = prev = n


def tiles(ap, t=T):
    return ap.rearrange("p (t d) -> p t d", t=t)




def setup(nc, m, IN):
    with ExitStack() as stack:
        mem = Memory(nc, stack)
        S = mem.sem
        W0 = mem.sb("gat_w", P, 128)
        A12 = mem.sb("gat_a", P, 2)
        GW = mem.sb("ode_w", P, 128)
        FW = mem.sb("fc_w", P, 128)
        FB = mem.sb("fc_b", P, 1)
        DC = mem.sb("ode_d", P, 1)
        WO = mem.sb("mamba_out_w", P, 2, 128)
        WL = mem.sb("mamba_lin_w", P, 128)
        NW = mem.sb("mamba_norm_w", P, 2)
        AL = mem.sb("alpha", P, T)
        SG = mem.sb("alpha_scaled", P, 3, T)
        BNR = mem.sb("bn_rows", 80, 128)
        BNT = mem.sb("bn_tmp", P, 2, 16)
        WT = mem.sb("turned_weights", P, 336)
        WOT = mem.sb("mamba_out_w_turned", P, 256)
        WTD = mem.sb("ode_wt_scaled", P, 128)
        RI = mem.sb("ode_decay_ident", P, 128)
        ADJ = mem.sb("adj", P, T, N)
        L = mem.sb("L", P, T, N)
        L3 = mem.sb("L3", P, T, N)
        RP = mem.sb("R_powers", P, 9, 128)
        FRP = mem.sb("F_R_powers", P, 9, 128)
        BK = mem.sb("fc_b_columns", P, 9, 9)
        V = mem.sb("L_powers_on_ones", P, T, 9)
        VT = mem.sb("L_powers_rows", 9, N)
        RB = mem.sb("fc_b_R_powers", 9, 128)
        ST = mem.sb("stats", P, Q, 6)
        bank = mem.banks("setup_bank", 8)

        def col(ap):
            return ap.rearrange("(p o) -> p o", o=1)

        def wide(ap, n):
            return ap.rearrange("(o n) -> o n", o=1).broadcast_to([P, n])

        with nc.Block() as block:

            @block.sync
            def _(sp):
                sp.dma_start(ADJ[:, :, :], IN["adj"].rearrange("(t p) m -> p t m", p=P)).then_inc(S("adj_loaded"), 16)
                for g in range(4):
                    for b in range(4 * g, 4 * g + 4):
                        sp.dma_start(tiles(m.X[:, b * 512:(b + 1) * 512]),
                                     IN["x"][b].rearrange("(t p) d -> p t d", p=P)).then_inc(S(f"x_loaded{g}"), 16)
                for dst, name, form in ((m.W1, "L1_ffn_W1", "e d h -> d e h"), (m.W2, "L1_ffn_W2", "e d h -> d e h"),
                                        (m.W3, "L1_ffn_Wo", "e d h -> d e h")):
                    sp.dma_start(dst[:, :, :], IN[name].rearrange(form)).then_inc(S("experts_loaded"), 16)
                sp.wait_ge(S("experts_loaded"), 48)

            @block.gpsimd
            def _(pool):
                pool.memset(m.IDENT[:, :], 0.0).then_inc(S("pool_zero"), 1)
                pool.memset(m.LE[:, :], 1.0).then_inc(S("pool_zero"), 1)
                pool.memset(m.GT[:, :], 1.0).then_inc(S("pool_zero"), 1)
                pool.memset(m.ONES[:, :], 1.0).then_inc(S("pool_zero"), 1)
                pool.memset(m.MHALF[:, :], -0.5).then_inc(S("pool_zero"), 1)
                pool.memset(BK[:, :, :], 0.0).then_inc(S("columns_zero"), 1)
                pool.memset(V[:, :, :], 1.0).then_inc(S("columns_zero"), 1)
                pool.wait_ge(S("pool_zero"), 5)
                pool.affine_select(out=m.IDENT[:, :], in_=m.IDENT[:, :], compare_op=ALU.not_equal, fill=1.0,
                                   base=0, pattern=[[-1, P]], channel_multiplier=1).then_inc(S("masks"), 1)
                pool.affine_select(out=m.LE[:, :], in_=m.LE[:, :], compare_op=ALU.is_ge, fill=0.0,
                                   base=0, pattern=[[1, P]], channel_multiplier=-1).then_inc(S("masks"), 1)
                pool.affine_select(out=m.GT[:, :], in_=m.GT[:, :], compare_op=ALU.is_gt, fill=0.0,
                                   base=0, pattern=[[-1, P]], channel_multiplier=1).then_inc(S("masks"), 1)
                pool.wait_ge(S("turned_copied"), 1)
                for k, at in enumerate((256 + 32, 256 + 72)):
                    pool.tensor_scalar(BNT[:, 0, 8 * k:8 * k + 8], WT[:, at:at + 8], BN_EPS, None,
                                       ALU.add).then_inc(S("bn_var"), 1)
                pool.wait_ge(S("bn_var"), 2)
                pool.tensor_tensor(BNT[:, 1, :], BNT[:, 0, :], m.MHALF[:, 0:16], ALU.pow).then_inc(S("bn_rstd"), 1)
                pool.wait_ge(S("stats_known"), Q)
                pool.tensor_scalar(m.RSTD[:, :], m.MV[:, :, 1], LN_EPS, None, ALU.add).then_inc(S("ln_var"), 1)
                pool.wait_ge(S("ln_var"), 1)
                pool.tensor_tensor(m.RSTD[:, :], m.RSTD[:, :], m.MHALF[:, :], ALU.pow)

            @block.scalar
            def _(act):
                n = 0
                for dst, src in ((W0[:, :], IN["L0_gnn_W"]), (A12[:, :], IN["L0_gnn_a"].rearrange("(k p) o -> p (k o)", k=2)),
                                 (GW[:, :], IN["L1_gnn_w"]), (FW[:, :], IN["L1_gnn_fc_in_w"]),
                                 (FB[:, :], col(IN["L1_gnn_fc_in_b"])), (DC[:, :], col(IN["L1_gnn_d"])),
                                 (WO[:, :, :], IN["L0_ffn_W_out"].rearrange("(g p) n -> p g n", p=P)),
                                 (WL[:, :], IN["L0_ffn_W_lin"]),
                                 (NW[:, :], IN["L0_ffn_norm_w"].rearrange("(g p) -> p g", p=P)),
                                 (AL[:, :], IN["L1_gnn_alpha_train"].rearrange("(t p) -> p t", p=P))):
                    act.dma_start(dst, src).then_inc(S("weights_loaded"), 16)
                for k, name in enumerate(("b1", "g1", "be1", "m1", "v1", "b2", "g2", "be2", "m2", "v2")):
                    act.dma_start(BNR[8 * k:8 * k + 8, :], IN["L1_ffn_" + name]).then_inc(S("weights_loaded"), 16)
                for dst, src in ((m.WIN[:, :], IN["L0_ffn_W_in"]),
                                 (m.CW[:, :, :], IN["L0_ffn_conv_w"].rearrange("(g p) k -> p g k", p=P)),
                                 (m.CB[:, :], IN["L0_ffn_conv_b"].rearrange("(g p) -> p g", p=P)),
                                 (m.DTB[:, :], wide(IN["L0_ffn_dt_bias"], 4)), (m.AH[:, :], wide(IN["L0_ffn_A_log"], 4)),
                                 (m.DH[:, :], wide(IN["L0_ffn_D"], 4)), (m.BLIN[:, :], wide(IN["L0_ffn_b_lin"], 128)),
                                 (m.WR[:, :], IN["L1_ffn_Wr"]), (m.BR[:, :], wide(IN["L1_ffn_br"], 8)),
                                 (m.BO[:, :], IN["L1_ffn_bo"])):
                    act.dma_start(dst, src).then_inc(S("later_loaded"), 16)
                act.wait_ge(S("weights_loaded"), 16 * 20)
                act.activation(SG[:, 0, :], AL[:, :], ACT.Exp, scale=-1.0).then_inc(S("alpha_exp"), 1)
                act.wait_ge(S("turned"), 1)
                act.activation(WT[:, :], bank[0][:, 0:336], ACT.Copy).then_inc(S("turned_copied"), 1)
                act.wait_ge(S("turned"), 2)
                act.activation(WOT[:, :], bank[1][:, 0:256], ACT.Copy).then_inc(S("turned_copied"), 1)
                for k, dst in enumerate((m.LT, m.L2T, m.L3T, L3, m.L6T)):
                    for t in range(T):
                        act.wait_ge(S("L_product"), T * k + t + 1)
                        act.activation(dst[:, t, :], bank[4 + t][:, :], ACT.Copy).then_inc(S("L_copied"), 1)
                act.wait_ge(S("later_loaded"), 16 * 10)
                act.activation(m.AH[:, :], m.AH[:, :], ACT.Exp)

            @block.tensor
            def _(pe):
                pe.wait_ge(S("masks"), 3)
                pe.wait_ge(S("weights_loaded"), 16 * 20)
                pe.transpose(bank[0][:, 0:128], W0[:, :], m.IDENT[:, :])
                pe.transpose(bank[0][:, 128:256], GW[:, :], m.IDENT[:, :])
                pe.transpose(bank[0][:, 256:336], BNR[:, :], m.IDENT[0:80, 0:80]).then_inc(S("turned"), 1)
                pe.transpose(bank[1][:, 0:128], WO[:, 0, :], m.IDENT[:, :])
                pe.transpose(bank[1][:, 128:256], WO[:, 1, :], m.IDENT[:, :]).then_inc(S("turned"), 1)
                pe.wait_ge(S("turned_copied"), 2)
                pe.wait_ge(S("ode_wt_scaled"), 1)
                pe.matmul(bank[2][:, 0:2], WT[:, 0:128], A12[:, :], start=True, stop=True)
                pe.matmul(bank[2][:, 128:256], WT[:, 128:256], WTD[:, :], start=True, stop=True)
                for g in range(2):
                    mm = pe.matmul(bank[2][:, 256 + 128 * g:384 + 128 * g], WOT[:, 128 * g:128 * g + 128], WL[:, :],
                                   start=True, stop=True)
                mm.then_inc(S("small_products"), 1)
                pe.wait_ge(S("R_known"), 1)
                pe.matmul(bank[3][:, 0:128], RP[:, 1, :], RP[:, 1, :], start=True, stop=True).then_inc(S("R_product"), 1)
                pe.wait_ge(S("R_known"), 2)
                pe.matmul(bank[3][:, 0:256], RP[:, 2, :], RP[:, 1:3, :], start=True, stop=True).then_inc(S("R_product"), 1)
                pe.wait_ge(S("R_known"), 3)
                pe.matmul(bank[3][:, :], RP[:, 4, :], RP[:, 1:5, :], start=True, stop=True).then_inc(S("R_product"), 1)
                pe.wait_ge(S("R_known"), 4)
                for k, n in ((0, 4), (4, 4), (8, 1)):
                    if k:
                        pe.wait_ge(S("FR_copied"), k // 4)
                    pe.matmul(bank[3][:, 0:128 * n], FW[:, :], RP[:, k:k + n, :], start=True, stop=True)\
                      .then_inc(S("FR_product"), 1)
                pe.wait_ge(S("L_known"), T)
                for t in range(T):
                    for s in range(T):
                        mm = pe.transpose(bank[4 + t][:, s * P:(s + 1) * P], L[:, s, t * P:(t + 1) * P], m.IDENT[:, :])
                    mm.then_inc(S("L_product"), 1)

                def power(k, left, right):
                    pe.wait_ge(S("L_copied"), T * k)
                    for t in range(T):
                        for s in range(T):
                            mm = pe.matmul(bank[4 + t][:, :], left[:, s, t * P:(t + 1) * P], right[:, s, :],
                                           start=(s == 0), stop=(s == T - 1))
                        mm.then_inc(S("L_product"), 1)

                power(1, L, m.LT)
                power(2, L, m.L2T)
                pe.wait_ge(S("L_copied"), 3 * T)
                for t in range(T):
                    for s in range(T):
                        mm = pe.transpose(bank[4 + t][:, s * P:(s + 1) * P], m.L3T[:, s, t * P:(t + 1) * P], m.IDENT[:, :])
                    mm.then_inc(S("L_product"), 1)
                power(4, L3, m.L3T)
                pe.wait_ge(S("L_copied"), 5 * T)
                pe.wait_ge(S("columns_zero"), 2)
                pe.wait_ge(S("FR_copied"), 3)
                for t in range(T):
                    for k, mat in ((1, m.LT), (2, m.L2T), (3, m.L3T), (6, m.L6T)):
                        for s in range(T):
                            mm = pe.matmul(bank[3][:, 16 * t + k:16 * t + k + 1], mat[:, s, t * P:(t + 1) * P], V[:, s, 0:1],
                                           start=(s == 0), stop=(s == T - 1))
                mm.then_inc(S("V_product"), 1)
                pe.wait_ge(S("V_known"), 4)
                for t in range(T):
                    for k, mat in ((4, m.L3T), (7, m.L6T)):
                        for s in range(T):
                            mm = pe.matmul(bank[3][:, 16 * t + k:16 * t + k + 2], mat[:, s, t * P:(t + 1) * P], V[:, s, 1:3],
                                           start=(s == 0), stop=(s == T - 1))
                mm.then_inc(S("V_product"), 1)
                pe.wait_ge(S("V_known"), 6)
                for t in range(T):
                    mm = pe.transpose(bank[0][0:9, t * P:(t + 1) * P], V[:, t, :], m.IDENT[:, :])
                mm.then_inc(S("V_turned"), 1)
                pe.wait_ge(S("fc_b_columns"), 9)
                for k in range(9):
                    mm = pe.matmul(bank[1][0:9, 0:128], BK[:, k, :], RP[:, 8 - k, :], start=(k == 0), stop=(k == 8))
                mm.then_inc(S("fc_b_products"), 1)
                pe.wait_ge(S("const_parts"), 2)
                for t in range(T):
                    mm = pe.matmul(bank[2][:, t * P:(t + 1) * P], VT[:, t * P:(t + 1) * P], RB[:, :], start=True, stop=True)
                mm.then_inc(S("const_known"), 1)

            @block.vector
            def _(dve):
                dve.wait_ge(S("weights_loaded"), 16 * 20)
                dve.wait_ge(S("alpha_exp"), 1)
                dve.tensor_scalar(SG[:, 0, :], SG[:, 0, :], 1.0, None, ALU.add).then_inc(S("alpha"), 1)
                dve.wait_ge(S("alpha"), 1)
                dve.reciprocal(SG[:, 2, :], SG[:, 0, :]).then_inc(S("alpha"), 1)
                dve.wait_ge(S("alpha"), 2)
                dve.tensor_scalar(SG[:, 1, :], SG[:, 2, :], 0.5 * DT, None, ALU.mult).then_inc(S("alpha"), 1)
                dve.wait_ge(S("alpha"), 3)
                dve.tensor_scalar(SG[:, 2, :], SG[:, 1, :], -1.0, None, ALU.mult).then_inc(S("alpha"), 1)
                dve.wait_ge(S("alpha"), 4)
                dve.wait_ge(S("adj_loaded"), 16)
                dve.wait_ge(S("masks"), 3)
                for t in range(T):
                    dve.tensor_scalar(L[:, t, :], ADJ[:, t, :], SG[:, 1, t:t + 1], None, ALU.mult).then_inc(S("L_adj"), 1)
                for t in range(T):
                    dve.wait_ge(S("L_adj"), t + 1)
                    diag = L[:, t, t * P:(t + 1) * P]
                    dve.scalar_tensor_tensor(out=diag, in0=m.IDENT[:, :], scalar=SG[:, 2, t:t + 1], in1=diag,
                                             op0=ALU.mult, op1=ALU.add).then_inc(S("L_known"), 1)
                dve.tensor_scalar(m.NEGM[:, :, :], ADJ[:, :, :], 0.0, NEG, ALU.is_equal, ALU.mult)
                dve.tensor_scalar(DC[:, :], DC[:, :], 0.0, 1.0, ALU.max, ALU.min).then_inc(S("clipped"), 1)
                dve.wait_ge(S("clipped"), 1)
                dve.wait_ge(S("turned_copied"), 1)
                dve.tensor_scalar(WTD[:, :], WT[:, 128:256], DC[:, 0:1], None, ALU.mult).then_inc(S("ode_wt_scaled"), 1)
                dve.tensor_scalar(RI[:, :], m.IDENT[:, :], 1.0 - DT, None, ALU.mult).then_inc(S("decay_ident"), 1)
                dve.tensor_copy(RP[:, 0, :], m.IDENT[:, :])
                dve.tensor_copy(m.WEXT[:, 0:128], W0[:, :])
                dve.wait_ge(S("decay_ident"), 1)
                dve.wait_ge(S("small_products"), 1)
                dve.scalar_tensor_tensor(out=RP[:, 1, :], in0=bank[2][:, 128:256], scalar=DT, in1=RI[:, :],
                                         op0=ALU.mult, op1=ALU.add).then_inc(S("R_known"), 1)
                dve.tensor_copy(m.WEXT[:, 128:130], bank[2][:, 0:2]).then_inc(S("wa_known"), 1)
                for g in range(2):
                    dve.tensor_scalar(m.WF[:, g, :], bank[2][:, 256 + 128 * g:384 + 128 * g], NW[:, g:g + 1], None, ALU.mult)
                dve.wait_ge(S("wa_known"), 1)
                dve.tensor_copy(m.WA2B[:, :], m.WEXT[:, 129:130].broadcast_to([P, P]))
                for k, (at, n) in enumerate(((2, 1), (3, 2), (5, 4))):
                    dve.wait_ge(S("R_product"), k + 1)
                    dve.tensor_copy(RP[:, at:at + n, :], bank[3][:, 0:128 * n].rearrange("p (k n) -> p k n", k=n))\
                       .then_inc(S("R_known"), 1)
                for k, n in ((0, 4), (4, 4), (8, 1)):
                    dve.wait_ge(S("FR_product"), k // 4 + 1)
                    dve.tensor_copy(FRP[:, k:k + n, :], bank[3][:, 0:128 * n].rearrange("p (k n) -> p k n", k=n))\
                       .then_inc(S("FR_copied"), 1)
                dve.wait_ge(S("R_known"), 4)
                dve.wait_ge(S("FR_copied"), 3)
                done = 0
                last = [0] * 9
                for k in range(9):
                    done += 1
                    last[k] = done
                    dve.tensor_scalar(m.E[:, k, :], FRP[:, STEPS - k, :], float(comb(STEPS, k)), None,
                                      ALU.mult).then_inc(S("E_terms"), 1)
                for r in range(STEPS):
                    for k in range(STEPS - r):
                        dve.wait_ge(S("E_terms"), last[k])
                        done += 1
                        last[k] = done
                        dve.scalar_tensor_tensor(out=m.E[:, k, :], in0=RP[:, r, :], scalar=DT * comb(r + k, k),
                                                 in1=m.E[:, k, :], op0=ALU.mult, op1=ALU.add).then_inc(S("E_terms"), 1)
                dve.wait_ge(S("bn_rstd"), 1)
                for k in range(2):
                    bb, g, be, mm_ = (WT[:, 256 + 40 * k + 8 * j:264 + 40 * k + 8 * j] for j in range(4))
                    a, c = m.BNA[:, 8 * k:8 * k + 8], m.BNC[:, 8 * k:8 * k + 8]
                    dve.tensor_tensor(a, g, BNT[:, 1, 8 * k:8 * k + 8], ALU.mult).then_inc(S("bn"), 1)
                    dve.tensor_tensor(c, bb, mm_, ALU.subtract).then_inc(S("bn"), 1)
                    dve.wait_ge(S("bn"), 4 * k + 2)
                    dve.tensor_tensor(c, c, a, ALU.mult).then_inc(S("bn"), 1)
                    dve.wait_ge(S("bn"), 4 * k + 3)
                    dve.tensor_tensor(c, c, be, ALU.add).then_inc(S("bn"), 1)
                for q in range(Q):
                    if q % 16 == 0:
                        dve.wait_ge(S(f"x_loaded{q // 16}"), 64)
                    dve.bn_stats(ST[:, q, :], m.X[:, q * P:(q + 1) * P]).then_inc(S("stats"), 1)
                for q in range(Q):
                    dve.wait_ge(S("stats"), q + 1)
                    dve.bn_aggr(m.MV[:, q, :], ST[:, q, :]).then_inc(S("stats_known"), 1)
                dve.wait_ge(S("columns_zero"), 2)
                for k in range(9):
                    dve.tensor_scalar(BK[:, k, k:k + 1], FB[:, :], float(comb(STEPS, k)), None,
                                      ALU.mult).then_inc(S("fc_b_columns"), 1)
                dve.wait_ge(S("V_product"), 1)
                pv = bank[3][:, 0:16 * T].rearrange("p (t k) -> p t k", t=T)
                dve.tensor_copy(V[:, :, 1:4], pv[:, :, 1:4]).then_inc(S("V_known"), 2)
                dve.tensor_copy(V[:, :, 6:7], pv[:, :, 6:7]).then_inc(S("V_known"), 2)
                dve.wait_ge(S("V_product"), 2)
                dve.tensor_copy(V[:, :, 4:6], pv[:, :, 4:6]).then_inc(S("V_known"), 1)
                dve.tensor_copy(V[:, :, 7:9], pv[:, :, 7:9]).then_inc(S("V_known"), 1)
                dve.wait_ge(S("V_turned"), 1)
                dve.tensor_copy(VT[:, :], bank[0][0:9, :]).then_inc(S("const_parts"), 1)
                dve.wait_ge(S("fc_b_products"), 1)
                dve.tensor_copy(RB[:, :], bank[1][0:9, 0:128]).then_inc(S("const_parts"), 1)
                dve.wait_ge(S("const_known"), 1)
                dve.tensor_copy(m.GB[:, :], bank[2][:, :])
        retire(nc, mem)




def attention(nc, m):
    with ExitStack() as stack:
        mem = Memory(nc, stack)
        S = mem.sem
        H = [mem.sb(f"gat_h{u}", P, T, P) for u in range(2)]
        HTS = [mem.sb(f"gat_ht{u}", P, N) for u in range(2)]
        WH = [mem.sb(f"gat_wh{u}", P, T, 130) for u in range(2)]
        ZM = [mem.sb(f"gat_masked{u}", P, T, N) for u in range(2)]
        V2 = mem.sb("gat_leaky", P, T, N)
        PS = mem.sb("gat_probs", P, T, N)
        PT = [mem.sb(f"gat_probs_t{k}", P, T, P) for k in range(2)]
        C = [mem.sb(f"gat_cols{u}", P, 6, T) for u in range(2)]
        RC = mem.sb("gat_recip", P, T)
        ST = mem.sb("gat_stats", P, T, 6)
        MVS = mem.sb("gat_mean_var", P, T, 2)
        b_ht, = mem.banks("gat_b_ht", 1)
        b_wh = mem.banks("gat_b_wh", 2)
        b_s2 = mem.banks("gat_b_s2", 2)
        b_pt = mem.banks("gat_b_pt", 2)
        b_o, = mem.banks("gat_b_o", 1)

        with nc.Block() as block:

            @block.vector
            def _(dve):
                def norm(b, u):
                    wait(dve, S("h_turned"), b - 1)
                    for t in range(T):
                        q = b * T + t
                        dve.tensor_scalar(H[u][:, t, :], m.X[:, bass.ds(q * P, P)], m.MV[:, bass.ds(q, 1), 0],
                                          m.RSTD[:, bass.ds(q, 1)], ALU.subtract, ALU.mult).then_inc(S("h_ready"), 1)

                def mask(b, u, ts):
                    if 0 in ts:
                        wait_apart(dve, S("s2_ready"), b + 1, m.waited)
                        wait_apart(dve, S("exped"), (b - 1) * T, m.waited)
                    for t in ts:
                        dve.tensor_tensor_reduce(ZM[u][:, t, :], b_s2[u][:, :], m.NEGM[:, t, :], 1.0, 3 * NEG, ALU.add,
                                                 ALU.max, C[u][:, 0, t:t + 1]).then_inc(S("masked"), 1)

                def columns(b, u):
                    s1 = WH[u][:, :, 128]
                    dve.wait_ge(S("masked"), b * T + T)
                    dve.wait_ge(S("wh_ready"), b + 1)
                    dve.tensor_tensor(C[u][:, 1, :], s1, C[u][:, 0, :], ALU.add).then_inc(S("cols"), 1)
                    dve.wait_ge(S("cols"), b * 4 + 1)
                    dve.scalar_tensor_tensor(out=C[u][:, 2, :], in0=C[u][:, 1, :], scalar=LEAK, in1=C[u][:, 1, :],
                                             op0=ALU.mult, op1=ALU.max).then_inc(S("cols"), 1)
                    dve.wait_ge(S("cols"), b * 4 + 2)
                    dve.tensor_tensor(C[u][:, 3, :], s1, C[u][:, 2, :], ALU.subtract).then_inc(S("cols"), 1)
                    dve.scalar_tensor_tensor(out=C[u][:, 4, :], in0=s1, scalar=LEAK, in1=C[u][:, 2, :],
                                             op0=ALU.mult, op1=ALU.subtract).then_inc(S("cols"), 1)

                def score(b, u, t):
                    if t == 0:
                        dve.wait_ge(S("cols"), b * 4 + 4)
                    dve.wait_ge(S("leaky_made"), b * T + t + 1)
                    dve.scalar_tensor_tensor(out=ZM[u][:, t, :], in0=ZM[u][:, t, :], scalar=C[u][:, 3, t:t + 1],
                                             in1=V2[:, t, :], op0=ALU.add, op1=ALU.max).then_inc(S("scored"), 1)

                def update(b, u):
                    dve.wait_ge(S("exped"), b * T + T)
                    dve.reciprocal(RC[:, :], C[u][:, 5, :]).then_inc(S("recip"), 1)
                    dve.wait_ge(S("recip"), b + 1)
                    for t in range(T):
                        dve.wait_ge(S("mixed"), b * T + T)
                        xt = m.X[:, bass.ds((b * T + t) * P, P)]
                        dve.scalar_tensor_tensor(out=xt, in0=b_o[:, t * P:(t + 1) * P], scalar=RC[:, t:t + 1], in1=xt,
                                                 op0=ALU.mult, op1=ALU.add).then_inc(S("x1"), 1)

                def stats(b):
                    wait_apart(dve, S("x1"), b * T + T, m.waited)
                    wait_apart(dve, S("stats1_known"), b * T, m.waited)
                    for t in range(T):
                        dve.bn_stats(ST[:, t, :], m.X[:, bass.ds((b * T + t) * P, P)]).then_inc(S("stats1"), 1)

                def means(b):
                    wait_apart(dve, S("stats1"), b * T + T, m.waited)
                    wait_apart(dve, S("stats1_kept"), b, m.waited)
                    for t in range(T):
                        dve.bn_aggr(MVS[:, t, :], ST[:, t, :]).then_inc(S("stats1_known"), 1)

                def keep(b):
                    dve.wait_ge(S("stats1_known"), b * T + T)
                    dve.tensor_scalar(m.MV[:, bass.ds(b * T, T), :], MVS[:, :, :], 1.0, None, ALU.mult)\
                       .then_inc(S("stats1_kept"), 1)

                norm(0, 0)
                norm(1, 1)
                mask(0, 0, range(T))
                columns(0, 0)

                def body(b, u, first, one_ahead, two_ahead):
                    for t in range(T):
                        score(b, u, t)
                    if not first:
                        update(b - 1, 1 - u)
                    if one_ahead:
                        mask(b + 1, 1 - u, (0, 1))
                    if not first:
                        stats(b - 1)
                    if one_ahead:
                        mask(b + 1, 1 - u, (2, 3))
                    if not first:
                        means(b - 1)
                    if one_ahead:
                        columns(b + 1, 1 - u)
                    if not first:
                        keep(b - 1)
                    if two_ahead:
                        norm(b + 2, u)

                turns(dve, body)
                update(B - 1, 1)
                stats(B - 1)
                means(B - 1)
                keep(B - 1)

            @block.tensor
            def _(pe):
                def transposes(b, u):
                    wait(pe, S("ht_ready"), b)
                    for t in range(T):
                        pe.wait_ge(S("h_ready"), b * T + t + 1)
                        mm = pe.transpose(b_ht[:, t * P:(t + 1) * P], H[u][:, t, :], m.IDENT[:, :])
                    mm.then_inc(S("h_turned"), 1)

                def project(b, u):
                    pe.wait_ge(S("ht_ready"), b + 1)
                    wait(pe, S("masked"), (b - 1) * T)
                    pe.matmul(b_s2[u][:, :], m.WA2B[:, :], HTS[u][:, :], start=True, stop=True).then_inc(S("s2_ready"), 1)
                    wait(pe, S("wh_ready"), b)
                    for t in range(T):
                        at = 130 * (t % 2)
                        mm = pe.matmul(b_wh[t // 2][:, at:at + 130], HTS[u][:, t * P:(t + 1) * P], m.WEXT[:, :],
                                       start=True, stop=True)
                    mm.then_inc(S("wh_product"), 1)

                def turn(b, u, t):
                    pe.wait_ge(S("exped"), b * T + t + 1)
                    wait(pe, S("probs_t"), b * T + t - 1)
                    for s in range(T):
                        mm = pe.transpose(b_pt[t % 2][:, s * P:(s + 1) * P], PS[:, t, s * P:(s + 1) * P], m.IDENT[:, :])
                    mm.then_inc(S("probs_turned"), 1)

                def mix(b, u, t):
                    pe.wait_ge(S("probs_t"), b * T + t + 1)
                    if t == 0:
                        wait(pe, S("x1"), b * T)
                    for s in range(T):
                        mm = pe.matmul(b_o[:, t * P:(t + 1) * P], PT[t % 2][:, s, :], WH[u][:, s, 0:128],
                                       start=(s == 0), stop=(s == T - 1))
                    mm.then_inc(S("mixed"), 1)

                for u in range(2):
                    transposes(u, u)
                    project(u, u)

                def body(b, u, first, one_ahead, two_ahead):
                    turn(b, u, 0)
                    turn(b, u, 1)
                    mix(b, u, 0)
                    turn(b, u, 2)
                    mix(b, u, 1)
                    turn(b, u, 3)
                    mix(b, u, 2)
                    if two_ahead:
                        transposes(b + 2, u)
                    mix(b, u, 3)
                    if two_ahead:
                        project(b + 2, u)

                turns(pe, body)

            @block.scalar
            def _(act):
                def keep_ht(b, u):
                    act.wait_ge(S("h_turned"), b + 1)
                    wait(act, S("wh_product"), b - 1)
                    act.activation(HTS[u][:, :], b_ht[:, :], ACT.Copy).then_inc(S("ht_ready"), 1)

                def keep_wh(b, u):
                    act.wait_ge(S("wh_product"), b + 1)
                    wait(act, S("mixed"), (b - 1) * T)
                    wait(act, S("cols"), (b - 1) * 4)
                    act.activation(WH[u][:, 0:2, :], b_wh[0][:, 0:260].rearrange("p (t n) -> p t n", t=2), ACT.Copy)
                    act.activation(WH[u][:, 2:4, :], b_wh[1][:, 0:260].rearrange("p (t n) -> p t n", t=2), ACT.Copy)\
                       .then_inc(S("wh_ready"), 1)

                def leaky(b, u):
                    act.wait_ge(S("cols"), b * 4 + 4)
                    wait(act, S("scored"), b * T)
                    for t in range(T):
                        act.activation(V2[:, t, :], ZM[u][:, t, :], ACT.Identity, bias=C[u][:, 4, t:t + 1], scale=LEAK)\
                           .then_inc(S("leaky_made"), 1)

                def exp(b, u, t):
                    act.wait_ge(S("scored"), b * T + t + 1)
                    if t == 0:
                        wait(act, S("recip"), b - 1)
                        wait(act, S("probs_turned"), b * T)
                    act.activation(PS[:, t, :], ZM[u][:, t, :], ACT.Exp, accum_out=C[u][:, 5, t:t + 1])\
                       .then_inc(S("exped"), 1)

                def evacuate(b, t):
                    act.wait_ge(S("probs_turned"), b * T + t + 1)
                    wait(act, S("mixed"), b * T + t - 1)
                    act.activation(PT[t % 2][:, :, :], tiles(b_pt[t % 2][:, :]), ACT.Copy).then_inc(S("probs_t"), 1)

                for u in range(2):
                    keep_ht(u, u)
                    keep_wh(u, u)
                leaky(0, 0)

                def body(b, u, first, one_ahead, two_ahead):
                    exp(b, u, 0)
                    exp(b, u, 1)
                    evacuate(b, 0)
                    exp(b, u, 2)
                    evacuate(b, 1)
                    exp(b, u, 3)
                    evacuate(b, 2)
                    evacuate(b, 3)
                    if two_ahead:
                        keep_ht(b + 2, u)
                    if one_ahead:
                        leaky(b + 1, 1 - u)
                    if two_ahead:
                        keep_wh(b + 2, u)

                turns(act, body)

        retire(nc, mem)




def normalise(nc, m, name, extra):
    with ExitStack() as stack:
        mem = Memory(nc, stack)
        S = mem.sem
        H = [mem.sb(f"{name}_h{u}", P, T, P) for u in range(2)]
        HTS = [mem.sb(f"{name}_ht{u}", P, N) for u in range(2)]
        b_ht = mem.banks(f"{name}_b_ht", 2)
        x = extra(nc, m, mem, H, HTS)

        with nc.Block() as block:

            @block.gpsimd
            def _(pool):
                pool.tensor_scalar(m.RSTD[:, :], m.MV[:, :, 1], LN_EPS, None, ALU.add).then_inc(S("ln_var"), 1)
                pool.wait_ge(S("ln_var"), 1)
                pool.tensor_tensor(m.RSTD[:, :], m.RSTD[:, :], m.MHALF[:, :], ALU.pow).then_inc(S("rstd_ready"), 1)
                over_batches(pool, lambda *a: x.pool(pool, *a))

            @block.vector
            def _(dve):
                x.dve_start(dve)
                dve.wait_ge(S("rstd_ready"), 1)

                def body(b, u, first, last):
                    wait(dve, S("h_turned"), b - 1)
                    x.wait_h_free(dve, b)
                    for t in range(T):
                        q = b * T + t
                        dve.tensor_scalar(H[u][:, t, :], m.X[:, bass.ds(q * P, P)], m.MV[:, bass.ds(q, 1), 0],
                                          m.RSTD[:, bass.ds(q, 1)], ALU.subtract, ALU.mult).then_inc(S("h_ready"), 1)
                    x.dve(dve, b, u, first, last)

                over_batches(dve, body)
                x.dve_end(dve)

            @block.tensor
            def _(pe):
                def body(b, u, first, last):
                    wait(pe, S("ht_ready"), b - 1)
                    for t in range(T):
                        pe.wait_ge(S("h_ready"), b * T + t + 1)
                        mm = pe.transpose(b_ht[u][:, t * P:(t + 1) * P], H[u][:, t, :], m.IDENT[:, :])
                    mm.then_inc(S("h_turned"), 1)
                    x.pe(pe, b, u, first, last)

                x.pe_start(pe)
                over_batches(pe, body)
                x.pe_end(pe)

            @block.scalar
            def _(act):
                def body(b, u, first, last):
                    act.wait_ge(S("h_turned"), b + 1)
                    wait(act, S(f"ht_kept{u}"), (b - u) * 8)
                    x.wait_ht_free(act, b)
                    act.activation(HTS[u][:, :], b_ht[u][:, :], ACT.Copy).then_inc(S("ht_ready"), 1)

                over_batches(act, body)
                x.act_end(act)

            @block.sync
            def _(sp):
                def body(b, u, first, last):
                    wait_apart(sp, S("ht_ready"), b + 1, m.waited)
                    sp.dma_start(m.HT[:, bass.ds(b * N, N)], HTS[u][:, :]).then_inc(S(f"ht_kept{u}"), 16)

                over_batches(sp, body)
                for u in range(2):
                    sp.wait_ge(S(f"ht_kept{u}"), 16 * B // 2)
        retire(nc, mem)


def mamba_steps(nc, m, mem, H, HTS):
    S = mem.sem
    RAW = mem.sb("dt_raw", P, Q, HEADS)
    EX = mem.sb("dt_exp", P, Q, HEADS)
    U = mem.sb("dt_one_plus", P, Q, HEADS)
    R = mem.sb("dt_recip", P, Q, HEADS)
    LN = mem.sb("dt_ln", P, Q, HEADS)
    b_dt = mem.banks("dt_b", 2)
    b_sum = mem.banks("dt_b_sum", 3)
    wide = [P, Q, HEADS]

    def flat(ap):
        return ap.rearrange("p q h -> p (q h)")

    def pe(e, b, u, first, last):
        e.wait_ge(S("ht_ready"), b + 1)
        wait(e, S("dt_raw"), b - 1)
        for t in range(T):
            mm = e.matmul(b_dt[u][:, HEADS * t:HEADS * t + HEADS], HTS[u][:, t * P:(t + 1) * P], m.WIN[:, 640:644],
                          start=True, stop=True)
        mm.then_inc(S("dt_product"), 1)

    def dve(e, b, u, first, last):
        e.wait_ge(S("dt_product"), b + 1)
        e.scalar_tensor_tensor(out=RAW[:, bass.ds(b * T, T), :].rearrange("p q h -> p (q h)"),
                               in0=b_dt[u][:, 0:T * HEADS], scalar=1.0, in1=DTB16[:, :],
                               op0=ALU.mult, op1=ALU.add).then_inc(S("dt_raw"), 1)

    DTB16 = mem.sb("dt_bias_wide", P, T * HEADS)
    AR = mem.sb("dt_abs", P, Q, HEADS)

    def dve_start(e):
        e.tensor_copy(DTB16[:, :].rearrange("p (t h) -> p t h", t=T), m.DTB[:, :].unsqueeze(1).broadcast_to([P, T, HEADS]))\
         .then_inc(S("dt_bias_wide"), 1)
        e.wait_ge(S("dt_bias_wide"), 1)

    def dve_end(e):
        e.wait_ge(S("dt_exp"), 1)
        e.tensor_scalar(U[:, :, :], EX[:, :, :], 1.0, None, ALU.add).then_inc(S("dt_one_plus"), 1)
        e.wait_ge(S("dt_one_plus"), 1)
        e.reciprocal(R[:, :, :], U[:, :, :]).then_inc(S("dt_rest"), 1)
        e.scalar_tensor_tensor(out=flat(EX[:, :, :]), in0=flat(U[:, :, :]), scalar=1.0, in1=flat(EX[:, :, :]),
                               op0=ALU.subtract, op1=ALU.subtract).then_inc(S("dt_rest"), 1)
        e.wait_ge(S("dt_rest"), 2)
        e.tensor_tensor(EX[:, :, :], EX[:, :, :], R[:, :, :], ALU.mult).then_inc(S("dt_rest"), 1)
        e.wait_ge(S("dt_rest"), 3)
        e.wait_ge(S("dt_ln"), 1)
        e.tensor_tensor(LN[:, :, :], LN[:, :, :], EX[:, :, :], ALU.subtract).then_inc(S("dt_rest"), 1)
        e.wait_ge(S("dt_rest"), 4)
        e.scalar_tensor_tensor(out=flat(m.DTS[:, :, :]), in0=flat(RAW[:, :, :]), scalar=0.0, in1=flat(LN[:, :, :]),
                               op0=ALU.max, op1=ALU.add).then_inc(S("dt_rest"), 1)
        e.wait_ge(S("dt_rest"), 5)
        e.tensor_tensor(m.DA[:, :, :], m.DTS[:, :, :], m.AH[:, :].unsqueeze(1).broadcast_to(wide), ALU.mult)\
         .then_inc(S("dA_positive"), 1)
        e.wait_ge(S("dA_positive"), 1)
        e.tensor_scalar(m.DA[:, :, :], m.DA[:, :, :], -1.0, None, ALU.mult).then_inc(S("dA_ready"), 1)
        e.wait_ge(S("decays"), 3)
        e.tensor_tensor(m.DD[:, :, :], m.DD[:, :, :], m.DTS[:, :, :], ALU.mult)

    def pe_end(e):
        e.wait_ge(S("dA_ready"), 1)
        for k, mask in enumerate((m.LE, m.GT, m.ONES)):
            e.matmul(b_sum[k][:, 0:Q * HEADS], mask[:, :], flat(m.DA[:, :, :]), start=True, stop=True)\
             .then_inc(S("dA_sums"), 1)

    def act_end(act):
        act.wait_ge(S("dt_raw"), B)
        act.activation(AR[:, :, :], RAW[:, :, :], ACT.Abs).then_inc(S("dt_abs"), 1)
        act.wait_ge(S("dt_abs"), 1)
        act.activation(EX[:, :, :], AR[:, :, :], ACT.Exp, scale=-1.0).then_inc(S("dt_exp"), 1)
        act.wait_ge(S("dt_one_plus"), 1)
        act.activation(LN[:, :, :], U[:, :, :], ACT.Ln).then_inc(S("dt_ln"), 1)
        for k, dst in enumerate((m.EA, m.DD, m.CD)):
            act.wait_ge(S("dA_sums"), k + 1)
            act.activation(dst[:, :, :], b_sum[k][:, 0:Q * HEADS].rearrange("p (q h) -> p q h", h=HEADS), ACT.Exp)\
               .then_inc(S("decays"), 1)

    def pool(e, b, u, first, last):
        xb = tiles(m.X[:, bass.ds(b * N, N)])
        wait_apart(e, S("h_ready"), b * T + T, m.waited)
        e.tensor_tensor(xb, xb, m.BLIN[:, :].unsqueeze(1).broadcast_to([P, T, P]), ALU.add)

    return Extra(pe_end, act_end, dve_end, pool, pe=pe, dve=dve, dve_start=dve_start,
                 wait_ht_free=lambda act, b: wait(act, S("dt_product"), b - 1))


def mamba_norm(nc, m):
    normalise(nc, m, "mamba", mamba_steps)




def mamba(nc, m):
    with ExitStack() as stack:
        mem = Memory(nc, stack)
        S = mem.sem
        HB = [mem.sb(f"mb_ht{u}", P, N) for u in range(2)]
        CV = [mem.sb(f"mb_conv{u}", P, 3, N) for u in range(2)]
        XC = [mem.sb(f"mb_xbc{u}", P, 3, N) for u in range(2)]
        CT = [mem.sb(f"mb_ct{u}", STATE, N) for u in range(2)]
        ZS = [mem.sb(f"mb_z{u}", P, T, INNER) for u in range(2)]
        XH = [mem.sb(f"mb_xh{k}", P, 320) for k in range(2)]
        SR = [mem.sb(f"mb_seg_rhs{k}", P, HEADS, P) for k in range(2)]
        ES = [mem.sb(f"mb_seg_exp{k}", P, HEADS, P) for k in range(2)]
        CM = [mem.sb(f"mb_cb{k}", P, P) for k in range(2)]
        XDT = [mem.sb(f"mb_xdt{k}", P, INNER) for k in range(2)]
        XW = [mem.sb(f"mb_xw{k}", P, INNER) for k in range(2)]
        XD = [mem.sb(f"mb_xd{k}", P, INNER) for k in range(2)]
        SS = [mem.sb(f"mb_state{c}", STATE, INNER) for c in range(1, T)]
        Y = [mem.sb(f"mb_y{k}", P, INNER) for k in range(2)]
        YT = [mem.sb(f"mb_yt{k}", P, 2, P) for k in range(2)]
        SQ = mem.sb("mb_square", P, INNER)
        RS = [mem.sb(f"mb_rms{k}", P, 2) for k in range(2)]
        ST = mem.sb("mb_stats", P, T, 6)
        MVS = mem.sb("mb_mean_var", P, T, 2)
        b_pj = mem.banks("mb_b_proj", 2)
        b_x, = mem.banks("mb_b_x", 1)
        b_seg, = mem.banks("mb_b_seg", 1)
        b_cs, = mem.banks("mb_b_cs", 1)
        b_y, = mem.banks("mb_b_y", 1)
        b_yt, = mem.banks("mb_b_yt", 1)
        b_o, = mem.banks("mb_b_o", 1)

        def heads(ap, n=HEADS):
            return ap.rearrange("p (h d) -> p h d", h=n)

        def over_heads(ap, b, c, width=HD, parts=P):
            return ap[0:parts, bass.ds(b * T + c, 1), :].rearrange("p q h -> p (q h)").unsqueeze(2)\
                .broadcast_to([parts, HEADS, width])

        def slot(u, k):
            return (5 * u + k) % 2

        with nc.Block() as block:

            @block.sync
            def _(sp):
                def load(b, u):
                    wait_apart(sp, S("z_product"), 2 * (b - 1), m.waited)
                    sp.dma_start(HB[u][:, :], m.HT[:, bass.ds(b * N, N)]).then_inc(S(f"ht_loaded{u}"), 16)

                def body(b, u, first, last):
                    if not last:
                        load(b + 1, 1 - u)
                    wait_apart(sp, S("xbc_ready"), 3 * b + 3, m.waited)
                    wait_apart(sp, S("outputs"), T * (b - 1), m.waited)
                    sp.dma_start(CT[u][:, :], XC[u][STATE:2 * STATE, 2, :]).then_inc(S(f"c_moved{u}"), 16)

                load(0, 0)
                over_batches(sp, body)
                for u in range(2):
                    sp.wait_ge(S(f"c_moved{u}"), 16 * B // 2)
                    sp.wait_ge(S(f"ht_loaded{u}"), 16 * B // 2)

            @block.tensor
            def _(pe):
                def project(b, u, k):
                    if k == 0:
                        pe.wait_ge(S(f"ht_loaded{u}"), (b - u) * 8 + 16)
                    if k == 0:
                        wait(pe, S("z_ready"), 2 * b - 1)
                    elif k == 1:
                        wait(pe, S("z_ready"), 2 * b)
                    else:
                        pe.wait_ge(S("conv_ready"), 3 * b + k - 1)
                    bank = b_pj[slot(u, k)]
                    if k < 3:
                        pe.matmul(bank[:, :], m.WIN[:, 256 + 128 * k:384 + 128 * k], HB[u][:, :],
                                  start=True, stop=True).then_inc(S("xbc_product"), 1)
                    else:
                        for t in range(2):
                            c = 2 * (k - 3) + t
                            mm = pe.matmul(bank[:, INNER * t:INNER * t + INNER], HB[u][:, c * P:(c + 1) * P],
                                           m.WIN[:, 0:INNER], start=True, stop=True)
                        mm.then_inc(S("z_product"), 1)

                def scores(b, u, c):
                    k = c % 2
                    at = slice(c * P, (c + 1) * P)
                    if c == 0:
                        pe.wait_ge(S("xbc_ready"), 3 * b + 3)
                    wait(pe, S("xh_ready"), T * b + c)
                    for g in range(2):
                        pe.transpose(b_x[:, g * P:(g + 1) * P], XC[u][:, g, at], m.IDENT[:, :])
                    pe.transpose(b_x[:, 256:320], XC[u][0:STATE, 2, at], m.IDENT[0:STATE, 0:STATE])\
                      .then_inc(S("x_turned"), 1)
                    pe.wait_ge(S("seg_rhs"), T * b + c + 1)
                    wait(pe, S("seg_exp"), T * b + c)
                    pe.matmul(b_seg[:, :], m.GT[:, :], SR[k][:, :, :].rearrange("p h l -> p (h l)"),
                              start=True, stop=True).then_inc(S("seg_sums"), 1)
                    if c == 0:
                        pe.wait_ge(S(f"c_moved{u}"), (b - u) * 8 + 16)
                    wait(pe, S("x2"), T * b + c - 2)
                    wait(pe, S("cb_masked"), T * b + c)
                    pe.matmul(b_o[:, 256:384], XC[u][0:STATE, 2, at], CT[u][:, at], start=True, stop=True)\
                      .then_inc(S("cb_product"), 1)

                def outputs(b, u, c):
                    k = c % 2
                    q = T * b + c
                    pe.wait_ge(S("m_ready"), q + 1)
                    pe.wait_ge(S("x_scaled"), 3 * q + 2)
                    wait(pe, S("y_summed"), q)
                    for h in range(HEADS):
                        mm = pe.matmul(b_y[:, HD * h:HD * h + HD], ES[k][:, h, :], XDT[k][:, HD * h:HD * h + HD],
                                       start=True, stop=True)
                    if c:
                        pe.wait_ge(S("states_done"), q)
                        mm = pe.matmul(b_y[:, INNER:2 * INNER], CT[u][:, c * P:(c + 1) * P], SS[c - 1][:, :],
                                       start=True, stop=True)
                    mm.then_inc(S("outputs"), 1)
                    if c < T - 1:
                        wait(pe, S("states_done"), q)
                        pe.matmul(b_cs[0:STATE, 256:512], XH[k][:, 256:320], XW[k][:, :], start=True, stop=True)\
                          .then_inc(S("state_products"), 1)

                def finish(b, u, c):
                    k = c % 2
                    q = T * b + c
                    pe.wait_ge(S("y_ready"), q + 1)
                    wait(pe, S("yt_ready"), q)
                    for g in range(2):
                        mm = pe.transpose(b_yt[:, g * P:(g + 1) * P], Y[k][:, g * P:(g + 1) * P], m.IDENT[:, :])
                    mm.then_inc(S("y_turned"), 1)
                    pe.wait_ge(S("yt_ready"), q + 1)
                    wait(pe, S("x2"), q)
                    pe.wait_ge(S("cb_masked"), min(q + 3, Q) if isinstance(q, int) else q + 3)
                    for g in range(2):
                        mm = pe.matmul(b_o[:, 0:P], YT[k][:, g, :], m.WF[:, g, :], start=(g == 0), stop=(g == 1))
                    mm.then_inc(S("out_product"), 1)

                for k in range(5):
                    project(0, 0, k)
                scores(0, 0, 0)

                def body(b, u, first, last):
                    for c in range(T):
                        if c < T - 1:
                            if not last:
                                project(b + 1, 1 - u, c)
                            scores(b, u, c + 1)
                        elif not last:
                            project(b + 1, 1 - u, 3)
                            project(b + 1, 1 - u, 4)
                            scores(b + 1, 1 - u, 0)
                        outputs(b, u, c)
                        if c:
                            finish(b, u, c - 1)
                        elif not first:
                            finish(b - 1, 1 - u, T - 1)

                over_batches(pe, body)
                finish(B - 1, 1, T - 1)

            @block.scalar
            def _(act):
                def tap(b, u, g):
                    act.wait_ge(S("xbc_product"), 3 * b + g + 1)
                    wait(act, S("xbc_ready"), 3 * (b - 1))
                    act.activation(CV[u][:, g, :], b_pj[slot(u, g)][:, :], ACT.Identity, bias=m.CB[:, g:g + 1],
                                   scale=m.CW[:, g, 3:4]).then_inc(S("tap_ready"), 1)

                def gate(b, u, k):
                    act.wait_ge(S("z_product"), 2 * b + k + 1)
                    wait(act, S("y_ready"), T * (b - 1))
                    act.activation(ZS[u][:, 2 * k:2 * k + 2, :], b_pj[slot(u, 3 + k)][:, :].rearrange("p (t n) -> p t n", t=2),
                                   ACT.Silu).then_inc(S("z_ready"), 1)

                def silu(b, u, g):
                    act.wait_ge(S("conv_ready"), 3 * b + g + 1)
                    wait(act, S("outputs"), T * (b - 1))
                    act.activation(XC[u][:, g, :], CV[u][:, g, :], ACT.Silu).then_inc(S("xbc_ready"), 1)

                def scores(b, u, c):
                    k = c % 2
                    q = T * b + c
                    act.wait_ge(S("x_turned"), q + 1)
                    wait(act, S("x_scaled"), 3 * (q - 1))
                    wait(act, S("outputs"), q - 1)
                    wait(act, S("state_products"), 3 * b + (c - 1 if c else 0))
                    act.activation(XH[k][:, :], b_x[:, 0:320], ACT.Copy).then_inc(S("xh_ready"), 1)
                    act.wait_ge(S("seg_sums"), q + 1)
                    act.activation(ES[k][:, :, :], b_seg[:, :].rearrange("p (h l) -> p h l", h=HEADS), ACT.Exp)\
                       .then_inc(S("seg_exp"), 1)

                def finish(b, u, c):
                    k = c % 2
                    q = T * b + c
                    act.wait_ge(S("y_ready"), q + 1)
                    wait(act, S("rms_ready"), q - 1)
                    wait(act, S("squared"), q)
                    act.activation(SQ[:, :], Y[k][:, :], ACT.Square, accum_out=RS[k][:, 0:1]).then_inc(S("squared"), 1)
                    act.wait_ge(S("y_turned"), q + 1)
                    wait(act, S("out_product"), q - 1)
                    act.activation(YT[k][:, :, :], b_yt[:, 0:256].rearrange("p (g l) -> p g l", g=2), ACT.Copy)\
                       .then_inc(S("yt_ready"), 1)

                for g in range(3):
                    tap(0, 0, g)
                for k in range(2):
                    gate(0, 0, k)
                for g in range(3):
                    silu(0, 0, g)
                scores(0, 0, 0)

                def body(b, u, first, last):
                    for c in range(T):
                        if c < T - 1:
                            if not last:
                                tap(b + 1, 1 - u, c)
                            scores(b, u, c + 1)
                        elif not last:
                            for g in range(3):
                                silu(b + 1, 1 - u, g)
                            for k in range(2):
                                gate(b + 1, 1 - u, k)
                            scores(b + 1, 1 - u, 0)
                        if c:
                            finish(b, u, c - 1)
                        elif not first:
                            finish(b - 1, 1 - u, T - 1)

                over_batches(act, body)
                finish(B - 1, 1, T - 1)

            @block.gpsimd
            def _(pool):
                def rhs(b, u, c):
                    k = c % 2
                    wait_apart(pool, S("seg_sums"), T * b + c - 1, m.waited)
                    pool.tensor_tensor(SR[k][:, :, :], m.LE[:, :].unsqueeze(1).broadcast_to([P, HEADS, P]),
                                       over_heads(m.DA, b, c, P), ALU.mult).then_inc(S("seg_rhs"), 1)

                def scale(b, u, c):
                    k = c % 2
                    q = T * b + c
                    wait(pool, S("outputs"), q - 1)
                    wait(pool, S("state_products"), 3 * b + (c - 1 if c else 0))
                    wait(pool, S("y_ready"), q - 1)
                    wait_apart(pool, S("xh_ready"), q + 1, m.waited)
                    xh = heads(XH[k][:, 0:INNER])
                    pool.tensor_tensor(heads(XDT[k][:, :]), xh, over_heads(m.DTS, b, c), ALU.mult).then_inc(S("x_scaled"), 1)
                    pool.tensor_tensor(heads(XW[k][:, :]), xh, over_heads(m.DD, b, c), ALU.mult).then_inc(S("x_scaled"), 1)
                    pool.tensor_tensor(heads(XD[k][:, :]), xh, m.DH[:, :].unsqueeze(2).broadcast_to([P, HEADS, HD]),
                                       ALU.mult).then_inc(S("x_scaled"), 1)

                def rms(b, u, c):
                    k = c % 2
                    q = T * b + c
                    pool.wait_ge(S("squared"), q + 1)
                    wait_apart(pool, S("x2"), q - 1, m.waited)
                    pool.tensor_scalar(RS[k][:, 1:2], RS[k][:, 0:1], 1.0 / INNER, LN_EPS, ALU.mult, ALU.add)\
                        .then_inc(S("mean_square"), 1)
                    pool.wait_ge(S("mean_square"), q + 1)
                    pool.tensor_tensor(RS[k][:, 1:2], RS[k][:, 1:2], m.MHALF[:, 0:1], ALU.pow).then_inc(S("rms_ready"), 1)

                rhs(0, 0, 0)

                def body(b, u, first, last):
                    for c in range(T):
                        if c < T - 1:
                            rhs(b, u, c + 1)
                        elif not last:
                            rhs(b + 1, 1 - u, 0)
                        scale(b, u, c)
                        if c:
                            rms(b, u, c - 1)
                        elif not first:
                            rms(b - 1, 1 - u, T - 1)

                over_batches(pool, body)
                rms(B - 1, 1, T - 1)

            @block.vector
            def _(dve):
                def conv(b, u, g):
                    for back in range(1, TAPS):
                        if back == 1:
                            dve.wait_ge(S("tap_ready"), 3 * b + g + 1)
                        else:
                            dve.wait_ge(S("taps"), (3 * b + g) * 2 + back - 1)
                        dst = CV[u][:, g, back:N]
                        op = dve.scalar_tensor_tensor(out=dst, in0=b_pj[slot(u, g)][:, 0:N - back],
                                                      scalar=m.CW[:, g, 3 - back:4 - back], in1=dst,
                                                      op0=ALU.mult, op1=ALU.add)
                        op.then_inc(S("taps") if back < TAPS - 1 else S("conv_ready"), 1)

                def scores(b, u, c):
                    k = c % 2
                    q = T * b + c
                    dve.wait_ge(S("cb_product"), q + 1)
                    dve.tensor_tensor(CM[k][:, :], b_o[:, 256:384], m.LE[:, :], ALU.mult).then_inc(S("cb_masked"), 1)
                    dve.wait_ge(S("cb_masked"), q + 1)
                    dve.wait_ge(S("seg_exp"), q + 1)
                    dve.tensor_tensor(ES[k][:, :, :], ES[k][:, :, :], CM[k][:, :].unsqueeze(1).broadcast_to([P, HEADS, P]),
                                      ALU.mult).then_inc(S("m_ready"), 1)

                def states(b, u, c):
                    q = T * b + c
                    if c == T - 1:
                        dve.sem_inc(S("states_done"), 1)
                        return
                    dve.wait_ge(S("state_products"), 3 * b + c + 1)
                    new = SS[c][:, :]
                    if c == 0:
                        wait(dve, S("y_summed"), q - 2)
                        dve.tensor_copy(new, b_cs[0:STATE, 256:512]).then_inc(S("states_done"), 1)
                        return
                    dve.wait_ge(S("states_done"), q)
                    wait_apart(dve, S("states_done"), q, m.waited)
                    dve.tensor_tensor(heads(new), heads(SS[c - 1][:, :]), over_heads(m.CD, b, c, parts=STATE), ALU.mult)\
                       .then_inc(S("decayed"), 1)
                    dve.wait_ge(S("decayed"), 2 * b + c)
                    dve.tensor_tensor(new, new, b_cs[0:STATE, 256:512], ALU.add).then_inc(S("states_done"), 1)

                def combine(b, u, c):
                    k = c % 2
                    q = T * b + c
                    y = Y[k][:, :]
                    dve.wait_ge(S("outputs"), q + 1)
                    dve.wait_ge(S("x_scaled"), 3 * q + 3)
                    wait(dve, S("squared"), q - 1)
                    wait(dve, S("y_turned"), q - 1)
                    if c:
                        wait_apart(dve, S("x_scaled"), 3 * q + 3, m.waited)
                        dve.tensor_tensor(heads(y), heads(b_y[:, INNER:2 * INNER]), over_heads(m.EA, b, c), ALU.mult)\
                           .then_inc(S("y_off"), 1)
                        dve.wait_ge(S("y_off"), 3 * b + c)
                        dve.tensor_tensor(XD[k][:, :], y, XD[k][:, :], ALU.add).then_inc(S("y_off_d"), 1)
                        dve.wait_ge(S("y_off_d"), 3 * b + c)
                    dve.tensor_tensor(y, b_y[:, 0:INNER], XD[k][:, :], ALU.add).then_inc(S("y_summed"), 1)
                    dve.wait_ge(S("y_summed"), q + 1)
                    if c % 2 == 0:
                        dve.wait_ge(S("z_ready"), 2 * b + c // 2 + 1)
                    dve.tensor_tensor(y, y, ZS[u][:, c, :], ALU.mult).then_inc(S("y_ready"), 1)

                def finish(b, u, c):
                    k = c % 2
                    q = T * b + c
                    dve.wait_ge(S("out_product"), q + 1)
                    dve.wait_ge(S("rms_ready"), q + 1)
                    xq = m.X[:, bass.ds(q * P, P)]
                    dve.scalar_tensor_tensor(out=xq, in0=b_o[:, 0:P], scalar=RS[k][:, 1:2], in1=xq, op0=ALU.mult,
                                             op1=ALU.add).then_inc(S("x2"), 1)
                    wait_apart(dve, S("x2"), q + 1, m.waited)
                    wait_apart(dve, S("stats_kept"), b, m.waited) if c == 0 else None
                    dve.bn_stats(ST[:, c, :], xq).then_inc(S("stats2"), 1)
                    wait_apart(dve, S("stats2"), q + 1, m.waited)
                    dve.bn_aggr(MVS[:, c, :], ST[:, c, :]).then_inc(S("stats2_known"), 1)
                    if c == T - 1:
                        dve.wait_ge(S("stats2_known"), q + 1)
                        dve.tensor_scalar(m.MV[:, bass.ds(b * T, T), :], MVS[:, :, :], 1.0, None, ALU.mult)\
                           .then_inc(S("stats_kept"), 1)

                for g in range(3):
                    conv(0, 0, g)
                scores(0, 0, 0)

                def body(b, u, first, last):
                    for c in range(T):
                        if c < T - 1:
                            if not last:
                                conv(b + 1, 1 - u, c)
                            scores(b, u, c + 1)
                        elif not last:
                            scores(b + 1, 1 - u, 0)
                        states(b, u, c)
                        combine(b, u, c)
                        if c:
                            finish(b, u, c - 1)
                        elif not first:
                            finish(b - 1, 1 - u, T - 1)

                over_batches(dve, body)
                finish(B - 1, 1, T - 1)
        retire(nc, mem)




def ode(nc, m):
    with ExitStack() as stack:
        mem = Memory(nc, stack)
        S = mem.sem

        def halves(name, *shape):
            return Halves(mem, name, *shape)

        L_POWERS = (m.LT, m.L2T, m.L3T, m.L6T)
        LP = [halves(f"ode_l_power{k}", P, T, N) for k in range(4)]
        ES = halves("ode_e", P, 9, 128)
        E4 = [e.rearrange("p (q k) e -> p q k e", k=3) for e in ES.at(slice(None), slice(None))]
        HTS = mem.sb("ode_h8_turned", P, N)
        H = [mem.sb(f"ode_h{u}", P, T, P) for u in range(2)]
        HS = [halves(f"ode_h{u}", P, T, P) for u in range(2)]
        ZS = halves("ode_z", P, 3, N)
        GS = halves("ode_g", P, T, 2 * P)
        ST = mem.sb("ode_stats", P, T, 6)
        MVS = mem.sb("ode_mean_var", P, T, 2)
        b_x, = mem.banks("ode_b_x", 1)
        b_z = mem.banks("ode_b_z", 2)
        b_g = mem.banks("ode_b_g", 2)
        b_ht, = mem.banks("ode_b_h8_turned", 1)
        b_h = mem.banks("ode_b_h8", 2)

        with nc.Block() as block:

            @block.gpsimd
            def _(pool):
                pool.tensor_scalar(m.RSTD[:, :], m.MV[:, :, 1], LN_EPS, None, ALU.add).then_inc(S("ln_var"), 1)
                pool.wait_ge(S("ln_var"), 1)
                pool.tensor_tensor(m.RSTD[:, :], m.RSTD[:, :], m.MHALF[:, :], ALU.pow).then_inc(S("rstd_ready"), 1)

                def body(b, u, first, last):
                    pool.wait_ge(S("h_high"), b + 1)
                    wait(pool, S("z_product"), 3 * (b - 1))
                    pool.tensor_tensor(HS[u].low[:, :, :], H[u][:, :, :], HS[u].seen[:, :, :], ALU.subtract)\
                        .then_inc(S("h_low"), 1)
                    wait_apart(pool, S("h_ready"), b * T + T, m.waited)
                    xb = m.X[:, bass.ds(b * N, N)]
                    pool.tensor_tensor(xb, xb, m.GB[:, :], ALU.add).then_inc(S("const_added"), 1)

                over_batches(pool, body)

            @block.vector
            def _(dve):
                def norm(b, u):
                    wait(dve, S("z_product"), 3 * (b - 1))
                    wait(dve, S("h_high"), b - 1)
                    wait(dve, S("h_low"), b - 1)
                    for t in range(T):
                        q = b * T + t
                        dve.tensor_scalar(H[u][:, t, :], m.X[:, bass.ds(q * P, P)], m.MV[:, bass.ds(q, 1), 0],
                                          m.RSTD[:, bass.ds(q, 1)], ALU.subtract, ALU.mult).then_inc(S("h_ready"), 1)

                def z_low(b, u):
                    wait(dve, S("h_begun"), b)
                    for k, bank in enumerate((b_x, *b_z)):
                        dve.wait_ge(S("z_high"), 3 * b + k + 1)
                        dve.tensor_tensor(ZS.low[:, k, :], bank[:, :], ZS.seen[:, k, :], ALU.subtract)\
                           .then_inc(S("z_low"), 1)

                def g_low(b, u):
                    wait(dve, S("h8"), b)
                    for k in range(2):
                        dve.wait_ge(S("g_high"), 2 * b + k + 1)
                        dve.tensor_tensor(GS.low[:, 2 * k:2 * k + 2, :], tiles(b_g[k][:, :], 2),
                                          GS.seen[:, 2 * k:2 * k + 2, :], ALU.subtract).then_inc(S("g_low"), 1)

                def update(b, u):
                    xb = m.X[:, bass.ds(b * N, N)]
                    dve.wait_ge(S("h8_turned"), b + 1)
                    dve.wait_ge(S("const_added"), b + 1)
                    dve.tensor_tensor(xb, b_h[u][:, :], xb, ALU.add).then_inc(S("x3"), 1)
                    wait_apart(dve, S("x3"), b + 1, m.waited)
                    wait_apart(dve, S("stats_kept"), b, m.waited)
                    for t in range(T):
                        dve.bn_stats(ST[:, t, :], m.X[:, bass.ds((b * T + t) * P, P)]).then_inc(S("stats3"), 1)
                    wait_apart(dve, S("stats3"), b * T + T, m.waited)
                    for t in range(T):
                        dve.bn_aggr(MVS[:, t, :], ST[:, t, :]).then_inc(S("stats3_known"), 1)
                    dve.wait_ge(S("stats3_known"), b * T + T)
                    dve.tensor_scalar(m.MV[:, bass.ds(b * T, T), :], MVS[:, :, :], 1.0, None, ALU.mult)\
                       .then_inc(S("stats_kept"), 1)

                for k in range(4):
                    for t in range(T):
                        dve.wait_ge(S("const_high"), T * k + t + 1)
                        dve.tensor_tensor(LP[k].low[:, t, :], L_POWERS[k][:, t, :], LP[k].seen[:, t, :], ALU.subtract)\
                           .then_inc(S("const_low"), 1)
                dve.wait_ge(S("const_high"), 4 * T + 1)
                dve.tensor_tensor(ES.low[:, :, :], m.E[:, :, :], ES.seen[:, :, :], ALU.subtract).then_inc(S("const_low"), 1)
                dve.wait_ge(S("rstd_ready"), 1)
                norm(0, 0)
                norm(1, 1)
                z_low(0, 0)
                g_low(0, 0)

                def body(b, u, first, one_ahead, two_ahead):
                    if not first:
                        update(b - 1, 1 - u)
                    if two_ahead:
                        norm(b + 2, u)
                    if one_ahead:
                        z_low(b + 1, 1 - u)
                        g_low(b + 1, 1 - u)

                turns(dve, body)
                update(B - 1, 1)

            @block.scalar
            def _(act):
                def h_high(b, u):
                    act.wait_ge(S("h_ready"), b * T + T)
                    wait(act, S("z_product"), 3 * (b - 1))
                    act.activation(HS[u].high[:, :, :], H[u][:, :, :], ACT.Copy).then_inc(S("h_high"), 1)

                def z_high(b, u):
                    wait(act, S("h_begun"), b)
                    for k, bank in enumerate((b_x, *b_z)):
                        act.wait_ge(S("z_product"), 3 * b + k + 1)
                        act.activation(ZS.high[:, k, :], bank[:, :], ACT.Copy).then_inc(S("z_high"), 1)

                def g_high(b, u):
                    wait(act, S("h8"), b)
                    for k in range(2):
                        act.wait_ge(S("g_product"), 2 * b + k + 1)
                        act.activation(GS.high[:, 2 * k:2 * k + 2, :], tiles(b_g[k][:, :], 2), ACT.Copy)                           .then_inc(S("g_high"), 1)

                def keep_h8(b):
                    act.wait_ge(S("h8"), b + 1)
                    wait(act, S("h8_turned"), b)
                    act.activation(HTS[:, :], b_ht[:, :], ACT.Copy).then_inc(S("h8_kept"), 1)

                for k in range(4):
                    for t in range(T):
                        act.activation(LP[k].high[:, t, :], L_POWERS[k][:, t, :], ACT.Copy).then_inc(S("const_high"), 1)
                act.activation(ES.high[:, :, :], m.E[:, :, :], ACT.Copy).then_inc(S("const_high"), 1)
                h_high(0, 0)
                h_high(1, 1)
                z_high(0, 0)
                g_high(0, 0)

                def body(b, u, first, one_ahead, two_ahead):
                    if one_ahead:
                        z_high(b + 1, 1 - u)
                    if two_ahead:
                        h_high(b + 2, u)
                    keep_h8(b)
                    if one_ahead:
                        g_high(b + 1, 1 - u)

                turns(act, body)

            @block.tensor
            def _(pe):
                def z(b, u):
                    pe.wait_ge(S("h_ready"), b * T + T)
                    wait(pe, S("z_low"), 3 * b - 2)
                    for t in range(T):
                        mm = pe.transpose(b_x[:, t * P:(t + 1) * P], H[u][:, t, :], m.IDENT[:, :])
                    mm.then_inc(S("z_product"), 1)
                    pe.wait_ge(S("h_high"), b + 1)
                    pe.wait_ge(S("h_low"), b + 1)
                    for k in range(2):
                        wait(pe, S("z_low"), 3 * b - 1 + k)
                        for s in range(T):
                            mm = in_halves(pe, b_z[k][:, :], HS[u].at(s, slice(None)), LP[k].at(s, slice(None)), s == 0, s == T - 1)
                        mm.then_inc(S("z_product"), 1)

                def g(b, u):
                    pe.wait_ge(S("z_low"), 3 * b + 3)
                    for t in range(T):
                        if t % 2 == 0:
                            wait(pe, S("g_low"), 2 * b - 1 + t // 2)
                        at = slice(t * P, (t + 1) * P)
                        for k in range(3):
                            mm = in_halves(pe, b_g[t // 2][:, 256 * (t % 2):256 * (t % 2) + 256], ZS.at(k, at),
                                           [e[:, 1:3, k, :] for e in E4], t % 2 == 0 and k == 0, t % 2 == 1 and k == 2)
                        if t % 2:
                            mm.then_inc(S("g_product"), 1)

                def h_from_z(b):
                    wait(pe, S("h8_kept"), b)
                    for k in range(3):
                        mm = in_halves(pe, b_ht[:, :], ES.at(k, slice(None)), ZS.at(k, slice(None)), k == 0, False)
                    mm.then_inc(S("h_begun"), 1)

                def h_from_g(b, q):
                    if q == 1:
                        pe.wait_ge(S("g_low"), 2 * b + 2)
                    for s in range(T):
                        mm = in_halves(pe, b_ht[:, :], GS.at(s, slice((q - 1) * P, q * P)), LP[1 + q].at(s, slice(None)),
                                       False, q == 2 and s == T - 1)
                    if q == 2:
                        mm.then_inc(S("h8"), 1)

                def turn_back(b, u):
                    pe.wait_ge(S("h8_kept"), b + 1)
                    wait(pe, S("x3"), b - 1)
                    for t in range(T):
                        mm = pe.transpose(b_h[u][:, t * P:(t + 1) * P], HTS[:, t * P:(t + 1) * P], m.IDENT[:, :])
                    mm.then_inc(S("h8_turned"), 1)

                pe.wait_ge(S("const_low"), 4 * T + 1)
                z(0, 0)
                g(0, 0)

                def body(b, u, first, last):
                    h_from_z(b)
                    h_from_g(b, 1)
                    if not last:
                        z(b + 1, 1 - u)
                    h_from_g(b, 2)
                    if not last:
                        g(b + 1, 1 - u)
                    turn_back(b, u)

                over_batches(pe, body)
        retire(nc, mem)




def router(nc, m, mem, H, HTS):
    S = mem.sem
    FE = mem.sb("feat_sum", P, T, P)
    FT = mem.sb("feat_t", P, N)
    LG = mem.sb("logits", P, T, EXPERTS)
    CO = mem.sb("router_cols", P, 2, T)
    W8 = mem.sb("router_rows", EXPERTS, N)
    b_f = mem.banks("rt_b", 6)
    per_expert = [P, T, EXPERTS]

    def pool(e, b, u, first, last):
        e.wait_ge(S("h_ready"), b * T + T)
        if first:
            e.tensor_copy(FE[:, :, :], H[u][:, :, :]).then_inc(S("feat_added"), 1)
        else:
            e.wait_ge(S("feat_added"), b)
            e.tensor_tensor(FE[:, :, :], FE[:, :, :], H[u][:, :, :], ALU.add).then_inc(S("feat_added"), 1)

    def pe_start(pe):
        for k in range(4):
            for e in range(4):
                mm = pe.matmul(b_f[2 + k][:, e * P:(e + 1) * P], m.BNA[:, 4 * k + e:4 * k + e + 1].broadcast_to([P, P]),
                               m.IDENT[:, :], start=True, stop=True)
            mm.then_inc(S("scales_wide"), 1)

    def pe_end(pe):
        pe.wait_ge(S("feat_added"), B)
        for t in range(T):
            mm = pe.transpose(b_f[0][:, t * P:(t + 1) * P], FE[:, t, :], m.IDENT[:, :])
        mm.then_inc(S("feat_turned"), 1)
        pe.wait_ge(S("feat_ready"), 1)
        for t in range(T):
            mm = pe.matmul(b_f[1][:, EXPERTS * t:EXPERTS * (t + 1)], FT[:, t * P:(t + 1) * P], m.WR[:, :],
                           start=True, stop=True)
        mm.then_inc(S("logits"), 1)
        pe.wait_ge(S("router_ready"), 1)
        for t in range(T):
            mm = pe.transpose(b_f[0][0:EXPERTS, t * P:(t + 1) * P], LG[:, t, :], m.IDENT[:, :])
        mm.then_inc(S("router_turned"), 1)
        pe.wait_ge(S("scaled"), 4)
        for e in range(EXPERTS):
            k = e % 4
            wait(pe, S("wide_copied"), e - 3)
            for t in range(T):
                mm = pe.matmul(b_f[2 + k][:, t * P:(t + 1) * P], LG[:, t, e:e + 1].broadcast_to([P, P]), m.IDENT[:, :],
                               start=True, stop=True)
            mm.then_inc(S("wide"), 1)
        pe.wait_ge(S("router_rows"), 1)
        for t in range(T):
            mm = pe.matmul(b_f[1][:, t * P:(t + 1) * P], W8[:, t * P:(t + 1) * P], m.BO[:, :], start=True, stop=True)
        mm.then_inc(S("out_bias"), 1)

    def act_end(act):
        act.wait_ge(S("scaled"), 4)
        for k, w in enumerate((m.W1, m.W2, m.W3)):
            act.activation(m.WS[k].high[:, :, :], w[:, :, :], ACT.Copy).then_inc(S("weights_high"), 1)
        act.wait_ge(S("feat_turned"), 1)
        act.activation(FT[:, :], b_f[0][:, :], ACT.Copy, scale=1.0 / B).then_inc(S("feat_ready"), 1)
        act.wait_ge(S("logits_shifted"), 1)
        act.activation(LG[:, :, :], LG[:, :, :], ACT.Exp).then_inc(S("router_exp"), 1)
        for e in range(EXPERTS):
            act.wait_ge(S("wide"), e + 1)
            act.activation(m.RW[:, e, :], b_f[2 + e % 4][:, :], ACT.Copy).then_inc(S("wide_copied"), 1)

    def dve_start(dve):
        for k in range(4):
            w = (m.W1, m.W2)[k // 2][:, 4 * (k % 2):4 * (k % 2) + 4, :]
            dve.wait_ge(S("scales_wide"), k + 1)
            dve.tensor_tensor(w, w, tiles(b_f[2 + k][:, :]), ALU.mult).then_inc(S("scaled"), 1)

    def dve_end(e):
        for k, w in enumerate((m.W1, m.W2, m.W3)):
            e.wait_ge(S("weights_high"), k + 1)
            e.tensor_tensor(m.WS[k].low[:, :, :], w[:, :, :], m.WS[k].seen[:, :, :], ALU.subtract)
        e.wait_ge(S("logits"), 1)
        e.tensor_tensor(LG[:, :, :], b_f[1][:, 0:T * EXPERTS].rearrange("p (t e) -> p t e", t=T),
                        m.BR[:, :].unsqueeze(1).broadcast_to(per_expert), ALU.add).then_inc(S("softmax"), 1)
        e.wait_ge(S("softmax"), 1)
        e.tensor_reduce(CO[:, 0, :], LG[:, :, :], mybir.AxisListType.X, ALU.max).then_inc(S("softmax"), 1)
        e.wait_ge(S("softmax"), 2)
        e.tensor_tensor(LG[:, :, :], LG[:, :, :], CO[:, 0, :].unsqueeze(2).broadcast_to(per_expert), ALU.subtract)\
         .then_inc(S("logits_shifted"), 1)
        e.wait_ge(S("router_exp"), 1)
        e.tensor_reduce(CO[:, 0, :], LG[:, :, :], mybir.AxisListType.X, ALU.add).then_inc(S("softmax"), 1)
        e.wait_ge(S("softmax"), 3)
        e.reciprocal(CO[:, 1, :], CO[:, 0, :]).then_inc(S("softmax"), 1)
        e.wait_ge(S("softmax"), 4)
        e.tensor_tensor(LG[:, :, :], LG[:, :, :], CO[:, 1, :].unsqueeze(2).broadcast_to(per_expert), ALU.mult)\
         .then_inc(S("router_ready"), 1)
        e.wait_ge(S("router_turned"), 1)
        e.tensor_copy(W8[:, :], b_f[0][0:EXPERTS, :]).then_inc(S("router_rows"), 1)
        e.wait_ge(S("out_bias"), 1)
        e.tensor_copy(m.YB[:, :], b_f[1][:, :])

    return Extra(pe_end, act_end, dve_end, pool, wait_h_free=lambda dve, b: wait(dve, S("feat_added"), b - 1),
                 dve_start=dve_start, pe_start=pe_start)


def experts(nc, m, out):
    with ExitStack() as stack:
        mem = Memory(nc, stack)
        m.RW = mem.sb("router_wide", P, EXPERTS, N)
        m.YB = mem.sb("expert_bias", P, N)
        WS = m.WS = [Halves(mem, f"ex_w{k}", P, EXPERTS, P) for k in range(3)]
        normalise(nc, m, "moe", router)
        S = mem.sem
        HB = [mem.sb(f"ex_ht{u}", P, N) for u in range(2)]
        HS = [Halves(mem, f"ex_ht{u}", P, N) for u in range(2)]
        R1 = [mem.sb(f"ex_r1_{k}", P, N) for k in range(4)]
        H1 = [Halves(mem, f"ex_h1_{k}", P, N) for k in range(4)]
        R2 = [mem.sb(f"ex_r2_{k}", P, N) for k in range(2)]
        HW = [mem.sb(f"ex_hw_{k}", P, N) for k in range(2)]
        HWS = [Halves(mem, f"ex_hw_{k}", P, N) for k in range(4)]
        YT = mem.sb("ex_y_turned", P, N)
        O = [mem.sb(f"ex_out{u}", P, N) for u in range(2)]
        b_1 = mem.banks("ex_b_1", 2)
        b_2 = mem.banks("ex_b_2", 2)
        b_yt = mem.banks("ex_b_y_turned", 2)
        b_y = mem.banks("ex_b_y", 2)
        E = EXPERTS
        every = slice(None)

        def ahead(b, u, e):
            return (b, u, e + 2) if e < E - 2 else (b + 1, 1 - u, e + 2 - E)

        def behind(b, u, e):
            return (b, u, e - 2) if e >= 2 else (b - 1, 1 - u, e - 2 + E)

        with nc.Block() as block:

            @block.sync
            def _(sp):
                def load(b, u):
                    wait_apart(sp, S("ht_high"), b - 1, m.waited)
                    wait_apart(sp, S("ht_low"), b - 1, m.waited)
                    sp.dma_start(HB[u][:, :], m.HT[:, bass.ds(b * N, N)]).then_inc(S(f"ht_loaded{u}"), 16)

                def body(b, u, first, one_ahead, two_ahead):
                    if two_ahead:
                        load(b + 2, u)
                    wait_apart(sp, S("x4"), b + 1, m.waited)
                    sp.dma_start(out[bass.ds(b, 1)].rearrange("o (t p) d -> p (o t) d", p=P), tiles(O[u][:, :]))\
                      .then_inc(S(f"stored{u}"), 16)

                load(0, 0)
                load(1, 1)
                turns(sp, body)
                for u in range(2):
                    sp.wait_ge(S(f"stored{u}"), 16 * B // 2)
                    sp.wait_ge(S(f"ht_loaded{u}"), 16 * B // 2)

            @block.gpsimd
            def _(pool):
                def ht_low(b, u):
                    pool.wait_ge(S("ht_high"), b + 1)
                    wait(pool, S("product1"), E * (b - 1))
                    pool.tensor_tensor(HS[u].low[:, :], HB[u][:, :], HS[u].seen[:, :], ALU.subtract)\
                        .then_inc(S("ht_low"), 1)

                def weigh(b, u, e):
                    pool.wait_ge(S("relu2"), E * b + e + 1)
                    wait(pool, S("hw_low"), E * b + e - 1)
                    pool.tensor_tensor(HW[e % 2][:, :], R2[e % 2][:, :], m.RW[:, e, :], ALU.mult).then_inc(S("hw_full"), 1)

                ht_low(0, 0)

                def body(b, u, first, last):
                    for e in range(E):
                        if e == 1:
                            xb = m.X[:, bass.ds(b * N, N)]
                            pool.tensor_tensor(xb, xb, m.YB[:, :], ALU.add).then_inc(S("bias_added"), 1)
                        if e == 4 and not last:
                            ht_low(b + 1, 1 - u)
                        weigh(b, u, e)

                over_batches(pool, body)

            @block.tensor
            def _(pe):
                def layer1(b, u, e):
                    if e == 0:
                        pe.wait_ge(S("ht_high"), b + 1)
                        pe.wait_ge(S("ht_low"), b + 1)
                    wait(pe, S("relu1"), E * b + e - 1)
                    in_halves(pe, b_1[e % 2][:, :], WS[0].at(e, every), HS[u].at(every), True, True)\
                        .then_inc(S("product1"), 1)

                def layer2(b, u, e):
                    pe.wait_ge(S("h1_high"), E * b + e + 1)
                    pe.wait_ge(S("h1_low"), E * b + e + 1)
                    wait(pe, S("relu2"), E * b + e - 1)
                    in_halves(pe, b_2[e % 2][:, :], WS[1].at(e, every), H1[e % 4].at(every), True, True)\
                        .then_inc(S("product2"), 1)

                def layer3(b, u, e):
                    pe.wait_ge(S("hw_low"), E * b + e + 1)
                    if e == 0:
                        wait(pe, S("y_kept"), b - 1)
                    in_halves(pe, b_yt[u][:, :], WS[2].at(e, every), HWS[e % 4].at(every), e == 0, e == E - 1)\
                        .then_inc(S("product3"), 1)

                def turn_back(b, u):
                    pe.wait_ge(S("y_kept"), b + 1)
                    wait(pe, S("x4"), b - 1)
                    for t in range(T):
                        mm = pe.transpose(b_y[u][:, t * P:(t + 1) * P], YT[:, t * P:(t + 1) * P], m.IDENT[:, :])
                    mm.then_inc(S("y_turned"), 1)

                layer1(0, 0, 0)
                layer1(0, 0, 1)

                def body(b, u, first, last):
                    for e in range(E):
                        if not (last and e >= E - 2):
                            layer1(*ahead(b, u, e))
                        layer2(b, u, e)
                        if not (first and e < 2):
                            layer3(*behind(b, u, e))
                        if e == 3 and not first:
                            turn_back(b - 1, 1 - u)

                over_batches(pe, body)
                layer3(B - 1, 1, E - 2)
                layer3(B - 1, 1, E - 1)
                turn_back(B - 1, 1)

            @block.scalar
            def _(act):
                def ht_high(b, u):
                    act.wait_ge(S(f"ht_loaded{u}"), (b - u) * 8 + 16)
                    wait(act, S("product1"), E * (b - 1))
                    act.activation(HS[u].high[:, :], HB[u][:, :], ACT.Copy).then_inc(S("ht_high"), 1)

                def relu1(b, u, e):
                    act.wait_ge(S("product1"), E * b + e + 1)
                    wait(act, S("product2"), E * b + e - 3)
                    act.activation(R1[e % 4][:, :], b_1[e % 2][:, :], ACT.Relu, bias=m.BNC[:, e:e + 1])\
                       .then_inc(S("relu1"), 1)

                def h1_high(b, u, e):
                    act.wait_ge(S("relu1"), E * b + e + 1)
                    act.activation(H1[e % 4].high[:, :], R1[e % 4][:, :], ACT.Copy).then_inc(S("h1_high"), 1)

                def relu2(b, u, e):
                    act.wait_ge(S("product2"), E * b + e + 1)
                    wait(act, S("hw_high"), E * b + e - 1)
                    wait(act, S("hw_full"), E * b + e - 1)
                    act.activation(R2[e % 2][:, :], b_2[e % 2][:, :], ACT.Relu, bias=m.BNC[:, E + e:E + e + 1])\
                       .then_inc(S("relu2"), 1)

                def keep_y(b, u):
                    act.wait_ge(S("product3"), E * b + E)
                    wait(act, S("y_turned"), b)
                    act.activation(YT[:, :], b_yt[u][:, :], ACT.Copy).then_inc(S("y_kept"), 1)

                ht_high(0, 0)
                for e in range(2):
                    relu1(0, 0, e)
                    h1_high(0, 0, e)

                def body(b, u, first, last):
                    for e in range(E):
                        if not (last and e >= E - 2):
                            relu1(*ahead(b, u, e))
                        relu2(b, u, e)
                        if not (last and e >= E - 2):
                            h1_high(*ahead(b, u, e))
                        if e == 2 and not first:
                            keep_y(b - 1, 1 - u)
                        if e == 3 and not last:
                            ht_high(b + 1, 1 - u)

                over_batches(act, body)
                keep_y(B - 1, 1)

            @block.vector
            def _(dve):
                def h1_low(b, u, e):
                    dve.wait_ge(S("h1_high"), E * b + e + 1)
                    wait(dve, S("product2"), E * b + e - 3)
                    k = e % 4
                    dve.tensor_tensor(H1[k].low[:, :], R1[k][:, :], H1[k].seen[:, :], ALU.subtract)\
                       .then_inc(S("h1_low"), 1)

                def weigh_high(b, u, e):
                    dve.wait_ge(S("relu2"), E * b + e + 1)
                    wait(dve, S("product3"), E * b + e - 3)
                    dve.tensor_tensor(HWS[e % 4].high[:, :], R2[e % 2][:, :], m.RW[:, e, :], ALU.mult)\
                       .then_inc(S("hw_high"), 1)

                def weigh_low(b, u, e):
                    dve.wait_ge(S("hw_full"), E * b + e + 1)
                    dve.wait_ge(S("hw_high"), E * b + e + 1)
                    dve.tensor_tensor(HWS[e % 4].low[:, :], HW[e % 2][:, :], HWS[e % 4].seen[:, :], ALU.subtract)\
                       .then_inc(S("hw_low"), 1)

                def update(b, u):
                    dve.wait_ge(S("y_turned"), b + 1)
                    dve.wait_ge(S("bias_added"), b + 1)
                    wait(dve, S(f"stored{u}"), (b - u) * 8)
                    dve.tensor_tensor(O[u][:, :], b_y[u][:, :], m.X[:, bass.ds(b * N, N)], ALU.add).then_inc(S("x4"), 1)

                h1_low(0, 0, 0)
                h1_low(0, 0, 1)

                def body(b, u, first, last):
                    for e in range(E):
                        weigh_high(b, u, e)
                        if not (last and e >= E - 2):
                            h1_low(*ahead(b, u, e))
                        weigh_low(b, u, e)
                        if e == 4 and not first:
                            update(b - 1, 1 - u)

                over_batches(dve, body)
                update(B - 1, 1)
        retire(nc, mem)


def build(nc, IN, out):
    with ExitStack() as stack:
        mem = Memory(nc, stack)
        sb = mem.sb
        m = Shared()
        m.waited = mem.sem("waited")
        m.X = sb("X", P, Q * P)
        m.MV = sb("mean_var", P, Q, 2)
        m.RSTD = sb("rstd", P, Q)
        m.IDENT = sb("ident", P, P)
        m.LE = sb("mask_le", P, P)
        m.GT = sb("mask_gt", P, P)
        m.ONES = sb("ones", P, P)
        m.MHALF = sb("minus_half", P, Q)
        m.WIN = sb("mamba_in_w", P, 644)
        m.CW = sb("conv_w", P, 3, 4)
        m.CB = sb("conv_b", P, 3)
        m.DTB = sb("dt_bias", P, 4)
        m.AH = sb("exp_a_log", P, 4)
        m.DH = sb("d_wide", P, 4)
        m.BLIN = sb("b_lin_wide", P, 128)
        m.WF = sb("mamba_w_out_lin", P, 2, 128)
        m.DTS = sb("dt", P, Q, HEADS)
        m.DA = sb("dA", P, Q, HEADS)
        m.EA = sb("decay_in", P, Q, HEADS)
        m.DD = sb("dt_decay_out", P, Q, HEADS)
        m.CD = sb("chunk_decay", P, Q, HEADS)
        m.W1 = sb("w1", P, 8, 128)
        m.W2 = sb("w2", P, 8, 128)
        m.W3 = sb("w3", P, 8, 128)
        m.WR = sb("w_router", P, 8)
        m.BR = sb("b_router", P, 8)
        m.BO = sb("b_out", 8, 128)
        m.BNA = sb("bn_a", P, 16)
        m.BNC = sb("bn_c", P, 16)
        with ExitStack() as to_ode:
            sb = Memory(nc, to_ode).sb
            m.LT = sb("LT", P, T, N)
            m.L2T = sb("L2T", P, T, N)
            m.L3T = sb("L3T", P, T, N)
            m.L6T = sb("L6T", P, T, N)
            m.E = sb("E", P, 9, 128)
            m.GB = sb("ode_const", P, N)
            with ExitStack() as to_attention:
                sb = Memory(nc, to_attention).sb
                m.NEGM = sb("neg_mask", P, T, N)
                m.WEXT = sb("gat_w_ext", P, 130)
                m.WA2B = sb("gat_wa2_wide", P, P)
                with nc.allow_non_contiguous_dma(reason="a few columns of weights"):
                    setup(nc, m, IN)
                attention(nc, m)
            with ExitStack() as in_mamba:
                m.HT = Memory(nc, in_mamba).sb("mamba_HT", P, Q * P)
                mamba_norm(nc, m)
                mamba(nc, m)
            ode(nc, m)
        m.HT = mem.sb("moe_HT", P, Q * P)
        experts(nc, m, out)


_INS = ['x', 'adj', 'L0_gnn_W', 'L0_gnn_a', 'L0_ffn_W_in', 'L0_ffn_conv_w', 'L0_ffn_conv_b', 'L0_ffn_dt_bias',
        'L0_ffn_A_log', 'L0_ffn_D', 'L0_ffn_norm_w', 'L0_ffn_W_out', 'L0_ffn_W_lin', 'L0_ffn_b_lin',
        'L1_gnn_alpha_train', 'L1_gnn_w', 'L1_gnn_d', 'L1_gnn_fc_in_w', 'L1_gnn_fc_in_b', 'L1_ffn_Wr', 'L1_ffn_br',
        'L1_ffn_W1', 'L1_ffn_b1', 'L1_ffn_g1', 'L1_ffn_be1', 'L1_ffn_m1', 'L1_ffn_v1', 'L1_ffn_W2', 'L1_ffn_b2',
        'L1_ffn_g2', 'L1_ffn_be2', 'L1_ffn_m2', 'L1_ffn_v2', 'L1_ffn_Wo', 'L1_ffn_bo']


def kernel(**inputs):
    import numpy as np
    import concourse.bacc as bacc
    from concourse.bass_utils import run_bass_kernel_spmd

    nc = bacc.Bacc("TRN2", target_bir_lowering=False, num_devices=1)
    arrays, IN = {}, {}
    for name in _INS:
        a = np.ascontiguousarray(inputs[name])
        arrays[f"in_{name}"] = a
        IN[name] = nc.dram_tensor(f"in_{name}", a.shape, mybir.dt.from_np(a.dtype), kind="ExternalInput").ap()
    out = nc.dram_tensor("out", (B, N, D), F32, kind="ExternalOutput").ap()
    build(nc, IN, out)
    r = run_bass_kernel_spmd(nc, [arrays], core_ids=[0])
    return r.results[0]["out"]
```

```python
from contextlib import ExitStack
from math import comb

import concourse.bass as bass
from concourse import mybir

F32 = mybir.dt.float32
F32R = mybir.dt.float32r
ALU = mybir.AluOpType
ACT = mybir.ActivationFunctionType

P = 128
B, N, D = 16, 512, 128
T = N // P
Q = B * T
LN_EPS = 1e-5
NEG = -1e30
LEAK = 0.2
HEADS, HD, STATE, INNER, TAPS = 4, 64, 64, 256, 4
STEPS = 8
DT = 1.0 / STEPS
EXPERTS = 8
BN_EPS = 1e-3


def wait(eng, sem, value):
    if isinstance(value, int) and value <= 0:
        return
    eng.wait_ge(sem, value)


def wait_apart(eng, sem, value, seen):
    wait(eng, sem, value)
    eng.sem_inc(seen, 1)


def over_batches(eng, body):
    body(0, 0, True, False)
    body(1, 1, False, False)
    body(2, 0, False, False)
    with eng.Fori(0, B // 2 - 2) as i:
        body(2 * i + 3, 1, False, False)
        body(2 * i + 4, 0, False, False)
    body(B - 1, 1, False, True)


def turns(eng, body):
    body(0, 0, True, True, True)
    body(1, 1, False, True, True)
    body(2, 0, False, True, True)
    with eng.Fori(0, B // 2 - 3) as i:
        body(2 * i + 3, 1, False, True, True)
        body(2 * i + 4, 0, False, True, True)
    body(B - 3, 1, False, True, True)
    body(B - 2, 0, False, True, False)
    body(B - 1, 1, False, False, False)


def two_before(b):
    return not isinstance(b, int) or b >= 2


def nothing(*unused):
    pass


class Shared:
    pass


class Extra:

    def __init__(self, pe_end, act_end, dve_end, pool, wait_h_free=nothing, wait_ht_free=nothing,
                 pe=nothing, dve=nothing, dve_start=nothing, pe_start=nothing):
        self.pe, self.dve, self.pool = pe, dve, pool
        self.pe_end, self.act_end, self.dve_end = pe_end, act_end, dve_end
        self.pe_start, self.dve_start = pe_start, dve_start
        self.wait_h_free, self.wait_ht_free = wait_h_free, wait_ht_free


class Memory:

    def __init__(self, nc, stack):
        self.nc, self.stack = nc, stack
        self.known = {}

    def sb(self, name, *shape, dt=F32):
        return self.stack.enter_context(self.nc.sbuf_tensor(name, list(shape), dt))

    def banks(self, name, count):
        return [self.stack.enter_context(self.nc.psum_tensor(f"{name}{k}", [P, 512], F32)) for k in range(count)]

    def sem(self, name):
        if name not in self.known:
            self.known[name] = self.stack.enter_context(self.nc.semaphore(name))
        return self.known[name]


class Halves:

    def __init__(self, mem, name, *shape):
        self.high = mem.sb(name + "_high", *shape, dt=F32R)
        self.low = mem.sb(name + "_low", *shape, dt=F32R)
        self.seen = self.high[tuple(slice(None) for _ in shape)].bitcast(F32)

    def at(self, *index):
        return self.high[(slice(None), *index)], self.low[(slice(None), *index)]


def in_halves(pe, out, left, right, start, stop):
    pe.matmul(out, left[0], right[0], start=start, stop=False, skip_group_check=True)
    pe.matmul(out, left[0], right[1], start=False, stop=False, skip_group_check=True)
    return pe.matmul(out, left[1], right[0], start=False, stop=stop, skip_group_check=True)


def keep_stats(dve, m, MVS, b, kept):
    dve.tensor_scalar(m.MV[:, bass.ds(b * T, T), :], MVS[:, :, :], 1.0, None, ALU.mult)
    dve.tensor_scalar(m.RSTD[:, bass.ds(b * T, T)], MVS[:, :, 1], LN_EPS, None, ALU.add).then_inc(kept, 1)


def make_rstd(pool, m, kept, b):
    at = bass.ds(b * T, T)
    wait_apart(pool, kept, b + 1, m.waited)
    pool.tensor_tensor(m.RSTD[:, at], m.RSTD[:, at], m.MHALF[:, 0:T], ALU.pow)


def retire(nc, mem):
    numbers = sorted(s.num for s in mem.known.values())
    with nc.Block() as block:

        @block.sync
        def _(sp):
            first = prev = numbers[0]
            for n in numbers[1:] + [None]:
                if n is not None and n == prev + 1:
                    prev = n
                    continue
                sp.sem_clear(range(first, prev + 1))
                first = prev = n


def tiles(ap, t=T):
    return ap.rearrange("p (t d) -> p t d", t=t)




def setup(nc, m, IN):
    with ExitStack() as stack:
        mem = Memory(nc, stack)
        S = mem.sem
        W0 = mem.sb("gat_w", P, 128)
        A12 = mem.sb("gat_a", P, 2)
        GW = mem.sb("ode_w", P, 128)
        FW = mem.sb("fc_w", P, 128)
        FB = mem.sb("fc_b", P, 1)
        DC = mem.sb("ode_d", P, 1)
        WO = mem.sb("mamba_out_w", P, 2, 128)
        WL = mem.sb("mamba_lin_w", P, 128)
        NW = mem.sb("mamba_norm_w", P, 2)
        AL = mem.sb("alpha", P, T)
        SG = mem.sb("alpha_scaled", P, 3, T)
        BNR = mem.sb("bn_rows", 80, 128)
        BNT = mem.sb("bn_tmp", P, 2, 16)
        WT = mem.sb("turned_weights", P, 256)
        BT = mem.sb("bn_columns", P, 80)
        WOT = mem.sb("mamba_out_w_turned", P, 256)
        WTD = mem.sb("ode_wt_scaled", P, 128)
        RI = mem.sb("ode_decay_ident", P, 128)
        ADJ = mem.sb("adj", P, T, N)
        L = mem.sb("L", P, T, N)
        L3 = mem.sb("L3", P, T, N)
        RP = mem.sb("R_powers", P, 9, 128)
        FRP = mem.sb("F_R_powers", P, 9, 128)
        BK = mem.sb("fc_b_columns", P, 9, 3)
        ST = mem.sb("stats", P, Q, 6)
        bank = mem.banks("setup_bank", 8)

        def col(ap):
            return ap.rearrange("(p o) -> p o", o=1)

        def wide(ap, n):
            return ap.rearrange("(o n) -> o n", o=1).broadcast_to([P, n])

        with nc.Block() as block:

            @block.sync
            def _(sp):
                sp.dma_start(ADJ[:, :, :], IN["adj"].rearrange("(t p) m -> p t m", p=P)).then_inc(S("adj_loaded"), 16)
                for g in range(4):
                    for b in range(4 * g, 4 * g + 4):
                        sp.dma_start(tiles(m.X[:, b * 512:(b + 1) * 512]),
                                     IN["x"][b].rearrange("(t p) d -> p t d", p=P)).then_inc(S(f"x_loaded{g}"), 16)
                for dst, name, form in ((m.W1, "L1_ffn_W1", "e d h -> d e h"), (m.W2, "L1_ffn_W2", "e d h -> d e h"),
                                        (m.W3, "L1_ffn_Wo", "e d h -> d e h")):
                    sp.dma_start(dst[:, :, :], IN[name].rearrange(form)).then_inc(S("experts_loaded"), 16)
                sp.wait_ge(S("experts_loaded"), 48)

            @block.gpsimd
            def _(pool):
                pool.memset(m.IDENT[:, :], 0.0).then_inc(S("pool_zero"), 1)
                pool.memset(m.LE[:, :], 1.0).then_inc(S("pool_zero"), 1)
                pool.memset(m.GT[:, :], 1.0).then_inc(S("pool_zero"), 1)
                pool.memset(m.ONES[:, :], 1.0).then_inc(S("pool_zero"), 1)
                pool.memset(m.MHALF[:, :], -0.5).then_inc(S("pool_zero"), 1)
                pool.memset(BK[:, :, :], 0.0).then_inc(S("columns_zero"), 1)
                pool.wait_ge(S("pool_zero"), 5)
                pool.affine_select(out=m.IDENT[:, :], in_=m.IDENT[:, :], compare_op=ALU.not_equal, fill=1.0,
                                   base=0, pattern=[[-1, P]], channel_multiplier=1).then_inc(S("masks"), 1)
                pool.affine_select(out=m.LE[:, :], in_=m.LE[:, :], compare_op=ALU.is_ge, fill=0.0,
                                   base=0, pattern=[[1, P]], channel_multiplier=-1).then_inc(S("masks"), 1)
                pool.affine_select(out=m.GT[:, :], in_=m.GT[:, :], compare_op=ALU.is_gt, fill=0.0,
                                   base=0, pattern=[[-1, P]], channel_multiplier=1).then_inc(S("masks"), 1)
                pool.wait_ge(S("bn_turned_copied"), 1)
                for k, at in enumerate((32, 72)):
                    pool.tensor_scalar(BNT[:, 0, 8 * k:8 * k + 8], BT[:, at:at + 8], BN_EPS, None,
                                       ALU.add).then_inc(S("bn_var"), 1)
                pool.wait_ge(S("bn_var"), 2)
                pool.tensor_tensor(BNT[:, 1, :], BNT[:, 0, :], m.MHALF[:, 0:16], ALU.pow).then_inc(S("bn_rstd"), 1)
                pool.wait_ge(S("stats_known"), Q)
                pool.tensor_scalar(m.RSTD[:, :], m.MV[:, :, 1], LN_EPS, None, ALU.add).then_inc(S("ln_var"), 1)
                pool.wait_ge(S("ln_var"), 1)
                pool.tensor_tensor(m.RSTD[:, :], m.RSTD[:, :], m.MHALF[:, :], ALU.pow)

            @block.scalar
            def _(act):
                act.dma_start(AL[:, :], IN["L1_gnn_alpha_train"].rearrange("(t p) -> p t", p=P)).then_inc(S("alpha_loaded"), 16)
                for dst, src in ((W0[:, :], IN["L0_gnn_W"]), (A12[:, :], IN["L0_gnn_a"].rearrange("(k p) o -> p (k o)", k=2)),
                                 (GW[:, :], IN["L1_gnn_w"]), (FW[:, :], IN["L1_gnn_fc_in_w"]),
                                 (FB[:, :], col(IN["L1_gnn_fc_in_b"])), (DC[:, :], col(IN["L1_gnn_d"])),
                                 (WO[:, :, :], IN["L0_ffn_W_out"].rearrange("(g p) n -> p g n", p=P)),
                                 (WL[:, :], IN["L0_ffn_W_lin"]),
                                 (NW[:, :], IN["L0_ffn_norm_w"].rearrange("(g p) -> p g", p=P))):
                    act.dma_start(dst, src).then_inc(S("weights_loaded"), 16)
                act.wait_ge(S("alpha_loaded"), 16)
                act.activation(SG[:, 0, :], AL[:, :], ACT.Exp, scale=-1.0).then_inc(S("alpha_exp"), 1)
                for k, name in enumerate(("b1", "g1", "be1", "m1", "v1", "b2", "g2", "be2", "m2", "v2")):
                    act.dma_start(BNR[8 * k:8 * k + 8, :], IN["L1_ffn_" + name]).then_inc(S("bn_loaded"), 16)
                for dst, src in ((m.WIN[:, :], IN["L0_ffn_W_in"]),
                                 (m.CW[:, :, :], IN["L0_ffn_conv_w"].rearrange("(g p) k -> p g k", p=P)),
                                 (m.CB[:, :], IN["L0_ffn_conv_b"].rearrange("(g p) -> p g", p=P)),
                                 (m.DTB[:, :], wide(IN["L0_ffn_dt_bias"], 4)), (m.AH[:, :], wide(IN["L0_ffn_A_log"], 4)),
                                 (m.DH[:, :], wide(IN["L0_ffn_D"], 4)), (m.BLIN[:, :], wide(IN["L0_ffn_b_lin"], 128)),
                                 (m.WR[:, :], IN["L1_ffn_Wr"]), (m.BR[:, :], wide(IN["L1_ffn_br"], 8)),
                                 (m.BO[:, :], IN["L1_ffn_bo"])):
                    act.dma_start(dst, src).then_inc(S("later_loaded"), 16)

                def keep_power(k, dst, ts):
                    for t in ts:
                        act.wait_ge(S("L_product"), T * k + t + 1)
                        act.activation(dst[:, t, :], bank[4 + t][:, :], ACT.Copy).then_inc(S("L_copied"), 1)

                keep_power(0, m.LT, range(T))
                keep_power(1, m.L2T, (0, 1))
                act.wait_ge(S("turned"), 1)
                act.activation(WT[:, :], bank[0][:, 0:256], ACT.Copy).then_inc(S("turned_copied"), 1)
                act.wait_ge(S("turned"), 2)
                act.activation(WOT[:, :], bank[1][:, 0:256], ACT.Copy).then_inc(S("turned_copied"), 1)
                keep_power(1, m.L2T, (2, 3))
                keep_power(2, m.L3T, range(T))
                keep_power(3, L3, range(T))
                act.wait_ge(S("bn_turned"), 1)
                act.activation(BT[:, :], bank[0][:, 256:336], ACT.Copy).then_inc(S("bn_turned_copied"), 1)
                act.wait_ge(S("fc_b_products"), 1)
                act.activation(m.CR[:, :], bank[1][0:3, 0:384], ACT.Copy)
                keep_power(4, m.L6T, range(T))
                act.wait_ge(S("later_loaded"), 16 * 10)
                act.activation(m.AH[:, :], m.AH[:, :], ACT.Exp)

            @block.tensor
            def _(pe):
                def turn_weights():
                    pe.wait_ge(S("weights_loaded"), 16 * 9)
                    pe.transpose(bank[0][:, 0:128], W0[:, :], m.IDENT[:, :])
                    pe.transpose(bank[0][:, 128:256], GW[:, :], m.IDENT[:, :]).then_inc(S("turned"), 1)
                    pe.transpose(bank[1][:, 0:128], WO[:, 0, :], m.IDENT[:, :])
                    pe.transpose(bank[1][:, 128:256], WO[:, 1, :], m.IDENT[:, :]).then_inc(S("turned"), 1)

                def small_products():
                    pe.wait_ge(S("turned_copied"), 2)
                    pe.wait_ge(S("ode_wt_scaled"), 1)
                    pe.matmul(bank[2][:, 0:2], WT[:, 0:128], A12[:, :], start=True, stop=True)
                    pe.matmul(bank[2][:, 128:256], WT[:, 128:256], WTD[:, :], start=True, stop=True)
                    for g in range(2):
                        mm = pe.matmul(bank[2][:, 256 + 128 * g:384 + 128 * g], WOT[:, 128 * g:128 * g + 128], WL[:, :],
                                       start=True, stop=True)
                    mm.then_inc(S("small_products"), 1)

                def r_powers(k):
                    pe.wait_ge(S("R_known"), {1: 1, 2: 2, 4: 3}[k])
                    pe.matmul(bank[3][:, 0:128 * k], RP[:, k, :], RP[:, 1:k + 1, :], start=True, stop=True)\
                      .then_inc(S("R_product"), 1)

                def f_powers(k, n):
                    pe.wait_ge(S("R_known"), 4)
                    if k:
                        pe.wait_ge(S("FR_copied"), k // 4)
                    pe.matmul(bank[3][:, 0:128 * n], FW[:, :], RP[:, k:k + n, :], start=True, stop=True)\
                      .then_inc(S("FR_product"), 1)

                def power(k, left, right, between):
                    pe.wait_ge(S("L_copied"), T * k)
                    for t in range(T):
                        for s in range(T):
                            mm = pe.matmul(bank[4 + t][:, :], left[:, s, t * P:(t + 1) * P], right[:, s, :],
                                           start=(s == 0), stop=(s == T - 1))
                        mm.then_inc(S("L_product"), 1)
                        between[t]()

                def turn(source):
                    for t in range(T):
                        for s in range(T):
                            mm = pe.transpose(bank[4 + t][:, s * P:(s + 1) * P], source[:, s, t * P:(t + 1) * P],
                                              m.IDENT[:, :])
                        mm.then_inc(S("L_product"), 1)

                pe.wait_ge(S("masks"), 3)
                pe.wait_ge(S("L_known"), T)
                turn(L)
                power(1, L, m.LT, (nothing, turn_weights, small_products, lambda: r_powers(1)))
                power(2, L, m.L2T, (lambda: r_powers(2), lambda: r_powers(4), lambda: f_powers(0, 4),
                                    lambda: f_powers(4, 4)))
                pe.wait_ge(S("L_copied"), 3 * T)
                turn(m.L3T)
                f_powers(8, 1)
                pe.wait_ge(S("bn_loaded"), 16 * 10)
                pe.transpose(bank[0][:, 256:336], BNR[:, :], m.IDENT[0:80, 0:80]).then_inc(S("bn_turned"), 1)
                pe.wait_ge(S("fc_b_columns"), 9)
                for q in range(3):
                    for j in range(3):
                        k = 3 * q + j
                        mm = pe.matmul(bank[1][0:3, 128 * q:128 * q + 128], BK[:, k, :], RP[:, STEPS - k, :],
                                       start=(j == 0), stop=(j == 2))
                mm.then_inc(S("fc_b_products"), 1)
                power(4, L3, m.L3T, (nothing,) * 4)

            @block.vector
            def _(dve):
                dve.wait_ge(S("alpha_exp"), 1)
                dve.tensor_scalar(SG[:, 0, :], SG[:, 0, :], 1.0, None, ALU.add).then_inc(S("alpha"), 1)
                dve.wait_ge(S("alpha"), 1)
                dve.reciprocal(SG[:, 2, :], SG[:, 0, :]).then_inc(S("alpha"), 1)
                dve.wait_ge(S("alpha"), 2)
                dve.tensor_scalar(SG[:, 1, :], SG[:, 2, :], 0.5 * DT, None, ALU.mult).then_inc(S("alpha"), 1)
                dve.wait_ge(S("alpha"), 3)
                dve.tensor_scalar(SG[:, 2, :], SG[:, 1, :], -1.0, None, ALU.mult).then_inc(S("alpha"), 1)
                dve.wait_ge(S("alpha"), 4)
                dve.wait_ge(S("adj_loaded"), 16)
                dve.wait_ge(S("masks"), 3)
                for t in range(T):
                    dve.tensor_scalar(L[:, t, :], ADJ[:, t, :], SG[:, 1, t:t + 1], None, ALU.mult).then_inc(S("L_adj"), 1)
                for t in range(T):
                    dve.wait_ge(S("L_adj"), t + 1)
                    diag = L[:, t, t * P:(t + 1) * P]
                    dve.scalar_tensor_tensor(out=diag, in0=m.IDENT[:, :], scalar=SG[:, 2, t:t + 1], in1=diag,
                                             op0=ALU.mult, op1=ALU.add).then_inc(S("L_known"), 1)
                dve.tensor_scalar(m.NEGM[:, :, :], ADJ[:, :, :], 0.0, NEG, ALU.is_equal, ALU.mult)
                dve.wait_ge(S("weights_loaded"), 16 * 9)
                dve.wait_ge(S("columns_zero"), 1)
                for k in range(9):
                    dve.tensor_scalar(BK[:, k, k % 3:k % 3 + 1], FB[:, :], float(comb(STEPS, k)), None,
                                      ALU.mult).then_inc(S("fc_b_columns"), 1)
                dve.tensor_scalar(DC[:, :], DC[:, :], 0.0, 1.0, ALU.max, ALU.min).then_inc(S("clipped"), 1)
                dve.wait_ge(S("clipped"), 1)
                dve.wait_ge(S("turned_copied"), 1)
                dve.tensor_scalar(WTD[:, :], WT[:, 128:256], DC[:, 0:1], None, ALU.mult).then_inc(S("ode_wt_scaled"), 1)
                dve.tensor_scalar(RI[:, :], m.IDENT[:, :], 1.0 - DT, None, ALU.mult).then_inc(S("decay_ident"), 1)
                dve.tensor_copy(RP[:, 0, :], m.IDENT[:, :])
                dve.tensor_copy(m.WEXT[:, 0:128], W0[:, :])
                dve.wait_ge(S("decay_ident"), 1)
                dve.wait_ge(S("small_products"), 1)
                dve.scalar_tensor_tensor(out=RP[:, 1, :], in0=bank[2][:, 128:256], scalar=DT, in1=RI[:, :],
                                         op0=ALU.mult, op1=ALU.add).then_inc(S("R_known"), 1)
                dve.tensor_copy(m.WEXT[:, 128:130], bank[2][:, 0:2]).then_inc(S("wa_known"), 1)
                for g in range(2):
                    dve.tensor_scalar(m.WF[:, g, :], bank[2][:, 256 + 128 * g:384 + 128 * g], NW[:, g:g + 1], None, ALU.mult)
                dve.wait_ge(S("wa_known"), 1)
                dve.tensor_copy(m.WA2B[:, :], m.WEXT[:, 129:130].broadcast_to([P, P]))

                def stats(g):
                    dve.wait_ge(S(f"x_loaded{g}"), 64)
                    for q in range(16 * g, 16 * g + 16):
                        dve.bn_stats(ST[:, q, :], m.X[:, q * P:(q + 1) * P]).then_inc(S("stats"), 1)

                stats(0)
                for k, (at, n) in enumerate(((2, 1), (3, 2), (5, 4))):
                    dve.wait_ge(S("R_product"), k + 1)
                    dve.tensor_copy(RP[:, at:at + n, :], bank[3][:, 0:128 * n].rearrange("p (k n) -> p k n", k=n))\
                       .then_inc(S("R_known"), 1)
                    stats(k + 1)
                for q in range(Q):
                    dve.wait_ge(S("stats"), q + 1)
                    dve.bn_aggr(m.MV[:, q, :], ST[:, q, :]).then_inc(S("stats_known"), 1)
                for k, n in ((0, 4), (4, 4), (8, 1)):
                    dve.wait_ge(S("FR_product"), k // 4 + 1)
                    dve.tensor_copy(FRP[:, k:k + n, :], bank[3][:, 0:128 * n].rearrange("p (k n) -> p k n", k=n))\
                       .then_inc(S("FR_copied"), 1)
                dve.wait_ge(S("R_known"), 4)
                dve.wait_ge(S("FR_copied"), 3)
                done = 0
                last = [0] * 9
                for k in range(9):
                    done += 1
                    last[k] = done
                    dve.tensor_scalar(m.E[:, k, :], FRP[:, STEPS - k, :], float(comb(STEPS, k)), None,
                                      ALU.mult).then_inc(S("E_terms"), 1)
                for r in range(STEPS):
                    for k in range(STEPS - r):
                        dve.wait_ge(S("E_terms"), last[k])
                        done += 1
                        last[k] = done
                        dve.scalar_tensor_tensor(out=m.E[:, k, :], in0=RP[:, r, :], scalar=DT * comb(r + k, k),
                                                 in1=m.E[:, k, :], op0=ALU.mult, op1=ALU.add).then_inc(S("E_terms"), 1)
                dve.wait_ge(S("bn_rstd"), 1)
                for k in range(2):
                    bb, g, be, mm_ = (BT[:, 40 * k + 8 * j:40 * k + 8 * j + 8] for j in range(4))
                    a, c = m.BNA[:, 8 * k:8 * k + 8], m.BNC[:, 8 * k:8 * k + 8]
                    dve.tensor_tensor(a, g, BNT[:, 1, 8 * k:8 * k + 8], ALU.mult).then_inc(S("bn"), 1)
                    dve.tensor_tensor(c, bb, mm_, ALU.subtract).then_inc(S("bn"), 1)
                    dve.wait_ge(S("bn"), 4 * k + 2)
                    dve.tensor_tensor(c, c, a, ALU.mult).then_inc(S("bn"), 1)
                    dve.wait_ge(S("bn"), 4 * k + 3)
                    dve.tensor_tensor(c, c, be, ALU.add).then_inc(S("bn"), 1)
        retire(nc, mem)




def attention(nc, m):
    with ExitStack() as stack:
        mem = Memory(nc, stack)
        S = mem.sem
        H = [mem.sb(f"gat_h{u}", P, T, P) for u in range(2)]
        HTS = [mem.sb(f"gat_ht{u}", P, N) for u in range(2)]
        WH = [mem.sb(f"gat_wh{u}", P, T, 130) for u in range(2)]
        ZM = [mem.sb(f"gat_masked{u}", P, T, N) for u in range(2)]
        V2 = mem.sb("gat_leaky", P, T, N)
        PS = mem.sb("gat_probs", P, T, N)
        PT = [mem.sb(f"gat_probs_t{k}", P, T, P) for k in range(2)]
        C = [mem.sb(f"gat_cols{u}", P, 6, T) for u in range(2)]
        RC = mem.sb("gat_recip", P, T)
        ST = mem.sb("gat_stats", P, T, 6)
        MVS = mem.sb("gat_mean_var", P, T, 2)
        b_ht, = mem.banks("gat_b_ht", 1)
        b_wh = mem.banks("gat_b_wh", 2)
        b_s2 = mem.banks("gat_b_s2", 2)
        b_pt = mem.banks("gat_b_pt", 2)
        b_o, = mem.banks("gat_b_o", 1)

        with nc.Block() as block:

            @block.gpsimd
            def _(pool):
                over_batches(pool, lambda b, u, first, last: make_rstd(pool, m, S("stats1_kept"), b))

            @block.vector
            def _(dve):
                def norm(b, u):
                    wait(dve, S("h_turned"), b - 1)
                    for t in range(T):
                        q = b * T + t
                        dve.tensor_scalar(H[u][:, t, :], m.X[:, bass.ds(q * P, P)], m.MV[:, bass.ds(q, 1), 0],
                                          m.RSTD[:, bass.ds(q, 1)], ALU.subtract, ALU.mult).then_inc(S("h_ready"), 1)

                def mask(b, u, ts):
                    if 0 in ts:
                        wait_apart(dve, S("s2_ready"), b + 1, m.waited)
                        wait_apart(dve, S("exped"), (b - 1) * T, m.waited)
                    for t in ts:
                        dve.tensor_tensor_reduce(ZM[u][:, t, :], b_s2[u][:, :], m.NEGM[:, t, :], 1.0, 3 * NEG, ALU.add,
                                                 ALU.max, C[u][:, 0, t:t + 1]).then_inc(S("masked"), 1)

                def columns(b, u):
                    s1 = WH[u][:, :, 128]
                    dve.wait_ge(S("masked"), b * T + T)
                    dve.wait_ge(S("wh_ready"), b + 1)
                    dve.tensor_tensor(C[u][:, 1, :], s1, C[u][:, 0, :], ALU.add).then_inc(S("cols"), 1)
                    dve.wait_ge(S("cols"), b * 4 + 1)
                    dve.scalar_tensor_tensor(out=C[u][:, 2, :], in0=C[u][:, 1, :], scalar=LEAK, in1=C[u][:, 1, :],
                                             op0=ALU.mult, op1=ALU.max).then_inc(S("cols"), 1)
                    dve.wait_ge(S("cols"), b * 4 + 2)
                    dve.tensor_tensor(C[u][:, 3, :], s1, C[u][:, 2, :], ALU.subtract).then_inc(S("cols"), 1)
                    dve.scalar_tensor_tensor(out=C[u][:, 4, :], in0=s1, scalar=LEAK, in1=C[u][:, 2, :],
                                             op0=ALU.mult, op1=ALU.subtract).then_inc(S("cols"), 1)

                def score(b, u, t):
                    if t == 0:
                        dve.wait_ge(S("cols"), b * 4 + 4)
                    dve.wait_ge(S("leaky_made"), b * T + t + 1)
                    dve.scalar_tensor_tensor(out=ZM[u][:, t, :], in0=ZM[u][:, t, :], scalar=C[u][:, 3, t:t + 1],
                                             in1=V2[:, t, :], op0=ALU.add, op1=ALU.max).then_inc(S("scored"), 1)

                def update(b, u):
                    dve.wait_ge(S("exped"), b * T + T)
                    dve.reciprocal(RC[:, :], C[u][:, 5, :]).then_inc(S("recip"), 1)
                    dve.wait_ge(S("recip"), b + 1)
                    for t in range(T):
                        dve.wait_ge(S("mixed"), b * T + T)
                        xt = m.X[:, bass.ds((b * T + t) * P, P)]
                        dve.scalar_tensor_tensor(out=xt, in0=b_o[:, t * P:(t + 1) * P], scalar=RC[:, t:t + 1], in1=xt,
                                                 op0=ALU.mult, op1=ALU.add).then_inc(S("x1"), 1)

                def stats(b):
                    wait_apart(dve, S("x1"), b * T + T, m.waited)
                    wait_apart(dve, S("stats1_known"), b * T, m.waited)
                    for t in range(T):
                        dve.bn_stats(ST[:, t, :], m.X[:, bass.ds((b * T + t) * P, P)]).then_inc(S("stats1"), 1)

                def means(b):
                    wait_apart(dve, S("stats1"), b * T + T, m.waited)
                    wait_apart(dve, S("stats1_kept"), b, m.waited)
                    for t in range(T):
                        dve.bn_aggr(MVS[:, t, :], ST[:, t, :]).then_inc(S("stats1_known"), 1)

                def keep(b):
                    dve.wait_ge(S("stats1_known"), b * T + T)
                    keep_stats(dve, m, MVS, b, S("stats1_kept"))

                norm(0, 0)
                norm(1, 1)
                mask(0, 0, range(T))
                columns(0, 0)

                def body(b, u, first, one_ahead, two_ahead):
                    for t in range(T):
                        score(b, u, t)
                    if not first:
                        update(b - 1, 1 - u)
                    if two_ahead:
                        norm(b + 2, u)
                    if one_ahead:
                        mask(b + 1, 1 - u, (0, 1))
                    if not first:
                        stats(b - 1)
                    if one_ahead:
                        mask(b + 1, 1 - u, (2, 3))
                    if not first:
                        means(b - 1)
                    if one_ahead:
                        columns(b + 1, 1 - u)
                    if not first:
                        keep(b - 1)

                turns(dve, body)
                update(B - 1, 1)
                stats(B - 1)
                means(B - 1)
                keep(B - 1)

            @block.tensor
            def _(pe):
                def transposes(b, u):
                    wait(pe, S("ht_ready"), b)
                    for t in range(T):
                        pe.wait_ge(S("h_ready"), b * T + t + 1)
                        mm = pe.transpose(b_ht[:, t * P:(t + 1) * P], H[u][:, t, :], m.IDENT[:, :])
                    mm.then_inc(S("h_turned"), 1)

                def project(b, u):
                    pe.wait_ge(S("ht_ready"), b + 1)
                    wait(pe, S("masked"), (b - 1) * T)
                    pe.matmul(b_s2[u][:, :], m.WA2B[:, :], HTS[u][:, :], start=True, stop=True).then_inc(S("s2_ready"), 1)
                    wait(pe, S("wh_ready"), b)
                    for t in range(T):
                        at = 130 * (t % 2)
                        mm = pe.matmul(b_wh[t // 2][:, at:at + 130], HTS[u][:, t * P:(t + 1) * P], m.WEXT[:, :],
                                       start=True, stop=True)
                    mm.then_inc(S("wh_product"), 1)

                def turn(b, u, t):
                    pe.wait_ge(S("exped"), b * T + t + 1)
                    wait(pe, S("probs_t"), b * T + t - 1)
                    for s in range(T):
                        mm = pe.transpose(b_pt[t % 2][:, s * P:(s + 1) * P], PS[:, t, s * P:(s + 1) * P], m.IDENT[:, :])
                    mm.then_inc(S("probs_turned"), 1)

                def mix(b, u, t):
                    pe.wait_ge(S("probs_t"), b * T + t + 1)
                    if t == 0:
                        wait(pe, S("x1"), b * T)
                    for s in range(T):
                        mm = pe.matmul(b_o[:, t * P:(t + 1) * P], PT[t % 2][:, s, :], WH[u][:, s, 0:128],
                                       start=(s == 0), stop=(s == T - 1))
                    mm.then_inc(S("mixed"), 1)

                for u in range(2):
                    transposes(u, u)
                    project(u, u)

                def body(b, u, first, one_ahead, two_ahead):
                    turn(b, u, 0)
                    turn(b, u, 1)
                    mix(b, u, 0)
                    turn(b, u, 2)
                    mix(b, u, 1)
                    turn(b, u, 3)
                    if two_ahead:
                        transposes(b + 2, u)
                    mix(b, u, 2)
                    mix(b, u, 3)
                    if two_ahead:
                        project(b + 2, u)

                turns(pe, body)

            @block.scalar
            def _(act):
                def keep_ht(b, u):
                    act.wait_ge(S("h_turned"), b + 1)
                    wait(act, S("wh_product"), b - 1)
                    act.activation(HTS[u][:, :], b_ht[:, :], ACT.Copy).then_inc(S("ht_ready"), 1)

                def keep_wh(b, u):
                    act.wait_ge(S("wh_product"), b + 1)
                    wait(act, S("mixed"), (b - 1) * T)
                    wait(act, S("cols"), (b - 1) * 4)
                    act.activation(WH[u][:, 0:2, :], b_wh[0][:, 0:260].rearrange("p (t n) -> p t n", t=2), ACT.Copy)
                    act.activation(WH[u][:, 2:4, :], b_wh[1][:, 0:260].rearrange("p (t n) -> p t n", t=2), ACT.Copy)\
                       .then_inc(S("wh_ready"), 1)

                def leaky(b, u):
                    act.wait_ge(S("cols"), b * 4 + 4)
                    wait(act, S("scored"), b * T)
                    for t in range(T):
                        act.activation(V2[:, t, :], ZM[u][:, t, :], ACT.Identity, bias=C[u][:, 4, t:t + 1], scale=LEAK)\
                           .then_inc(S("leaky_made"), 1)

                def exp(b, u, t):
                    act.wait_ge(S("scored"), b * T + t + 1)
                    if t == 0:
                        wait(act, S("recip"), b - 1)
                        wait(act, S("probs_turned"), b * T)
                    act.activation(PS[:, t, :], ZM[u][:, t, :], ACT.Exp, accum_out=C[u][:, 5, t:t + 1])\
                       .then_inc(S("exped"), 1)

                def evacuate(b, t):
                    act.wait_ge(S("probs_turned"), b * T + t + 1)
                    wait(act, S("mixed"), b * T + t - 1)
                    act.activation(PT[t % 2][:, :, :], tiles(b_pt[t % 2][:, :]), ACT.Copy).then_inc(S("probs_t"), 1)

                for u in range(2):
                    keep_ht(u, u)
                    keep_wh(u, u)
                leaky(0, 0)

                def body(b, u, first, one_ahead, two_ahead):
                    exp(b, u, 0)
                    exp(b, u, 1)
                    evacuate(b, 0)
                    exp(b, u, 2)
                    evacuate(b, 1)
                    exp(b, u, 3)
                    evacuate(b, 2)
                    if two_ahead:
                        keep_ht(b + 2, u)
                    evacuate(b, 3)
                    if one_ahead:
                        leaky(b + 1, 1 - u)
                    if two_ahead:
                        keep_wh(b + 2, u)

                turns(act, body)

        retire(nc, mem)




def normalise(nc, m, name, extra):
    with ExitStack() as stack:
        mem = Memory(nc, stack)
        S = mem.sem
        H = [mem.sb(f"{name}_h{u}", P, T, P) for u in range(2)]
        HTS = [mem.sb(f"{name}_ht{u}", P, N) for u in range(2)]
        b_ht = mem.banks(f"{name}_b_ht", 2)
        x = extra(nc, m, mem, H, HTS)

        with nc.Block() as block:

            @block.gpsimd
            def _(pool):
                over_batches(pool, lambda *a: x.pool(pool, *a))

            @block.vector
            def _(dve):
                x.dve_start(dve)

                def norm(b, u):
                    wait(dve, S("h_turned"), b - 1)
                    x.wait_h_free(dve, b)
                    for t in range(T):
                        q = b * T + t
                        dve.tensor_scalar(H[u][:, t, :], m.X[:, bass.ds(q * P, P)], m.MV[:, bass.ds(q, 1), 0],
                                          m.RSTD[:, bass.ds(q, 1)], ALU.subtract, ALU.mult).then_inc(S("h_ready"), 1)

                norm(0, 0)
                norm(1, 1)

                def body(b, u, first, one_ahead, two_ahead):
                    if two_ahead:
                        norm(b + 2, u)
                    x.dve(dve, b, u)

                turns(dve, body)
                x.dve_end(dve)

            @block.tensor
            def _(pe):
                def turn(b, u):
                    wait(pe, S("ht_ready"), b - 1)
                    for t in range(T):
                        pe.wait_ge(S("h_ready"), b * T + t + 1)
                        mm = pe.transpose(b_ht[u][:, t * P:(t + 1) * P], H[u][:, t, :], m.IDENT[:, :])
                    mm.then_inc(S("h_turned"), 1)

                def body(b, u, first, last):
                    if not last:
                        turn(b + 1, 1 - u)
                    x.pe(pe, b, u)

                x.pe_start(pe)
                turn(0, 0)
                over_batches(pe, body)
                x.pe_end(pe)

            @block.scalar
            def _(act):
                def body(b, u, first, last):
                    act.wait_ge(S("h_turned"), b + 1)
                    wait(act, S(f"ht_kept{u}"), (b - u) * 8)
                    x.wait_ht_free(act, b)
                    act.activation(HTS[u][:, :], b_ht[u][:, :], ACT.Copy).then_inc(S("ht_ready"), 1)

                over_batches(act, body)
                x.act_end(act)

            @block.sync
            def _(sp):
                def body(b, u, first, last):
                    wait_apart(sp, S("ht_ready"), b + 1, m.waited)
                    sp.dma_start(m.HT[:, bass.ds(b * N, N)], HTS[u][:, :]).then_inc(S(f"ht_kept{u}"), 16)

                over_batches(sp, body)
                for u in range(2):
                    sp.wait_ge(S(f"ht_kept{u}"), 16 * B // 2)
        retire(nc, mem)


def mamba_steps(nc, m, mem, H, HTS):
    S = mem.sem
    RAW = mem.sb("dt_raw", P, Q, HEADS)
    EX = mem.sb("dt_exp", P, Q, HEADS)
    U = mem.sb("dt_one_plus", P, Q, HEADS)
    R = mem.sb("dt_recip", P, Q, HEADS)
    LN = mem.sb("dt_ln", P, Q, HEADS)
    b_dt = mem.banks("dt_b", 2)
    b_sum = mem.banks("dt_b_sum", 3)
    wide = [P, Q, HEADS]

    def flat(ap):
        return ap.rearrange("p q h -> p (q h)")

    def pe(e, b, u):
        e.wait_ge(S("ht_ready"), b + 1)
        wait(e, S("dt_raw"), b - 1)
        for t in range(T):
            mm = e.matmul(b_dt[u][:, HEADS * t:HEADS * t + HEADS], HTS[u][:, t * P:(t + 1) * P], m.WIN[:, 640:644],
                          start=True, stop=True)
        mm.then_inc(S("dt_product"), 1)

    def dve(e, b, u):
        e.wait_ge(S("dt_product"), b + 1)
        e.scalar_tensor_tensor(out=RAW[:, bass.ds(b * T, T), :].rearrange("p q h -> p (q h)"),
                               in0=b_dt[u][:, 0:T * HEADS], scalar=1.0, in1=DTB16[:, :],
                               op0=ALU.mult, op1=ALU.add).then_inc(S("dt_raw"), 1)

    DTB16 = mem.sb("dt_bias_wide", P, T * HEADS)
    AR = mem.sb("dt_abs", P, Q, HEADS)

    def dve_start(e):
        e.tensor_copy(DTB16[:, :].rearrange("p (t h) -> p t h", t=T), m.DTB[:, :].unsqueeze(1).broadcast_to([P, T, HEADS]))\
         .then_inc(S("dt_bias_wide"), 1)
        e.wait_ge(S("dt_bias_wide"), 1)

    def dve_end(e):
        e.wait_ge(S("dt_exp"), 1)
        e.tensor_scalar(U[:, :, :], EX[:, :, :], 1.0, None, ALU.add).then_inc(S("dt_one_plus"), 1)
        e.wait_ge(S("dt_one_plus"), 1)
        e.reciprocal(R[:, :, :], U[:, :, :]).then_inc(S("dt_rest"), 1)
        e.scalar_tensor_tensor(out=flat(EX[:, :, :]), in0=flat(U[:, :, :]), scalar=1.0, in1=flat(EX[:, :, :]),
                               op0=ALU.subtract, op1=ALU.subtract).then_inc(S("dt_rest"), 1)
        e.wait_ge(S("dt_rest"), 2)
        e.tensor_tensor(EX[:, :, :], EX[:, :, :], R[:, :, :], ALU.mult).then_inc(S("dt_rest"), 1)
        e.wait_ge(S("dt_rest"), 3)
        e.wait_ge(S("dt_ln"), 1)
        e.tensor_tensor(LN[:, :, :], LN[:, :, :], EX[:, :, :], ALU.subtract).then_inc(S("dt_rest"), 1)
        e.wait_ge(S("dt_rest"), 4)
        e.scalar_tensor_tensor(out=flat(m.DTS[:, :, :]), in0=flat(RAW[:, :, :]), scalar=0.0, in1=flat(LN[:, :, :]),
                               op0=ALU.max, op1=ALU.add).then_inc(S("dt_rest"), 1)
        e.wait_ge(S("dt_rest"), 5)
        e.tensor_tensor(m.DA[:, :, :], m.DTS[:, :, :], m.AH[:, :].unsqueeze(1).broadcast_to(wide), ALU.mult)\
         .then_inc(S("dA_positive"), 1)
        e.wait_ge(S("dA_positive"), 1)
        e.tensor_scalar(m.DA[:, :, :], m.DA[:, :, :], -1.0, None, ALU.mult).then_inc(S("dA_ready"), 1)
        e.wait_ge(S("decays"), 3)
        e.tensor_tensor(m.DD[:, :, :], m.DD[:, :, :], m.DTS[:, :, :], ALU.mult)

    def pe_end(e):
        e.wait_ge(S("dA_ready"), 1)
        for k, mask in enumerate((m.LE, m.GT, m.ONES)):
            e.matmul(b_sum[k][:, 0:Q * HEADS], mask[:, :], flat(m.DA[:, :, :]), start=True, stop=True)\
             .then_inc(S("dA_sums"), 1)

    def act_end(act):
        act.wait_ge(S("dt_raw"), B)
        act.activation(AR[:, :, :], RAW[:, :, :], ACT.Abs).then_inc(S("dt_abs"), 1)
        act.wait_ge(S("dt_abs"), 1)
        act.activation(EX[:, :, :], AR[:, :, :], ACT.Exp, scale=-1.0).then_inc(S("dt_exp"), 1)
        act.wait_ge(S("dt_one_plus"), 1)
        act.activation(LN[:, :, :], U[:, :, :], ACT.Ln).then_inc(S("dt_ln"), 1)
        for k, dst in enumerate((m.EA, m.DD, m.CD)):
            act.wait_ge(S("dA_sums"), k + 1)
            act.activation(dst[:, :, :], b_sum[k][:, 0:Q * HEADS].rearrange("p (q h) -> p q h", h=HEADS), ACT.Exp)\
               .then_inc(S("decays"), 1)

    def pool(e, b, u, first, last):
        xb = tiles(m.X[:, bass.ds(b * N, N)])
        wait_apart(e, S("h_ready"), b * T + T, m.waited)
        e.tensor_tensor(xb, xb, m.BLIN[:, :].unsqueeze(1).broadcast_to([P, T, P]), ALU.add)

    return Extra(pe_end, act_end, dve_end, pool, pe=pe, dve=dve, dve_start=dve_start,
                 wait_ht_free=lambda act, b: wait(act, S("dt_product"), b - 1))


def mamba_norm(nc, m):
    normalise(nc, m, "mamba", mamba_steps)




def mamba(nc, m):
    with ExitStack() as stack:
        mem = Memory(nc, stack)
        S = mem.sem
        HB = [mem.sb(f"mb_ht{u}", P, N) for u in range(2)]
        CV = [mem.sb(f"mb_conv{u}", P, 3, N) for u in range(2)]
        XC = [mem.sb(f"mb_xbc{u}", P, 3, N) for u in range(2)]
        CT = [mem.sb(f"mb_ct{u}", STATE, N) for u in range(2)]
        ZS = [mem.sb(f"mb_z{u}", P, T, INNER) for u in range(2)]
        XH = [mem.sb(f"mb_xh{k}", P, 320) for k in range(2)]
        SR = [mem.sb(f"mb_seg_rhs{k}", P, HEADS, P) for k in range(2)]
        ES = [mem.sb(f"mb_seg_exp{k}", P, HEADS, P) for k in range(2)]
        CM = [mem.sb(f"mb_cb{k}", P, P) for k in range(2)]
        XDT = [mem.sb(f"mb_xdt{k}", P, INNER) for k in range(2)]
        XW = [mem.sb(f"mb_xw{k}", P, INNER) for k in range(2)]
        XD = [mem.sb(f"mb_xd{k}", P, INNER) for k in range(2)]
        SS = [mem.sb(f"mb_state{c}", STATE, INNER) for c in range(1, T)]
        Y = [mem.sb(f"mb_y{k}", P, INNER) for k in range(2)]
        YT = [mem.sb(f"mb_yt{k}", P, 2, P) for k in range(2)]
        SQ = mem.sb("mb_square", P, INNER)
        RS = [mem.sb(f"mb_rms{k}", P, 2) for k in range(2)]
        ST = mem.sb("mb_stats", P, T, 6)
        MVS = mem.sb("mb_mean_var", P, T, 2)
        b_pj = mem.banks("mb_b_proj", 2)
        b_x, = mem.banks("mb_b_x", 1)
        b_seg, = mem.banks("mb_b_seg", 1)
        b_cs, = mem.banks("mb_b_cs", 1)
        b_y, = mem.banks("mb_b_y", 1)
        b_yt, = mem.banks("mb_b_yt", 1)
        b_o, = mem.banks("mb_b_o", 1)

        def heads(ap, n=HEADS):
            return ap.rearrange("p (h d) -> p h d", h=n)

        def over_heads(ap, b, c, width=HD, parts=P):
            return ap[0:parts, bass.ds(b * T + c, 1), :].rearrange("p q h -> p (q h)").unsqueeze(2)\
                .broadcast_to([parts, HEADS, width])

        def after(b, u, c, chunks=1):
            return (b, u, c + chunks) if c + chunks < T else (b + 1, 1 - u, c + chunks - T)

        def before(b, u, c):
            return (b, u, c - 1) if c else (b - 1, 1 - u, T - 1)

        def slot(u, k):
            return (5 * u + k) % 2

        with nc.Block() as block:

            @block.sync
            def _(sp):
                def load(b, u):
                    wait_apart(sp, S("z_product"), 2 * (b - 1), m.waited)
                    sp.dma_start(HB[u][:, :], m.HT[:, bass.ds(b * N, N)]).then_inc(S(f"ht_loaded{u}"), 16)

                def body(b, u, first, last):
                    if not last:
                        load(b + 1, 1 - u)
                    wait_apart(sp, S("xbc_ready"), 3 * b + 3, m.waited)
                    wait_apart(sp, S("outputs"), T * (b - 1), m.waited)
                    sp.dma_start(CT[u][:, :], XC[u][STATE:2 * STATE, 2, :]).then_inc(S(f"c_moved{u}"), 16)

                load(0, 0)
                over_batches(sp, body)
                for u in range(2):
                    sp.wait_ge(S(f"c_moved{u}"), 16 * B // 2)
                    sp.wait_ge(S(f"ht_loaded{u}"), 16 * B // 2)

            @block.tensor
            def _(pe):
                def project(b, u, k):
                    if k == 0:
                        pe.wait_ge(S(f"ht_loaded{u}"), (b - u) * 8 + 16)
                    if k == 0:
                        wait(pe, S("z_ready"), 2 * b - 1)
                    elif k == 1:
                        wait(pe, S("z_ready"), 2 * b)
                    else:
                        pe.wait_ge(S("conv_ready"), 3 * b + k - 1)
                    bank = b_pj[slot(u, k)]
                    if k < 3:
                        pe.matmul(bank[:, :], m.WIN[:, 256 + 128 * k:384 + 128 * k], HB[u][:, :],
                                  start=True, stop=True).then_inc(S("xbc_product"), 1)
                    else:
                        for t in range(2):
                            c = 2 * (k - 3) + t
                            mm = pe.matmul(bank[:, INNER * t:INNER * t + INNER], HB[u][:, c * P:(c + 1) * P],
                                           m.WIN[:, 0:INNER], start=True, stop=True)
                        mm.then_inc(S("z_product"), 1)

                def scores(b, u, c):
                    k = c % 2
                    at = slice(c * P, (c + 1) * P)
                    if c == 0:
                        pe.wait_ge(S("xbc_ready"), 3 * b + 3)
                    wait(pe, S("xh_ready"), T * b + c)
                    for g in range(2):
                        pe.transpose(b_x[:, g * P:(g + 1) * P], XC[u][:, g, at], m.IDENT[:, :])
                    pe.transpose(b_x[:, 256:320], XC[u][0:STATE, 2, at], m.IDENT[0:STATE, 0:STATE])\
                      .then_inc(S("x_turned"), 1)
                    pe.wait_ge(S("seg_rhs"), T * b + c + 1)
                    wait(pe, S("seg_exp"), T * b + c)
                    pe.matmul(b_seg[:, :], m.GT[:, :], SR[k][:, :, :].rearrange("p h l -> p (h l)"),
                              start=True, stop=True).then_inc(S("seg_sums"), 1)
                    if c == 0:
                        pe.wait_ge(S(f"c_moved{u}"), (b - u) * 8 + 16)
                    wait(pe, S("x2"), T * b + c - 2)
                    wait(pe, S("cb_masked"), T * b + c)
                    pe.matmul(b_o[:, 256:384], XC[u][0:STATE, 2, at], CT[u][:, at], start=True, stop=True)\
                      .then_inc(S("cb_product"), 1)

                def outputs(b, u, c):
                    k = c % 2
                    q = T * b + c
                    pe.wait_ge(S("m_ready"), q + 1)
                    pe.wait_ge(S("x_scaled"), 3 * q + 2)
                    wait(pe, S("y_summed"), q)
                    for h in range(HEADS):
                        mm = pe.matmul(b_y[:, HD * h:HD * h + HD], ES[k][:, h, :], XDT[k][:, HD * h:HD * h + HD],
                                       start=True, stop=True)
                    if c:
                        pe.wait_ge(S("states_done"), q)
                        mm = pe.matmul(b_y[:, INNER:2 * INNER], CT[u][:, c * P:(c + 1) * P], SS[c - 1][:, :],
                                       start=True, stop=True)
                    mm.then_inc(S("outputs"), 1)
                    if c < T - 1:
                        wait(pe, S("states_done"), q)
                        pe.matmul(b_cs[0:STATE, 256:512], XH[k][:, 256:320], XW[k][:, :], start=True, stop=True)\
                          .then_inc(S("state_products"), 1)

                def turn_y(b, u, c):
                    k = c % 2
                    q = T * b + c
                    pe.wait_ge(S("y_ready"), q + 1)
                    wait(pe, S("yt_ready"), q)
                    for g in range(2):
                        mm = pe.transpose(b_yt[:, g * P:(g + 1) * P], Y[k][:, g * P:(g + 1) * P], m.IDENT[:, :])
                    mm.then_inc(S("y_turned"), 1)

                def finish(b, u, c):
                    k = c % 2
                    q = T * b + c
                    pe.wait_ge(S("yt_ready"), q + 1)
                    wait(pe, S("x2"), q)
                    pe.wait_ge(S("cb_masked"), min(q + 3, Q) if isinstance(q, int) else q + 3)
                    for g in range(2):
                        mm = pe.matmul(b_o[:, 0:P], YT[k][:, g, :], m.WF[:, g, :], start=(g == 0), stop=(g == 1))
                    mm.then_inc(S("out_product"), 1)

                for k in range(5):
                    project(0, 0, k)
                scores(0, 0, 0)

                def body(b, u, first, last):
                    for c in range(T):
                        if c < T - 1:
                            if not last:
                                project(b + 1, 1 - u, c)
                            scores(b, u, c + 1)
                        elif not last:
                            project(b + 1, 1 - u, 3)
                            project(b + 1, 1 - u, 4)
                            scores(b + 1, 1 - u, 0)
                        if not (first and c == 0):
                            turn_y(*before(b, u, c))
                        outputs(b, u, c)
                        if not (first and c == 0):
                            finish(*before(b, u, c))

                over_batches(pe, body)
                turn_y(B - 1, 1, T - 1)
                finish(B - 1, 1, T - 1)

            @block.scalar
            def _(act):
                def tap(b, u, g):
                    act.wait_ge(S("xbc_product"), 3 * b + g + 1)
                    wait(act, S("xbc_ready"), 3 * (b - 1))
                    act.activation(CV[u][:, g, :], b_pj[slot(u, g)][:, :], ACT.Identity, bias=m.CB[:, g:g + 1],
                                   scale=m.CW[:, g, 3:4]).then_inc(S("tap_ready"), 1)

                def gate(b, u, k):
                    act.wait_ge(S("z_product"), 2 * b + k + 1)
                    wait(act, S("y_ready"), T * (b - 1))
                    act.activation(ZS[u][:, 2 * k:2 * k + 2, :], b_pj[slot(u, 3 + k)][:, :].rearrange("p (t n) -> p t n", t=2),
                                   ACT.Silu).then_inc(S("z_ready"), 1)

                def silu(b, u, g):
                    act.wait_ge(S("conv_ready"), 3 * b + g + 1)
                    wait(act, S("outputs"), T * (b - 1))
                    act.activation(XC[u][:, g, :], CV[u][:, g, :], ACT.Silu).then_inc(S("xbc_ready"), 1)

                def scores(b, u, c):
                    k = c % 2
                    q = T * b + c
                    act.wait_ge(S("x_turned"), q + 1)
                    wait(act, S("x_scaled"), 3 * (q - 1))
                    wait(act, S("outputs"), q - 1)
                    wait(act, S("state_products"), 3 * b + (c - 1 if c else 0))
                    act.activation(XH[k][:, :], b_x[:, 0:320], ACT.Copy).then_inc(S("xh_ready"), 1)
                    act.wait_ge(S("seg_sums"), q + 1)
                    act.activation(ES[k][:, :, :], b_seg[:, :].rearrange("p (h l) -> p h l", h=HEADS), ACT.Exp)\
                       .then_inc(S("seg_exp"), 1)

                def finish(b, u, c):
                    k = c % 2
                    q = T * b + c
                    act.wait_ge(S("y_ready"), q + 1)
                    wait(act, S("rms_ready"), q - 1)
                    wait(act, S("squared"), q)
                    act.activation(SQ[:, :], Y[k][:, :], ACT.Square, accum_out=RS[k][:, 0:1]).then_inc(S("squared"), 1)
                    act.wait_ge(S("y_turned"), q + 1)
                    wait(act, S("out_product"), q - 1)
                    act.activation(YT[k][:, :, :], b_yt[:, 0:256].rearrange("p (g l) -> p g l", g=2), ACT.Copy)\
                       .then_inc(S("yt_ready"), 1)

                for g in range(3):
                    tap(0, 0, g)
                for k in range(2):
                    gate(0, 0, k)
                for g in range(3):
                    silu(0, 0, g)
                scores(0, 0, 0)

                def body(b, u, first, last):
                    for c in range(T):
                        if c < T - 1:
                            if not last:
                                tap(b + 1, 1 - u, c)
                            scores(b, u, c + 1)
                        elif not last:
                            for g in range(3):
                                silu(b + 1, 1 - u, g)
                            for k in range(2):
                                gate(b + 1, 1 - u, k)
                            scores(b + 1, 1 - u, 0)
                        if c:
                            finish(b, u, c - 1)
                        elif not first:
                            finish(b - 1, 1 - u, T - 1)

                over_batches(act, body)
                finish(B - 1, 1, T - 1)

            @block.gpsimd
            def _(pool):
                def rhs(b, u, c):
                    k = c % 2
                    wait_apart(pool, S("seg_sums"), T * b + c - 1, m.waited)
                    pool.tensor_tensor(SR[k][:, :, :], m.LE[:, :].unsqueeze(1).broadcast_to([P, HEADS, P]),
                                       over_heads(m.DA, b, c, P), ALU.mult).then_inc(S("seg_rhs"), 1)

                def scale(b, u, c):
                    k = c % 2
                    q = T * b + c
                    wait(pool, S("outputs"), q - 1)
                    wait(pool, S("state_products"), 3 * b + (c - 1 if c else 0))
                    wait(pool, S("y_ready"), q - 1)
                    wait_apart(pool, S("xh_ready"), q + 1, m.waited)
                    xh = heads(XH[k][:, 0:INNER])
                    pool.tensor_tensor(heads(XDT[k][:, :]), xh, over_heads(m.DTS, b, c), ALU.mult).then_inc(S("x_scaled"), 1)
                    pool.tensor_tensor(heads(XW[k][:, :]), xh, over_heads(m.DD, b, c), ALU.mult).then_inc(S("x_scaled"), 1)
                    pool.tensor_tensor(heads(XD[k][:, :]), xh, m.DH[:, :].unsqueeze(2).broadcast_to([P, HEADS, HD]),
                                       ALU.mult).then_inc(S("x_scaled"), 1)

                def rms(b, u, c):
                    k = c % 2
                    q = T * b + c
                    pool.wait_ge(S("squared"), q + 1)
                    wait_apart(pool, S("x2"), q - 1, m.waited)
                    pool.tensor_scalar(RS[k][:, 1:2], RS[k][:, 0:1], 1.0 / INNER, LN_EPS, ALU.mult, ALU.add)\
                        .then_inc(S("mean_square"), 1)
                    pool.wait_ge(S("mean_square"), q + 1)
                    pool.tensor_tensor(RS[k][:, 1:2], RS[k][:, 1:2], m.MHALF[:, 0:1], ALU.pow).then_inc(S("rms_ready"), 1)

                rhs(0, 0, 0)
                rhs(0, 0, 1)
                scale(0, 0, 0)

                def body(b, u, first, last):
                    for c in range(T):
                        if not (last and c + 2 >= T):
                            rhs(*after(b, u, c, 2))
                        if not (last and c + 1 >= T):
                            scale(*after(b, u, c))
                        if not (first and c == 0):
                            rms(*before(b, u, c))
                        if c == 0 and two_before(b):
                            make_rstd(pool, m, S("stats_kept"), b - 2)

                over_batches(pool, body)
                rms(B - 1, 1, T - 1)
                make_rstd(pool, m, S("stats_kept"), B - 2)
                make_rstd(pool, m, S("stats_kept"), B - 1)

            @block.vector
            def _(dve):
                def tap(b, u, g, back):
                    if back == 1:
                        dve.wait_ge(S("tap_ready"), 3 * b + g + 1)
                    else:
                        dve.wait_ge(S("taps"), (3 * b + g) * 2 + back - 1)
                    dst = CV[u][:, g, back:N]
                    op = dve.scalar_tensor_tensor(out=dst, in0=b_pj[slot(u, g)][:, 0:N - back],
                                                  scalar=m.CW[:, g, 3 - back:4 - back], in1=dst,
                                                  op0=ALU.mult, op1=ALU.add)
                    op.then_inc(S("taps") if back < TAPS - 1 else S("conv_ready"), 1)

                def mask_cb(b, u, c):
                    q = T * b + c
                    dve.wait_ge(S("cb_product"), q + 1)
                    wait(dve, S("m_ready"), q - 1)
                    dve.tensor_tensor(CM[c % 2][:, :], b_o[:, 256:384], m.LE[:, :], ALU.mult).then_inc(S("cb_masked"), 1)

                def weigh_cb(b, u, c):
                    k = c % 2
                    q = T * b + c
                    dve.wait_ge(S("cb_masked"), q + 1)
                    dve.wait_ge(S("seg_exp"), q + 1)
                    dve.tensor_tensor(ES[k][:, :, :], ES[k][:, :, :], CM[k][:, :].unsqueeze(1).broadcast_to([P, HEADS, P]),
                                      ALU.mult).then_inc(S("m_ready"), 1)

                def decay(b, c):
                    wait_apart(dve, S("states_done"), T * b + c, m.waited)
                    dve.tensor_tensor(heads(SS[c][:, :]), heads(SS[c - 1][:, :]), over_heads(m.CD, b, c, parts=STATE),
                                      ALU.mult).then_inc(S("decayed"), 1)

                def state(b, c):
                    if c == T - 1:
                        dve.sem_inc(S("states_done"), 1)
                        return
                    dve.wait_ge(S("state_products"), 3 * b + c + 1)
                    new = SS[c][:, :]
                    if c == 0:
                        wait(dve, S("outputs"), T * b - 2)
                        dve.tensor_copy(new, b_cs[0:STATE, 256:512]).then_inc(S("states_done"), 1)
                        return
                    dve.wait_ge(S("decayed"), 2 * b + c)
                    dve.tensor_tensor(new, new, b_cs[0:STATE, 256:512], ALU.add).then_inc(S("states_done"), 1)

                def add_off(b, u, c):
                    q = T * b + c
                    k = c % 2
                    wait_apart(dve, S("outputs"), q + 1, m.waited)
                    wait_apart(dve, S("x_scaled"), 3 * q + 3, m.waited)
                    for h in range(HEADS):
                        at = slice(HD * h, HD * h + HD)
                        dve.scalar_tensor_tensor(out=XD[k][:, at], in0=b_y[:, INNER + HD * h:INNER + HD * h + HD],
                                                 scalar=m.EA[:, bass.ds(q, 1), h], in1=XD[k][:, at], op0=ALU.mult,
                                                 op1=ALU.add).then_inc(S("off_added"), 1)

                def add_diagonal(b, u, c):
                    k = c % 2
                    q = T * b + c
                    dve.wait_ge(S("outputs"), q + 1)
                    dve.wait_ge(S("x_scaled"), 3 * q + 3)
                    if c:
                        dve.wait_ge(S("off_added"), HEADS * (3 * b + c))
                    wait(dve, S("squared"), q - 1)
                    wait(dve, S("y_turned"), q - 1)
                    dve.tensor_tensor(Y[k][:, :], b_y[:, 0:INNER], XD[k][:, :], ALU.add).then_inc(S("y_summed"), 1)

                def gate(b, u, c):
                    q = T * b + c
                    y = Y[c % 2][:, :]
                    dve.wait_ge(S("y_summed"), q + 1)
                    if c % 2 == 0:
                        dve.wait_ge(S("z_ready"), 2 * b + c // 2 + 1)
                    dve.tensor_tensor(y, y, ZS[u][:, c, :], ALU.mult).then_inc(S("y_ready"), 1)

                def finish(b, u, c):
                    q = T * b + c
                    dve.wait_ge(S("out_product"), q + 1)
                    dve.wait_ge(S("rms_ready"), q + 1)
                    xq = m.X[:, bass.ds(q * P, P)]
                    dve.scalar_tensor_tensor(out=xq, in0=b_o[:, 0:P], scalar=RS[c % 2][:, 1:2], in1=xq, op0=ALU.mult,
                                             op1=ALU.add).then_inc(S("x2"), 1)

                def stats(b):
                    wait_apart(dve, S("x2"), T * b + T, m.waited)
                    wait_apart(dve, S("stats2_known"), T * b, m.waited)
                    for c in range(T):
                        dve.bn_stats(ST[:, c, :], m.X[:, bass.ds((b * T + c) * P, P)]).then_inc(S("stats2"), 1)

                def means(b):
                    wait_apart(dve, S("stats2"), T * b + T, m.waited)
                    wait_apart(dve, S("stats_kept"), b, m.waited)
                    for c in range(T):
                        dve.bn_aggr(MVS[:, c, :], ST[:, c, :]).then_inc(S("stats2_known"), 1)

                def keep(b):
                    dve.wait_ge(S("stats2_known"), T * b + T)
                    keep_stats(dve, m, MVS, b, S("stats_kept"))

                for g in range(3):
                    for back in range(1, TAPS):
                        tap(0, 0, g, back)
                mask_cb(0, 0, 0)
                weigh_cb(0, 0, 0)

                def body(b, u, first, last):
                    for c in range(T):
                        more = not (last and c == T - 1)
                        taps = c < T - 1 and not last
                        if more:
                            mask_cb(*after(b, u, c))
                        if taps:
                            tap(b + 1, 1 - u, c, 1)
                        if c == T - 1 and not first:
                            stats(b - 1)
                        if more:
                            weigh_cb(*after(b, u, c))
                        if taps:
                            tap(b + 1, 1 - u, c, 2)
                        if c in (1, 2):
                            decay(b, c)
                        if c == T - 1 and not first:
                            means(b - 1)
                        if taps:
                            tap(b + 1, 1 - u, c, 3)
                        state(b, c)
                        if c:
                            add_off(b, u, c)
                        if not (first and c == 0):
                            finish(*before(b, u, c))
                        add_diagonal(b, u, c)
                        if c == T - 1 and not first:
                            keep(b - 1)
                        gate(b, u, c)

                over_batches(dve, body)
                finish(B - 1, 1, T - 1)
                stats(B - 1)
                means(B - 1)
                keep(B - 1)
        retire(nc, mem)




def ode(nc, m):
    with ExitStack() as stack:
        mem = Memory(nc, stack)
        S = mem.sem

        def halves(name, *shape):
            return Halves(mem, name, *shape)

        L_POWERS = (m.LT, m.L2T, m.L3T, m.L6T)
        LP = [halves(f"ode_l_power{k}", P, T, N) for k in range(4)]
        ES = halves("ode_e", P, 9, 128)
        E4 = [e.rearrange("p (q k) e -> p q k e", k=3) for e in ES.at(slice(None), slice(None))]
        HTS = mem.sb("ode_h8_turned", P, N)
        V = mem.sb("ode_ones", P, T, 3)
        VT = mem.sb("ode_ones_turned", 3, N)
        GC = mem.sb("ode_const_g", P, T, 2 * P)
        GB = mem.sb("ode_const", P, N)
        H = [mem.sb(f"ode_h{u}", P, T, P) for u in range(2)]
        HS = [halves(f"ode_h{u}", P, T, P) for u in range(2)]
        ZS = halves("ode_z", P, 3, N)
        GS = halves("ode_g", P, T, 2 * P)
        ST = mem.sb("ode_stats", P, T, 6)
        MVS = mem.sb("ode_mean_var", P, T, 2)
        b_x, = mem.banks("ode_b_x", 1)
        b_z = mem.banks("ode_b_z", 2)
        b_g = mem.banks("ode_b_g", 2)
        b_ht, = mem.banks("ode_b_h8_turned", 1)
        b_h = mem.banks("ode_b_h8", 2)

        with nc.Block() as block:

            @block.gpsimd
            def _(pool):
                pool.memset(V[:, :, :], 1.0).then_inc(S("ones_ready"), 1)

                def body(b, u, first, last):
                    pool.wait_ge(S("h_high"), b + 1)
                    wait(pool, S("z_product"), 3 * (b - 1))
                    pool.tensor_tensor(HS[u].low[:, :, :], H[u][:, :, :], HS[u].seen[:, :, :], ALU.subtract)\
                        .then_inc(S("h_low"), 1)
                    wait_apart(pool, S("h_ready"), b * T + T, m.waited)
                    if first:
                        pool.wait_ge(S("const_known"), 1)
                    xb = m.X[:, bass.ds(b * N, N)]
                    pool.tensor_tensor(xb, xb, GB[:, :], ALU.add).then_inc(S("const_added"), 1)
                    if two_before(b):
                        make_rstd(pool, m, S("stats_kept"), b - 2)

                over_batches(pool, body)
                make_rstd(pool, m, S("stats_kept"), B - 2)
                make_rstd(pool, m, S("stats_kept"), B - 1)

            @block.vector
            def _(dve):
                def norm(b, u):
                    wait(dve, S("z_product"), 3 * (b - 1))
                    wait(dve, S("h_high"), b - 1)
                    wait(dve, S("h_low"), b - 1)
                    for t in range(T):
                        q = b * T + t
                        dve.tensor_scalar(H[u][:, t, :], m.X[:, bass.ds(q * P, P)], m.MV[:, bass.ds(q, 1), 0],
                                          m.RSTD[:, bass.ds(q, 1)], ALU.subtract, ALU.mult).then_inc(S("h_ready"), 1)

                def z_low(b, u):
                    wait(dve, S("h_begun"), b)
                    for k, bank in enumerate((b_x, *b_z)):
                        dve.wait_ge(S("z_high"), 3 * b + k + 1)
                        dve.tensor_tensor(ZS.low[:, k, :], bank[:, :], ZS.seen[:, k, :], ALU.subtract)\
                           .then_inc(S("z_low"), 1)

                def g_low(b, u):
                    wait(dve, S("h8"), b)
                    for k in range(2):
                        dve.wait_ge(S("g_high"), 2 * b + k + 1)
                        dve.tensor_tensor(GS.low[:, 2 * k:2 * k + 2, :], tiles(b_g[k][:, :], 2),
                                          GS.seen[:, 2 * k:2 * k + 2, :], ALU.subtract).then_inc(S("g_low"), 1)

                def update(b, u):
                    xb = m.X[:, bass.ds(b * N, N)]
                    dve.wait_ge(S("h8_turned"), b + 1)
                    dve.wait_ge(S("const_added"), b + 1)
                    dve.tensor_tensor(xb, b_h[u][:, :], xb, ALU.add).then_inc(S("x3"), 1)
                    wait_apart(dve, S("x3"), b + 1, m.waited)
                    wait_apart(dve, S("stats_kept"), b, m.waited)
                    for t in range(T):
                        dve.bn_stats(ST[:, t, :], m.X[:, bass.ds((b * T + t) * P, P)]).then_inc(S("stats3"), 1)
                    wait_apart(dve, S("stats3"), b * T + T, m.waited)
                    for t in range(T):
                        dve.bn_aggr(MVS[:, t, :], ST[:, t, :]).then_inc(S("stats3_known"), 1)
                    dve.wait_ge(S("stats3_known"), b * T + T)
                    keep_stats(dve, m, MVS, b, S("stats_kept"))

                norm(0, 0)
                norm(1, 1)
                for k in range(4):
                    for t in range(T):
                        dve.wait_ge(S("const_high"), T * k + t + 1)
                        dve.tensor_tensor(LP[k].low[:, t, :], L_POWERS[k][:, t, :], LP[k].seen[:, t, :], ALU.subtract)\
                           .then_inc(S("const_low"), 1)
                dve.wait_ge(S("const_high"), 4 * T + 1)
                dve.tensor_tensor(ES.low[:, :, :], m.E[:, :, :], ES.seen[:, :, :], ALU.subtract).then_inc(S("const_low"), 1)
                z_low(0, 0)
                dve.wait_ge(S("const_product"), 1)
                dve.tensor_copy(GB[:, :], b_ht[:, :]).then_inc(S("const_known"), 1)
                g_low(0, 0)

                def body(b, u, first, one_ahead, two_ahead):
                    if not first:
                        update(b - 1, 1 - u)
                    if two_ahead:
                        norm(b + 2, u)
                    if one_ahead:
                        z_low(b + 1, 1 - u)
                        g_low(b + 1, 1 - u)

                turns(dve, body)
                update(B - 1, 1)

            @block.scalar
            def _(act):
                def h_high(b, u):
                    act.wait_ge(S("h_ready"), b * T + T)
                    wait(act, S("z_product"), 3 * (b - 1))
                    act.activation(HS[u].high[:, :, :], H[u][:, :, :], ACT.Copy).then_inc(S("h_high"), 1)

                def z_high(b, u):
                    wait(act, S("h_begun"), b)
                    for k, bank in enumerate((b_x, *b_z)):
                        act.wait_ge(S("z_product"), 3 * b + k + 1)
                        act.activation(ZS.high[:, k, :], bank[:, :], ACT.Copy).then_inc(S("z_high"), 1)

                def g_high(b, u):
                    wait(act, S("h8"), b)
                    for k in range(2):
                        act.wait_ge(S("g_product"), 2 * b + k + 1)
                        act.activation(GS.high[:, 2 * k:2 * k + 2, :], tiles(b_g[k][:, :], 2), ACT.Copy)                           .then_inc(S("g_high"), 1)

                def keep_h8(b):
                    act.wait_ge(S("h8"), b + 1)
                    wait(act, S("h8_turned"), b)
                    act.activation(HTS[:, :], b_ht[:, :], ACT.Copy).then_inc(S("h8_kept"), 1)

                for k in range(4):
                    for t in range(T):
                        act.activation(LP[k].high[:, t, :], L_POWERS[k][:, t, :], ACT.Copy).then_inc(S("const_high"), 1)
                act.activation(ES.high[:, :, :], m.E[:, :, :], ACT.Copy).then_inc(S("const_high"), 1)
                h_high(0, 0)
                act.wait_ge(S("ones_product"), 1)
                act.activation(V[:, :, 1:3], b_h[0][:, 0:2 * T].rearrange("p (t k) -> p t k", t=T), ACT.Copy)\
                   .then_inc(S("ones_kept"), 1)
                h_high(1, 1)
                z_high(0, 0)
                act.wait_ge(S("ones_turned"), 1)
                act.activation(VT[:, :], b_h[1][0:3, :], ACT.Copy).then_inc(S("ones_kept"), 1)
                for k in range(2):
                    act.wait_ge(S("const_g_product"), k + 1)
                    act.activation(GC[:, 2 * k:2 * k + 2, :], tiles(b_h[k][:, :], 2), ACT.Copy).then_inc(S("const_g"), 1)
                g_high(0, 0)

                def body(b, u, first, one_ahead, two_ahead):
                    if one_ahead:
                        z_high(b + 1, 1 - u)
                    if two_ahead:
                        h_high(b + 2, u)
                    keep_h8(b)
                    if one_ahead:
                        g_high(b + 1, 1 - u)

                turns(act, body)

            @block.tensor
            def _(pe):
                def z(b, u):
                    pe.wait_ge(S("h_ready"), b * T + T)
                    wait(pe, S("z_low"), 3 * b - 2)
                    for t in range(T):
                        mm = pe.transpose(b_x[:, t * P:(t + 1) * P], H[u][:, t, :], m.IDENT[:, :])
                    mm.then_inc(S("z_product"), 1)
                    pe.wait_ge(S("h_high"), b + 1)
                    pe.wait_ge(S("h_low"), b + 1)
                    for k in range(2):
                        wait(pe, S("z_low"), 3 * b - 1 + k)
                        for s in range(T):
                            mm = in_halves(pe, b_z[k][:, :], HS[u].at(s, slice(None)), LP[k].at(s, slice(None)), s == 0, s == T - 1)
                        mm.then_inc(S("z_product"), 1)

                def g(b, u):
                    pe.wait_ge(S("z_low"), 3 * b + 3)
                    for t in range(T):
                        if t % 2 == 0:
                            wait(pe, S("g_low"), 2 * b - 1 + t // 2)
                        at = slice(t * P, (t + 1) * P)
                        for k in range(3):
                            mm = in_halves(pe, b_g[t // 2][:, 256 * (t % 2):256 * (t % 2) + 256], ZS.at(k, at),
                                           [e[:, 1:3, k, :] for e in E4], t % 2 == 0 and k == 0, t % 2 == 1 and k == 2)
                        if t % 2:
                            mm.then_inc(S("g_product"), 1)

                def h_from_z(b):
                    wait(pe, S("h8_kept"), b)
                    for k in range(3):
                        mm = in_halves(pe, b_ht[:, :], ES.at(k, slice(None)), ZS.at(k, slice(None)), k == 0, False)
                    mm.then_inc(S("h_begun"), 1)

                def h_from_g(b, q):
                    if q == 1:
                        pe.wait_ge(S("g_low"), 2 * b + 2)
                    for s in range(T):
                        mm = in_halves(pe, b_ht[:, :], GS.at(s, slice((q - 1) * P, q * P)), LP[1 + q].at(s, slice(None)),
                                       False, q == 2 and s == T - 1)
                    if q == 2:
                        mm.then_inc(S("h8"), 1)

                def turn_back(b, u):
                    pe.wait_ge(S("h8_kept"), b + 1)
                    wait(pe, S("x3"), b - 1)
                    for t in range(T):
                        mm = pe.transpose(b_h[u][:, t * P:(t + 1) * P], HTS[:, t * P:(t + 1) * P], m.IDENT[:, :])
                    mm.then_inc(S("h8_turned"), 1)

                pe.wait_ge(S("ones_ready"), 1)
                for t in range(T):
                    for k, mat in enumerate((m.LT, m.L2T)):
                        for s in range(T):
                            mm = pe.matmul(b_h[0][:, 2 * t + k:2 * t + k + 1], mat[:, s, t * P:(t + 1) * P], V[:, s, 0:1],
                                           start=(s == 0), stop=(s == T - 1))
                mm.then_inc(S("ones_product"), 1)
                pe.wait_ge(S("const_low"), 4 * T + 1)
                z(0, 0)
                pe.wait_ge(S("ones_kept"), 1)
                for t in range(T):
                    mm = pe.transpose(b_h[1][0:3, t * P:(t + 1) * P], V[:, t, :], m.IDENT[:, :])
                mm.then_inc(S("ones_turned"), 1)
                pe.wait_ge(S("ones_kept"), 2)
                for t in range(T):
                    mm = pe.matmul(b_h[t // 2][:, 256 * (t % 2):256 * (t % 2) + 256], VT[:, t * P:(t + 1) * P],
                                   m.CR[:, P:3 * P], start=True, stop=True)
                    if t % 2:
                        mm.then_inc(S("const_g_product"), 1)
                g(0, 0)
                pe.wait_ge(S("const_g"), 2)
                for t in range(T):
                    at = slice(t * P, (t + 1) * P)
                    pe.matmul(b_ht[:, at], VT[:, at], m.CR[:, 0:P], start=True, stop=False)
                    for k, mat in enumerate((m.L3T, m.L6T)):
                        for s in range(T):
                            mm = pe.matmul(b_ht[:, at], mat[:, s, at], GC[:, s, k * P:(k + 1) * P],
                                           start=False, stop=(k == 1 and s == T - 1))
                mm.then_inc(S("const_product"), 1)
                pe.wait_ge(S("const_known"), 1)

                def body(b, u, first, last):
                    h_from_z(b)
                    h_from_g(b, 1)
                    if not last:
                        z(b + 1, 1 - u)
                    h_from_g(b, 2)
                    if not last:
                        g(b + 1, 1 - u)
                    turn_back(b, u)

                over_batches(pe, body)
        retire(nc, mem)




def router(nc, m, mem, H, HTS):
    S = mem.sem
    FE = mem.sb("feat_sum", P, T, P)
    FT = mem.sb("feat_t", P, N)
    LG = mem.sb("logits", P, T, EXPERTS)
    CO = mem.sb("router_cols", P, 2, T)
    W8 = mem.sb("router_rows", EXPERTS, N)
    b_f = mem.banks("rt_b", 6)
    per_expert = [P, T, EXPERTS]

    def pool(e, b, u, first, last):
        e.wait_ge(S("h_ready"), b * T + T)
        if first:
            e.tensor_copy(FE[:, :, :], H[u][:, :, :]).then_inc(S("feat_added"), 1)
        else:
            e.wait_ge(S("feat_added"), b)
            e.tensor_tensor(FE[:, :, :], FE[:, :, :], H[u][:, :, :], ALU.add).then_inc(S("feat_added"), 1)

    def pe_start(pe):
        for k in range(4):
            for e in range(4):
                mm = pe.matmul(b_f[2 + k][:, e * P:(e + 1) * P], m.BNA[:, 4 * k + e:4 * k + e + 1].broadcast_to([P, P]),
                               m.IDENT[:, :], start=True, stop=True)
            mm.then_inc(S("scales_wide"), 1)

    def pe_end(pe):
        pe.wait_ge(S("feat_added"), B)
        for t in range(T):
            mm = pe.transpose(b_f[0][:, t * P:(t + 1) * P], FE[:, t, :], m.IDENT[:, :])
        mm.then_inc(S("feat_turned"), 1)
        pe.wait_ge(S("feat_ready"), 1)
        for t in range(T):
            mm = pe.matmul(b_f[1][:, EXPERTS * t:EXPERTS * (t + 1)], FT[:, t * P:(t + 1) * P], m.WR[:, :],
                           start=True, stop=True)
        mm.then_inc(S("logits"), 1)
        pe.wait_ge(S("router_ready"), 1)
        for t in range(T):
            mm = pe.transpose(b_f[0][0:EXPERTS, t * P:(t + 1) * P], LG[:, t, :], m.IDENT[:, :])
        mm.then_inc(S("router_turned"), 1)
        pe.wait_ge(S("scaled"), 4)
        for e in range(EXPERTS):
            k = e % 4
            wait(pe, S("wide_copied"), e - 3)
            for t in range(T):
                mm = pe.matmul(b_f[2 + k][:, t * P:(t + 1) * P], LG[:, t, e:e + 1].broadcast_to([P, P]), m.IDENT[:, :],
                               start=True, stop=True)
            mm.then_inc(S("wide"), 1)
        pe.wait_ge(S("router_rows"), 1)
        for t in range(T):
            mm = pe.matmul(b_f[1][:, t * P:(t + 1) * P], W8[:, t * P:(t + 1) * P], m.BO[:, :], start=True, stop=True)
        mm.then_inc(S("out_bias"), 1)

    def act_end(act):
        act.wait_ge(S("feat_turned"), 1)
        act.activation(FT[:, :], b_f[0][:, :], ACT.Copy, scale=1.0 / B).then_inc(S("feat_ready"), 1)
        act.wait_ge(S("logits_shifted"), 1)
        act.activation(LG[:, :, :], LG[:, :, :], ACT.Exp).then_inc(S("router_exp"), 1)
        for e in range(EXPERTS):
            act.wait_ge(S("wide"), e + 1)
            act.activation(m.RW[:, e, :], b_f[2 + e % 4][:, :], ACT.Copy).then_inc(S("wide_copied"), 1)
            if e < 3:
                act.wait_ge(S("scaled"), 4)
                w = (m.W1, m.W2, m.W3)[e]
                act.activation(m.WS[e].high[:, :, :], w[:, :, :], ACT.Copy).then_inc(S("weights_high"), 1)

    def dve_start(dve):
        for k in range(4):
            w = (m.W1, m.W2)[k // 2][:, 4 * (k % 2):4 * (k % 2) + 4, :]
            dve.wait_ge(S("scales_wide"), k + 1)
            dve.tensor_tensor(w, w, tiles(b_f[2 + k][:, :]), ALU.mult).then_inc(S("scaled"), 1)

    def dve_end(e):
        e.wait_ge(S("logits"), 1)
        e.tensor_tensor(LG[:, :, :], b_f[1][:, 0:T * EXPERTS].rearrange("p (t e) -> p t e", t=T),
                        m.BR[:, :].unsqueeze(1).broadcast_to(per_expert), ALU.add).then_inc(S("softmax"), 1)
        e.wait_ge(S("softmax"), 1)
        e.tensor_reduce(CO[:, 0, :], LG[:, :, :], mybir.AxisListType.X, ALU.max).then_inc(S("softmax"), 1)
        e.wait_ge(S("softmax"), 2)
        e.tensor_tensor(LG[:, :, :], LG[:, :, :], CO[:, 0, :].unsqueeze(2).broadcast_to(per_expert), ALU.subtract)\
         .then_inc(S("logits_shifted"), 1)
        e.wait_ge(S("router_exp"), 1)
        e.tensor_reduce(CO[:, 0, :], LG[:, :, :], mybir.AxisListType.X, ALU.add).then_inc(S("softmax"), 1)
        e.wait_ge(S("softmax"), 3)
        e.reciprocal(CO[:, 1, :], CO[:, 0, :]).then_inc(S("softmax"), 1)
        e.wait_ge(S("softmax"), 4)
        e.tensor_tensor(LG[:, :, :], LG[:, :, :], CO[:, 1, :].unsqueeze(2).broadcast_to(per_expert), ALU.mult)\
         .then_inc(S("router_ready"), 1)
        e.wait_ge(S("router_turned"), 1)
        e.tensor_copy(W8[:, :], b_f[0][0:EXPERTS, :]).then_inc(S("router_rows"), 1)
        for k, w in enumerate((m.W1, m.W2, m.W3)):
            e.wait_ge(S("weights_high"), k + 1)
            e.tensor_tensor(m.WS[k].low[:, :, :], w[:, :, :], m.WS[k].seen[:, :, :], ALU.subtract)
        e.wait_ge(S("out_bias"), 1)
        e.tensor_copy(m.YB[:, :], b_f[1][:, :])

    return Extra(pe_end, act_end, dve_end, pool, wait_h_free=lambda dve, b: wait(dve, S("feat_added"), b - 1),
                 dve_start=dve_start, pe_start=pe_start)


def experts(nc, m, out):
    with ExitStack() as stack:
        mem = Memory(nc, stack)
        m.RW = mem.sb("router_wide", P, EXPERTS, N)
        m.YB = mem.sb("expert_bias", P, N)
        WS = m.WS = [Halves(mem, f"ex_w{k}", P, EXPERTS, P) for k in range(3)]
        normalise(nc, m, "moe", router)
        S = mem.sem
        HB = [mem.sb(f"ex_ht{u}", P, N) for u in range(2)]
        HS = [Halves(mem, f"ex_ht{u}", P, N) for u in range(2)]
        R1 = [mem.sb(f"ex_r1_{k}", P, N) for k in range(4)]
        H1 = [Halves(mem, f"ex_h1_{k}", P, N) for k in range(4)]
        R2 = [mem.sb(f"ex_r2_{k}", P, N) for k in range(2)]
        HW = [mem.sb(f"ex_hw_{k}", P, N) for k in range(2)]
        HWS = [Halves(mem, f"ex_hw_{k}", P, N) for k in range(4)]
        YT = mem.sb("ex_y_turned", P, N)
        O = [mem.sb(f"ex_out{u}", P, N) for u in range(2)]
        b_1 = mem.banks("ex_b_1", 2)
        b_2 = mem.banks("ex_b_2", 2)
        b_yt = mem.banks("ex_b_y_turned", 2)
        b_y = mem.banks("ex_b_y", 2)
        E = EXPERTS
        every = slice(None)

        def ahead(b, u, e):
            return (b, u, e + 2) if e < E - 2 else (b + 1, 1 - u, e + 2 - E)

        def behind(b, u, e):
            return (b, u, e - 2) if e >= 2 else (b - 1, 1 - u, e - 2 + E)

        with nc.Block() as block:

            @block.sync
            def _(sp):
                def load(b, u):
                    wait_apart(sp, S("ht_high"), b - 1, m.waited)
                    wait_apart(sp, S("ht_low"), b - 1, m.waited)
                    sp.dma_start(HB[u][:, :], m.HT[:, bass.ds(b * N, N)]).then_inc(S(f"ht_loaded{u}"), 16)

                def body(b, u, first, one_ahead, two_ahead):
                    if two_ahead:
                        load(b + 2, u)
                    wait_apart(sp, S("x4"), b + 1, m.waited)
                    sp.dma_start(out[bass.ds(b, 1)].rearrange("o (t p) d -> p (o t) d", p=P), tiles(O[u][:, :]))\
                      .then_inc(S(f"stored{u}"), 16)

                load(0, 0)
                load(1, 1)
                turns(sp, body)
                for u in range(2):
                    sp.wait_ge(S(f"stored{u}"), 16 * B // 2)
                    sp.wait_ge(S(f"ht_loaded{u}"), 16 * B // 2)

            @block.gpsimd
            def _(pool):
                def ht_low(b, u):
                    pool.wait_ge(S("ht_high"), b + 1)
                    wait(pool, S("product1"), E * (b - 1))
                    pool.tensor_tensor(HS[u].low[:, :], HB[u][:, :], HS[u].seen[:, :], ALU.subtract)\
                        .then_inc(S("ht_low"), 1)

                def weigh(b, u, e):
                    pool.wait_ge(S("relu2"), E * b + e + 1)
                    wait(pool, S("hw_low"), E * b + e - 1)
                    pool.tensor_tensor(HW[e % 2][:, :], R2[e % 2][:, :], m.RW[:, e, :], ALU.mult).then_inc(S("hw_full"), 1)

                ht_low(0, 0)

                def body(b, u, first, last):
                    for e in range(E):
                        if e == 1:
                            xb = m.X[:, bass.ds(b * N, N)]
                            pool.tensor_tensor(xb, xb, m.YB[:, :], ALU.add).then_inc(S("bias_added"), 1)
                        if e == 4 and not last:
                            ht_low(b + 1, 1 - u)
                        weigh(b, u, e)

                over_batches(pool, body)

            @block.tensor
            def _(pe):
                def layer1(b, u, e):
                    if e == 0:
                        pe.wait_ge(S("ht_high"), b + 1)
                        pe.wait_ge(S("ht_low"), b + 1)
                    wait(pe, S("relu1"), E * b + e - 1)
                    in_halves(pe, b_1[e % 2][:, :], WS[0].at(e, every), HS[u].at(every), True, True)\
                        .then_inc(S("product1"), 1)

                def layer2(b, u, e):
                    pe.wait_ge(S("h1_high"), E * b + e + 1)
                    pe.wait_ge(S("h1_low"), E * b + e + 1)
                    wait(pe, S("relu2"), E * b + e - 1)
                    in_halves(pe, b_2[e % 2][:, :], WS[1].at(e, every), H1[e % 4].at(every), True, True)\
                        .then_inc(S("product2"), 1)

                def layer3(b, u, e):
                    pe.wait_ge(S("hw_low"), E * b + e + 1)
                    if e == 0:
                        wait(pe, S("y_kept"), b - 1)
                    in_halves(pe, b_yt[u][:, :], WS[2].at(e, every), HWS[e % 4].at(every), e == 0, e == E - 1)\
                        .then_inc(S("product3"), 1)

                def turn_back(b, u):
                    pe.wait_ge(S("y_kept"), b + 1)
                    wait(pe, S("x4"), b - 1)
                    for t in range(T):
                        mm = pe.transpose(b_y[u][:, t * P:(t + 1) * P], YT[:, t * P:(t + 1) * P], m.IDENT[:, :])
                    mm.then_inc(S("y_turned"), 1)

                layer1(0, 0, 0)
                layer1(0, 0, 1)

                def body(b, u, first, last):
                    for e in range(E):
                        if not (last and e >= E - 2):
                            layer1(*ahead(b, u, e))
                        layer2(b, u, e)
                        if not (first and e < 2):
                            layer3(*behind(b, u, e))
                        if e == 3 and not first:
                            turn_back(b - 1, 1 - u)

                over_batches(pe, body)
                layer3(B - 1, 1, E - 2)
                layer3(B - 1, 1, E - 1)
                turn_back(B - 1, 1)

            @block.scalar
            def _(act):
                def ht_high(b, u):
                    act.wait_ge(S(f"ht_loaded{u}"), (b - u) * 8 + 16)
                    wait(act, S("product1"), E * (b - 1))
                    act.activation(HS[u].high[:, :], HB[u][:, :], ACT.Copy).then_inc(S("ht_high"), 1)

                def relu1(b, u, e):
                    act.wait_ge(S("product1"), E * b + e + 1)
                    wait(act, S("product2"), E * b + e - 3)
                    act.activation(R1[e % 4][:, :], b_1[e % 2][:, :], ACT.Relu, bias=m.BNC[:, e:e + 1])\
                       .then_inc(S("relu1"), 1)

                def h1_high(b, u, e):
                    act.wait_ge(S("relu1"), E * b + e + 1)
                    act.activation(H1[e % 4].high[:, :], R1[e % 4][:, :], ACT.Copy).then_inc(S("h1_high"), 1)

                def relu2(b, u, e):
                    act.wait_ge(S("product2"), E * b + e + 1)
                    wait(act, S("hw_high"), E * b + e - 1)
                    wait(act, S("hw_full"), E * b + e - 1)
                    act.activation(R2[e % 2][:, :], b_2[e % 2][:, :], ACT.Relu, bias=m.BNC[:, E + e:E + e + 1])\
                       .then_inc(S("relu2"), 1)

                def keep_y(b, u):
                    act.wait_ge(S("product3"), E * b + E)
                    wait(act, S("y_turned"), b)
                    act.activation(YT[:, :], b_yt[u][:, :], ACT.Copy).then_inc(S("y_kept"), 1)

                ht_high(0, 0)
                for e in range(2):
                    relu1(0, 0, e)
                    h1_high(0, 0, e)

                def body(b, u, first, last):
                    for e in range(E):
                        if not (last and e >= E - 2):
                            relu1(*ahead(b, u, e))
                        relu2(b, u, e)
                        if not (last and e >= E - 2):
                            h1_high(*ahead(b, u, e))
                        if e == 2 and not first:
                            keep_y(b - 1, 1 - u)
                        if e == 3 and not last:
                            ht_high(b + 1, 1 - u)

                over_batches(act, body)
                keep_y(B - 1, 1)

            @block.vector
            def _(dve):
                def h1_low(b, u, e):
                    dve.wait_ge(S("h1_high"), E * b + e + 1)
                    wait(dve, S("product2"), E * b + e - 3)
                    k = e % 4
                    dve.tensor_tensor(H1[k].low[:, :], R1[k][:, :], H1[k].seen[:, :], ALU.subtract)\
                       .then_inc(S("h1_low"), 1)

                def weigh_high(b, u, e):
                    dve.wait_ge(S("relu2"), E * b + e + 1)
                    wait(dve, S("product3"), E * b + e - 3)
                    dve.tensor_tensor(HWS[e % 4].high[:, :], R2[e % 2][:, :], m.RW[:, e, :], ALU.mult)\
                       .then_inc(S("hw_high"), 1)

                def weigh_low(b, u, e):
                    dve.wait_ge(S("hw_full"), E * b + e + 1)
                    dve.wait_ge(S("hw_high"), E * b + e + 1)
                    dve.tensor_tensor(HWS[e % 4].low[:, :], HW[e % 2][:, :], HWS[e % 4].seen[:, :], ALU.subtract)\
                       .then_inc(S("hw_low"), 1)

                def update(b, u):
                    dve.wait_ge(S("y_turned"), b + 1)
                    dve.wait_ge(S("bias_added"), b + 1)
                    wait(dve, S(f"stored{u}"), (b - u) * 8)
                    dve.tensor_tensor(O[u][:, :], b_y[u][:, :], m.X[:, bass.ds(b * N, N)], ALU.add).then_inc(S("x4"), 1)

                h1_low(0, 0, 0)
                h1_low(0, 0, 1)

                def body(b, u, first, last):
                    for e in range(E):
                        weigh_high(b, u, e)
                        if not (last and e >= E - 2):
                            h1_low(*ahead(b, u, e))
                        weigh_low(b, u, e)
                        if e == 4 and not first:
                            update(b - 1, 1 - u)

                over_batches(dve, body)
                update(B - 1, 1)
        retire(nc, mem)


def build(nc, IN, out):
    with ExitStack() as stack:
        mem = Memory(nc, stack)
        sb = mem.sb
        m = Shared()
        m.waited = mem.sem("waited")
        m.X = sb("X", P, Q * P)
        m.MV = sb("mean_var", P, Q, 2)
        m.RSTD = sb("rstd", P, Q)
        m.IDENT = sb("ident", P, P)
        m.LE = sb("mask_le", P, P)
        m.GT = sb("mask_gt", P, P)
        m.ONES = sb("ones", P, P)
        m.MHALF = sb("minus_half", P, Q)
        m.WIN = sb("mamba_in_w", P, 644)
        m.CW = sb("conv_w", P, 3, 4)
        m.CB = sb("conv_b", P, 3)
        m.DTB = sb("dt_bias", P, 4)
        m.AH = sb("exp_a_log", P, 4)
        m.DH = sb("d_wide", P, 4)
        m.BLIN = sb("b_lin_wide", P, 128)
        m.WF = sb("mamba_w_out_lin", P, 2, 128)
        m.W1 = sb("w1", P, 8, 128)
        m.W2 = sb("w2", P, 8, 128)
        m.W3 = sb("w3", P, 8, 128)
        m.WR = sb("w_router", P, 8)
        m.BR = sb("b_router", P, 8)
        m.BO = sb("b_out", 8, 128)
        m.BNA = sb("bn_a", P, 16)
        m.BNC = sb("bn_c", P, 16)
        with ExitStack() as to_ode:
            sb = Memory(nc, to_ode).sb
            m.LT = sb("LT", P, T, N)
            m.L2T = sb("L2T", P, T, N)
            m.L3T = sb("L3T", P, T, N)
            m.L6T = sb("L6T", P, T, N)
            m.E = sb("E", P, 9, 128)
            m.CR = sb("ode_const_rows", 3, 3 * P)
            with ExitStack() as to_attention:
                sb = Memory(nc, to_attention).sb
                m.NEGM = sb("neg_mask", P, T, N)
                m.WEXT = sb("gat_w_ext", P, 130)
                m.WA2B = sb("gat_wa2_wide", P, P)
                with nc.allow_non_contiguous_dma(reason="a few columns of weights"):
                    setup(nc, m, IN)
                attention(nc, m)
            with ExitStack() as in_mamba:
                sb = Memory(nc, in_mamba).sb
                m.HT = sb("mamba_HT", P, Q * P)
                m.DTS = sb("dt", P, Q, HEADS)
                m.DA = sb("dA", P, Q, HEADS)
                m.EA = sb("decay_in", P, Q, HEADS)
                m.DD = sb("dt_decay_out", P, Q, HEADS)
                m.CD = sb("chunk_decay", P, Q, HEADS)
                mamba_norm(nc, m)
                mamba(nc, m)
            ode(nc, m)
        m.HT = mem.sb("moe_HT", P, Q * P)
        experts(nc, m, out)


_INS = ['x', 'adj', 'L0_gnn_W', 'L0_gnn_a', 'L0_ffn_W_in', 'L0_ffn_conv_w', 'L0_ffn_conv_b', 'L0_ffn_dt_bias',
        'L0_ffn_A_log', 'L0_ffn_D', 'L0_ffn_norm_w', 'L0_ffn_W_out', 'L0_ffn_W_lin', 'L0_ffn_b_lin',
        'L1_gnn_alpha_train', 'L1_gnn_w', 'L1_gnn_d', 'L1_gnn_fc_in_w', 'L1_gnn_fc_in_b', 'L1_ffn_Wr', 'L1_ffn_br',
        'L1_ffn_W1', 'L1_ffn_b1', 'L1_ffn_g1', 'L1_ffn_be1', 'L1_ffn_m1', 'L1_ffn_v1', 'L1_ffn_W2', 'L1_ffn_b2',
        'L1_ffn_g2', 'L1_ffn_be2', 'L1_ffn_m2', 'L1_ffn_v2', 'L1_ffn_Wo', 'L1_ffn_bo']


def kernel(**inputs):
    import numpy as np
    import concourse.bacc as bacc
    from concourse.bass_utils import run_bass_kernel_spmd

    nc = bacc.Bacc("TRN2", target_bir_lowering=False, num_devices=1)
    arrays, IN = {}, {}
    for name in _INS:
        a = np.ascontiguousarray(inputs[name])
        arrays[f"in_{name}"] = a
        IN[name] = nc.dram_tensor(f"in_{name}", a.shape, mybir.dt.from_np(a.dtype), kind="ExternalInput").ap()
    out = nc.dram_tensor("out", (B, N, D), F32, kind="ExternalOutput").ap()
    build(nc, IN, out)
    r = run_bass_kernel_spmd(nc, [arrays], core_ids=[0])
    return r.results[0]["out"]
```
